# Optimizing a Trainium2 kernel written in Bass

```python
import numpy as np
import jax
import jax.numpy as jnp

def _softmax(x, axis=-1):
    return jax.nn.softmax(x, axis=axis)

def _gelu(x):
    return jax.nn.gelu(x, approximate=True)

def _silu(x):
    return jax.nn.silu(x)

def _sigmoid(x):
    return jax.nn.sigmoid(x)

def _layernorm(x, axis=-1, eps=1e-05):
    m = jnp.mean(x, axis=axis, keepdims=True)
    v = jnp.var(x, axis=axis, keepdims=True)
    return (x - m) / jnp.sqrt(v + eps)

def _scatter_add(tgt, idx, src, axis=0):
    return tgt.at[idx].add(src)

def _segment_sum(src, seg, n):
    return jax.ops.segment_sum(src, seg, n)
kernel_name = 'mk_cond_resid_d4_seqx_r4_f68d38'

def setup_inputs(seed: int=0):
    np.random.seed(seed)
    _w = jnp.asarray

    def _rec_inputs():
        import jax
        import jax.numpy as jnp
        _rk = jax.random.key(seed)
        x = -0.0002928 + 1 * jax.random.normal(jax.random.fold_in(_rk, 1), (32, 256, 256), jnp.float32)
        _lenS = 256 - jax.random.randint(jax.random.fold_in(_rk, 7), (32,), 0, max(1, 256 // 4) + 1, jnp.int32)
        _lenS2 = 256 - jax.random.randint(jax.random.fold_in(_rk, 8), (32,), 0, max(1, 256 // 4) + 1, jnp.int32)
        itok_Sx32_0_1023 = jax.random.randint(jax.random.fold_in(_rk, 12), (256, 32), 0, 256, jnp.int32)
        condB_uprev = -0.456674 + 0.753242 * jax.random.normal(jax.random.fold_in(_rk, 14), (32,), jnp.float32)
        condB_tauraws = -5.74692 + 0.777674 * jax.random.normal(jax.random.fold_in(_rk, 15), (32,), jnp.float32)
        cond_256 = -0.000235209 + 0.019331 * jax.random.normal(jax.random.fold_in(_rk, 16), (32, 64), jnp.float32)
        condB_bn2 = jnp.zeros((32,), jnp.float32)
        cond_1024 = -4.10585e-05 + 0.0199478 * jax.random.normal(jax.random.fold_in(_rk, 18), (32, 256), jnp.float32)
        itok_B_0_7 = jax.random.randint(jax.random.fold_in(_rk, 19), (32,), 0, 8, jnp.int32)
        fside_BxSxS_0 = 4.13588e-05 + 0.999923 * jax.random.normal(jax.random.fold_in(_rk, 20), (32, 256, 256), jnp.float32)
        itok_B_0_5 = jax.random.randint(jax.random.fold_in(_rk, 21), (32,), 0, 6, jnp.int32)
        _validS = jnp.arange(256)[None, :] < _lenS[:, None]
        _validS2 = jnp.arange(256)[None, :] < _lenS2[:, None]
        _causal = jnp.tril(jnp.ones((256, 256), dtype=bool))
        mask_SxS_bk0 = jnp.logical_not(jnp.broadcast_to(_validS[0:1, :], (256, 256)))
        mask_Sx32_bk1 = jnp.ones((256, 32), dtype=bool)
        return (x, itok_Sx32_0_1023, condB_uprev, condB_tauraws, cond_256, condB_bn2, cond_1024, itok_B_0_7, fside_BxSxS_0, itok_B_0_5, mask_SxS_bk0, mask_Sx32_bk1)
    x, itok_Sx32_0_1023, condB_uprev, condB_tauraws, cond_256, condB_bn2, cond_1024, itok_B_0_7, fside_BxSxS_0, itok_B_0_5, mask_SxS_bk0, mask_Sx32_bk1 = _rec_inputs()

    def _L0_cond_setup():
        import jax, jax.numpy as jnp
        import numpy as np
        B, S, D, H = (4, 256, 256, 16)
        DH = D // H
        K_SPARSE = 32
        LAMBDA_MAX, ALPHA = (10.0, 5.0)
        SPARSE_THRESHOLD = 1.0
        key = jax.random.key(seed)
        ks = jax.random.split(key, 12)
        x = jax.random.normal(ks[0], (B, S, D), dtype=jnp.float32)
        prior_mask = jax.random.bernoulli(ks[1], 0.1, (S, S))
        prior_indices = jax.random.randint(ks[2], (S, K_SPARSE), 0, S)
        prior_index_mask = jax.random.bernoulli(ks[3], 0.9, (S, K_SPARSE))
        prior_index_mask = prior_index_mask.at[:, 0].set(True)
        u_prev = jax.random.normal(ks[4], (B, 1), dtype=jnp.float32)
        sc = 1.0 / np.sqrt(D)
        Wq = jax.random.normal(ks[5], (D, D), dtype=jnp.float32) * sc
        Wk = jax.random.normal(ks[6], (D, D), dtype=jnp.float32) * sc
        Wv = jax.random.normal(ks[7], (D, D), dtype=jnp.float32) * sc
        Wo = jax.random.normal(ks[8], (D, D), dtype=jnp.float32) * sc
        bq = jnp.zeros((D,), jnp.float32)
        bk = jnp.zeros((D,), jnp.float32)
        bv = jnp.zeros((D,), jnp.float32)
        bo = jnp.zeros((D,), jnp.float32)
        return {'x': x, 'prior_mask': prior_mask, 'prior_indices': prior_indices, 'prior_index_mask': prior_index_mask, 'u_prev': u_prev, 'Wq': Wq, 'bq': bq, 'Wk': Wk, 'bk': bk, 'Wv': Wv, 'bv': bv, 'Wo': Wo, 'bo': bo}
    _L0_cond_all = _L0_cond_setup()
    _L0_cond_in = {k: v for k, v in _L0_cond_all.items() if k in ('Wq', 'bq', 'Wk', 'bk', 'Wv', 'bv', 'Wo', 'bo')}
    del _L0_cond_all

    def _L1_cond_setup():
        import jax, jax.numpy as jnp
        import numpy as np
        import math
        B, T, E, D = (4, 512, 256, 4)

        def _tau_init(t):
            a = 0.1 ** (1.0 / max(t - 1, 1))
            tt = -math.log(max(a, 1e-10))
            return math.log(math.exp(tt) - 1 + 1e-10)

        def causal_ema(b, tau_raw):
            alpha = jnp.exp(-jax.nn.softplus(tau_raw)).astype(b.dtype)

            def step(h, bt):
                h = alpha * h + bt
                return (h, h)
            h0 = jnp.zeros((b.shape[0], b.shape[2]), b.dtype)
            _, hs = jax.lax.scan(step, h0, jnp.swapaxes(b, 0, 1))
            return jnp.swapaxes(hs, 0, 1)
        key = jax.random.key(seed)
        ks = jax.random.split(key, 10)
        s = 0.02
        return {'x': jax.random.normal(ks[0], (B, T, E), jnp.float32), 'tau_ctx': jnp.float32(_tau_init(max(T // 2, 4))), 'tau_raws': jnp.array([_tau_init(max(T // 2 ** i, 2)) for i in range(D)], jnp.float32), 'Wg': jax.random.normal(ks[1], (E, 2 * E), jnp.float32) * s, 'bg': jnp.full((E,), -0.5, jnp.float32), 'Wn1': jax.random.normal(ks[2], (E // 4, E), jnp.float32) * s, 'bn1': jnp.zeros((E // 4,), jnp.float32), 'Wn2': jax.random.normal(ks[3], (D, E // 4), jnp.float32) * s, 'bn2': jnp.zeros((D,), jnp.float32), 'blend': jax.random.normal(ks[4], (D, E), jnp.float32) * s, 'Wsoma': jax.random.normal(ks[5], (E, E), jnp.float32) * s, 'bsoma': jnp.zeros((E,), jnp.float32), 'Wtemp': jax.random.normal(ks[6], (E, E), jnp.float32) * s, 'btemp': jnp.zeros((E,), jnp.float32), 'Wout': jax.random.normal(ks[7], (E, E), jnp.float32) * s, 'gamma': jnp.ones((E,), jnp.float32), 'beta': jnp.zeros((E,), jnp.float32)}
    _L1_cond_all = _L1_cond_setup()
    _L1_cond_in = {k: v for k, v in _L1_cond_all.items() if k in ('tau_ctx', 'Wg', 'bg', 'Wn1', 'bn1', 'Wsoma', 'bsoma', 'Wtemp', 'btemp', 'Wout', 'gamma', 'beta')}
    del _L1_cond_all

    def _L2_cond_setup():
        import jax, jax.numpy as jnp
        import numpy as np
        IN, HID, OUT, PART, E = (256, 1024, 256, 64, 8)
        B, N = (16, 512)
        key = jax.random.key(seed)
        ks = jax.random.split(key, 8)
        s1 = 1.0 / np.sqrt(IN)
        s2 = 1.0 / np.sqrt(HID)
        return {'x': jax.random.normal(ks[0], (B, N, IN), dtype=jnp.float32), 'indices': jax.random.randint(ks[1], (B,), 0, E, dtype=jnp.int64), 'W1': jax.random.uniform(ks[2], (IN, HID), jnp.float32, -s1, s1), 'b1': jax.random.uniform(ks[3], (HID,), jnp.float32, -s1, s1), 'W2': jax.random.uniform(ks[4], (HID, OUT - PART), jnp.float32, -s2, s2), 'b2': jax.random.uniform(ks[5], (OUT - PART,), jnp.float32, -s2, s2), 'We': jax.random.uniform(ks[6], (E, HID, PART), jnp.float32, -s2, s2), 'be': jax.random.uniform(ks[7], (E, PART), jnp.float32, -s2, s2)}
    _L2_cond_all = _L2_cond_setup()
    _L2_cond_in = {k: v for k, v in _L2_cond_all.items() if k in ('W1', 'b1', 'W2', 'b2', 'We', 'be')}
    del _L2_cond_all

    def _L3_cond_setup():
        import jax, jax.numpy as jnp
        import numpy as np
        B, S, D = (8, 256, 256)
        NUM_STAGES = 6
        key = jax.random.key(seed)
        k1, k2, k3, k4, k5 = jax.random.split(key, 5)
        return {'query': jax.random.normal(k1, (B, S, D), dtype=jnp.float32), 'key': jax.random.normal(k2, (B, S, D), dtype=jnp.float32), 'value': jax.random.normal(k3, (B, S, D), dtype=jnp.float32), 'braak_embed': jax.random.normal(k4, (NUM_STAGES, D), dtype=jnp.float32), 'braak_stages': jax.random.randint(k5, (B,), 0, NUM_STAGES, dtype=jnp.int64)}
    _L3_cond_all = _L3_cond_setup()
    _L3_cond_in = {k: v for k, v in _L3_cond_all.items() if k in ('braak_embed',)}
    del _L3_cond_all
    return {'x': x, 'itok_Sx32_0_1023': itok_Sx32_0_1023, 'condB_uprev': condB_uprev, 'condB_tauraws': condB_tauraws, 'cond_256': cond_256, 'condB_bn2': condB_bn2, 'cond_1024': cond_1024, 'itok_B_0_7': itok_B_0_7, 'fside_BxSxS_0': fside_BxSxS_0, 'itok_B_0_5': itok_B_0_5, 'mask_SxS_bk0': mask_SxS_bk0, 'mask_Sx32_bk1': mask_Sx32_bk1, 'L0_cond_Wq': _L0_cond_in['Wq'], 'L0_cond_bq': _L0_cond_in['bq'], 'L0_cond_Wk': _L0_cond_in['Wk'], 'L0_cond_bk': _L0_cond_in['bk'], 'L0_cond_Wv': _L0_cond_in['Wv'], 'L0_cond_bv': _L0_cond_in['bv'], 'L0_cond_Wo': _L0_cond_in['Wo'], 'L0_cond_bo': _L0_cond_in['bo'], 'L1_cond_tau_ctx': _L1_cond_in['tau_ctx'], 'L1_cond_Wg': _L1_cond_in['Wg'], 'L1_cond_bg': _L1_cond_in['bg'], 'L1_cond_Wn1': _L1_cond_in['Wn1'], 'L1_cond_bn1': _L1_cond_in['bn1'], 'L1_cond_Wsoma': _L1_cond_in['Wsoma'], 'L1_cond_bsoma': _L1_cond_in['bsoma'], 'L1_cond_Wtemp': _L1_cond_in['Wtemp'], 'L1_cond_btemp': _L1_cond_in['btemp'], 'L1_cond_Wout': _L1_cond_in['Wout'], 'L1_cond_gamma': _L1_cond_in['gamma'], 'L1_cond_beta': _L1_cond_in['beta'], 'L2_cond_W1': _L2_cond_in['W1'], 'L2_cond_b1': _L2_cond_in['b1'], 'L2_cond_W2': _L2_cond_in['W2'], 'L2_cond_b2': _L2_cond_in['b2'], 'L2_cond_We': _L2_cond_in['We'], 'L2_cond_be': _L2_cond_in['be'], 'L3_cond_braak_embed': _L3_cond_in['braak_embed']}

def reference(x, itok_Sx32_0_1023, condB_uprev, condB_tauraws, cond_256, condB_bn2, cond_1024, itok_B_0_7, fside_BxSxS_0, itok_B_0_5, mask_SxS_bk0, mask_Sx32_bk1, L0_cond_Wq, L0_cond_bq, L0_cond_Wk, L0_cond_bk, L0_cond_Wv, L0_cond_bv, L0_cond_Wo, L0_cond_bo, L1_cond_tau_ctx, L1_cond_Wg, L1_cond_bg, L1_cond_Wn1, L1_cond_bn1, L1_cond_Wsoma, L1_cond_bsoma, L1_cond_Wtemp, L1_cond_btemp, L1_cond_Wout, L1_cond_gamma, L1_cond_beta, L2_cond_W1, L2_cond_b1, L2_cond_W2, L2_cond_b2, L2_cond_We, L2_cond_be, L3_cond_braak_embed):
    import jax
    import jax.numpy as jnp

    def _L0_cond_ref(x, prior_mask, prior_indices, prior_index_mask, u_prev, Wq, bq, Wk, bk, Wv, bv, Wo, bo):
        import jax, jax.numpy as jnp
        import numpy as np
        B, S, D, H = (4, 256, 256, 16)
        DH = D // H
        K_SPARSE = 32
        LAMBDA_MAX, ALPHA = (10.0, 5.0)
        SPARSE_THRESHOLD = 1.0
        Bb, Ss, Dd = x.shape
        scale = 1.0 / jnp.sqrt(jnp.asarray(DH, x.dtype))

        def proj(W, b):
            return (x @ W.T + b).reshape(Bb, Ss, H, DH).transpose(0, 2, 1, 3)
        Q, K, V = (proj(Wq, bq), proj(Wk, bk), proj(Wv, bv))
        lam = LAMBDA_MAX * jnp.exp(-ALPHA * u_prev.reshape(Bb))
        use_sparse = lam >= SPARSE_THRESHOLD
        scores = jnp.einsum('bhqd,bhkd->bhqk', Q, K) * scale
        prior_bias = jnp.where(prior_mask[:Ss, :Ss], 0.0, -1.0).astype(x.dtype)
        bias = lam[:, None, None, None] * prior_bias[None, None]
        dense_out = jnp.einsum('bhqk,bhkd->bhqd', jax.nn.softmax(scores + bias, axis=-1), V)
        idx = prior_indices[:Ss]
        Kg = K[:, :, idx]
        Vg = V[:, :, idx]
        s_scores = jnp.einsum('bhsd,bhskd->bhsk', Q, Kg) * scale
        s_scores = jnp.where(prior_index_mask[:Ss][None, None], s_scores, jnp.asarray(-jnp.inf, x.dtype))
        sparse_out = jnp.einsum('bhsk,bhskd->bhsd', jax.nn.softmax(s_scores, axis=-1), Vg)
        out = jnp.where(use_sparse[:, None, None, None], sparse_out, dense_out)
        out = out.transpose(0, 2, 1, 3).reshape(Bb, Ss, Dd)
        return out @ Wo.T + bo

    def _L1_cond_ref(x, tau_ctx, tau_raws, Wg, bg, Wn1, bn1, Wn2, bn2, blend, Wsoma, bsoma, Wtemp, btemp, Wout, gamma, beta):
        import jax, jax.numpy as jnp
        import numpy as np
        import math
        B, T, E, D = (4, 512, 256, 4)

        def _tau_init(t):
            a = 0.1 ** (1.0 / max(t - 1, 1))
            tt = -math.log(max(a, 1e-10))
            return math.log(math.exp(tt) - 1 + 1e-10)

        def causal_ema(b, tau_raw):
            alpha = jnp.exp(-jax.nn.softplus(tau_raw)).astype(b.dtype)

            def step(h, bt):
                h = alpha * h + bt
                return (h, h)
            h0 = jnp.zeros((b.shape[0], b.shape[2]), b.dtype)
            _, hs = jax.lax.scan(step, h0, jnp.swapaxes(b, 0, 1))
            return jnp.swapaxes(hs, 0, 1)
        ctx = causal_ema(x, tau_ctx)
        gate_in = jnp.concatenate([x, ctx], axis=-1)
        wg = jax.nn.sigmoid(jnp.einsum('btc,ec->bte', gate_in, Wg) + bg)
        gated = x * wg
        h1 = jax.nn.gelu(jnp.einsum('btc,hc->bth', x, Wn1) + bn1, approximate=False)
        mod = 0.5 + jax.nn.sigmoid(jnp.einsum('bth,dh->btd', h1, Wn2) + bn2)
        traces = jax.vmap(lambda tau, m: causal_ema(gated * m[..., None], tau))(tau_raws, jnp.moveaxis(mod, -1, 0))
        blend_w = jax.nn.softmax(blend, axis=0)
        temporal = jnp.einsum('dbtc,dc->btc', traces, blend_w)
        gate = jax.nn.sigmoid(jnp.einsum('btc,ec->bte', temporal, Wtemp) + btemp)
        soma = jax.nn.gelu(jnp.einsum('btc,ec->bte', x, Wsoma) + bsoma, approximate=False)
        out = jnp.einsum('btc,ec->bte', soma * gate, Wout)
        mu = out.mean(-1, keepdims=True)
        var = out.var(-1, keepdims=True)
        return (out - mu) / jnp.sqrt(var + 1e-05) * gamma + beta

    def _L2_cond_ref(x, indices, W1, b1, W2, b2, We, be):
        import jax, jax.numpy as jnp
        import numpy as np
        IN, HID, OUT, PART, E = (256, 1024, 256, 64, 8)
        B, N = (16, 512)
        h = jax.nn.gelu(jnp.einsum('bni,ih->bnh', x, W1) + b1, approximate=False)
        shared_x = jnp.einsum('bnh,ho->bno', h, W2) + b2
        We_sel = We[indices]
        be_sel = be[indices]
        expert_x = jnp.einsum('bnh,bhp->bnp', h, We_sel) + be_sel[:, None, :]
        return jnp.concatenate([shared_x, expert_x], axis=-1)

    def _L3_cond_ref(query, key, value, braak_embed, braak_stages):
        import jax, jax.numpy as jnp
        import numpy as np
        B, S, D = (8, 256, 256)
        NUM_STAGES = 6
        bias = braak_embed[braak_stages][..., None]
        q = query + bias
        attn = jnp.einsum('bsd,btd->bst', q, key)
        attn = jax.nn.softmax(attn, axis=-1)
        return jnp.einsum('bst,btd->bsd', attn, value)
    x = x + _L0_cond_ref(x, mask_SxS_bk0, itok_Sx32_0_1023, mask_Sx32_bk1, condB_uprev[:, None], L0_cond_Wq, L0_cond_bq, L0_cond_Wk, L0_cond_bk, L0_cond_Wv, L0_cond_bv, L0_cond_Wo, L0_cond_bo)
    x = x + _L1_cond_ref(x, L1_cond_tau_ctx, condB_tauraws, L1_cond_Wg, L1_cond_bg, L1_cond_Wn1, L1_cond_bn1, cond_256, condB_bn2, cond_1024, L1_cond_Wsoma, L1_cond_bsoma, L1_cond_Wtemp, L1_cond_btemp, L1_cond_Wout, L1_cond_gamma, L1_cond_beta)
    x = x + _L2_cond_ref(x, itok_B_0_7, L2_cond_W1, L2_cond_b1, L2_cond_W2, L2_cond_b2, L2_cond_We, L2_cond_be)
    x = x + _L3_cond_ref(x, fside_BxSxS_0, fside_BxSxS_0, L3_cond_braak_embed, itok_B_0_5)
    return x

_drawn_inputs = setup_inputs


def setup_inputs(seed=0):
    import zlib

    import numpy as np

    out = dict(_drawn_inputs(seed))
    spreads = {'condB_bn2': (0.0, 2.0),
     'L0_cond_bq': (0.0, 0.1),
     'L0_cond_bk': (0.0, 2.0),
     'L0_cond_bv': (0.0, 0.1),
     'L0_cond_bo': (0.0, 0.1),
     'L1_cond_bg': (-0.5, 0.565),
     'L1_cond_bn1': (0.0, 2.0),
     'L1_cond_bsoma': (0.0, 0.1),
     'L1_cond_btemp': (0.0, 0.1),
     'L1_cond_gamma': (1.0, 0.2),
     'L1_cond_beta': (0.0, 0.1)}
    factors = {'condB_tauraws': 8.0,
     'cond_256': 8.0,
     'cond_1024': 47.549,
     'L1_cond_Wn1': 8.0,
     'L2_cond_b1': 2.816,
     'L2_cond_be': 4.057}
    for name, (base, spread) in spreads.items():
        noise = np.random.default_rng([zlib.crc32(name.encode()), seed]).standard_normal(out[name].shape)
        drawn = base * np.exp(spread * noise) if base else spread * noise
        out[name] = jnp.asarray(drawn.astype(out[name].dtype))
    for name, factor in factors.items():
        out[name] = (out[name] * factor).astype(out[name].dtype)
    return out
```

```python
from contextlib import contextmanager, ExitStack

import concourse.bass as bass
from concourse import mybir

F32 = mybir.dt.float32
F32R = mybir.dt.float32r
BF16 = mybir.dt.bfloat16
I32 = mybir.dt.int32
U8 = mybir.dt.uint8
ALU = mybir.AluOpType
ACT = mybir.ActivationFunctionType
AX = mybir.AxisListType

P = 128
S = 256
D = 256
C = D // P
HEADS, DH = 16, 16
K_SPARSE = 32
NEG = -1.0e30
BIG = 3.0e38
GROUPS = 8
TERMS = 3
E_BUFS = 4


def at_least(eng, sem, value):
    if isinstance(value, int) and value <= 0:
        return
    eng.wait_ge(sem, value)


def rows_group(g):
    half, c, rows = g // 4, g // 2 % 2, g % 2
    return 2 * c + half, rows


def landed(n, par):
    return 8 * (n - par) + 16


@contextmanager
def pairs(eng, first, end):
    with eng.Fori(0, (end - first) // 2) as i:
        yield i * 2 + first


def attention_layer(nc, sem_ctx, ctx, t, X, NB, consts):
    def sb(name, shape, dt):
        return ctx.enter_context(nc.sbuf_tensor("a_" + name, shape, dt))

    def ps(name, shape, dt=F32):
        return ctx.enter_context(nc.psum_tensor("a_" + name, shape, dt))

    def sem(name):
        return sem_ctx.enter_context(nc.semaphore("a_" + name))

    ident, ident_bf, iota, sel_den, sel_rep = consts["ident"], consts["ident_bf"], consts["iota"], consts["sel_den"], consts["sel_rep"]

    wq, wk, wv, wo = (sb(n, [P, C, D], F32) for n in ("wq", "wk", "wv", "wo"))
    bias = sb("bias", [P, 4, C], F32)
    bq_s = sb("bq_s", [P, C, 2], F32)
    bo_all = sb("bo_all", [P, C], F32)
    par_mask = consts["par_mask"]
    xs = [sb(f"xs{i}", [P, C, S], F32) for i in range(2)]
    q_hi = sb("q_hi", [P, C, 2, S], F32R)
    q_lo = sb("q_lo", [P, C, 2, S], F32R)
    q_full = sb("q_full", [P, C, 2, S], F32)
    k_hi = sb("k_hi", [P, C, S], F32R)
    k_lo = sb("k_lo", [P, C, S], F32R)
    q_st = [sb(f"q_st{i}", [P, HEADS, S], F32R) for i in range(2)]
    k_st = [sb(f"k_st{i}", [P, HEADS // 2, S], F32R) for i in range(2)]
    v_pad = [sb(f"v_pad{i}", [P, C, HEADS, 32], F32) for i in range(2)]
    e = [sb(f"e{i}", [P, 4, S], F32) for i in range(E_BUFS)]
    neg_max = sb("neg_max", [P, C, HEADS], F32)
    max_row = sb("max_row", [HEADS, S], F32R)
    r_den = sb("r_den", [P, S], F32)
    r_rep = sb("r_rep", [P, C, S], F32)
    att = sb("att", [P, C, S], F32)
    u_all = sb("u_all", [P, NB], F32)
    lam = sb("lam", [P, NB], F32)
    decay = sb("decay", [P, NB], F32)
    mix = sb("mix", [P, NB, 4], F32)
    mixn = [sb(f"mixn{i}", [P, 4], F32) for i in range(2)]
    idx_i = sb("idx_i", [P, C, K_SPARSE], I32)
    idx_f = sb("idx_f", [P, C, K_SPARSE], F32)
    val_u = sb("val_u", [P, C, K_SPARSE], U8)
    val_f = sb("val_f", [P, C, K_SPARSE], F32)
    cnt = sb("cnt", [P, C, S], F32)
    cnt_t = sb("cnt_t", [P, C, S], F32)
    absent = sb("absent", [P, C, S], F32)
    msk_u = sb("msk_u", [P, 2, C, S], U8)
    off = sb("off", [P, C, S], F32)
    off_t = sb("off_t", [P, C, S], F32)
    w_off, w_cnt, m_off, m_abs = (sb(n, [P, C, S], F32) for n in ("w_off", "w_cnt", "m_off", "m_abs"))
    w_t = [sb(f"w_t{i}", [P, C, S], F32) for i in range(2)]
    add_m = [sb(f"add_m{i}", [P, C, S], BF16) for i in range(2)]

    ps_s = ps("s", [P, 2, 512])
    ps_t = ps("t", [P, 2, 512])
    ps_o = ps("o", [P, C, S])
    ps_den = ps("den", [P, 512])
    bank0 = ps("bank0", [P, C, S])
    bank1 = ps("bank1", [P, C, S])

    d_w, d_small = sem("d_w"), sem("d_small")
    g_ready, g_step, s_ready, a_step = sem("g_ready"), sem("g_step"), sem("s_ready"), sem("a_step")
    setup_pe, setup_done = sem("setup_pe"), sem("setup_done")
    d_xs, d_x = [sem("d_xs0"), sem("d_xs1")], sem("d_x")
    stack_free = [sem("stack_free0"), sem("stack_free1")]
    proj_q, proj_k, proj_v = sem("proj_q"), sem("proj_k"), sem("proj_v")
    qf_done, qhi_done, qlo_done, khi_done, klo_done, v_done = (sem(n) for n in ("qf", "qhi", "qlo", "khi", "klo", "v"))
    d_stack, d_max = [sem("d_stack0"), sem("d_stack1")], sem("d_max")
    s_done, red_done = sem("s_done"), sem("red_done")
    t_done, exp_done, p_done, pv_done = sem("t_done"), sem("exp_done"), sem("p_done"), sem("pv_done")
    mt_done, mrow_done = sem("mt_done"), sem("mrow_done")
    rden_done, rep_done, rrep_done, att_done, wo_done, x1_done = (sem(n) for n in ("rden", "rep", "rrep", "att", "wo", "x1"))
    mix_done, pool_mix, pool_step, w_ready, m_ready = (sem(n) for n in ("mix", "pmix", "pstep", "w_ready", "m_ready"))
    zero_done = sem("zero")

    N_W = 4
    STACK_DMAS = 2 * TERMS * 2

    block = ctx.enter_context(nc.Block())

    @block.sync
    def _(sp):
        for w, name in ((wq, "wq"), (wk, "wk"), (wv, "wv"), (wo, "wo")):
            sp.dma_start(w[:], t[name].rearrange("(k p) e -> p k e", p=P)).then_inc(d_w, 16)
        for n in range(2):
            sp.dma_start(xs[n][:], t["xT"][n].rearrange("(k p) s -> p k s", p=P)).then_inc(d_xs[n], 16)

        def stack(n, par, half):
            sp.wait_ge(stack_free[half], n + 1)
            for dst, parts, parts_done in ((k_st[par], (k_hi, k_hi, k_lo), (khi_done, klo_done)),
                                           (q_st[par], (q_hi, q_lo, q_hi), (qhi_done, qlo_done))):
                for done in parts_done:
                    sp.wait_ge(done, n + 1)
                for term, src in enumerate(parts):
                    for j in (2 * half, 2 * half + 1):
                        rows = src[32 * j:32 * j + 32].bitcast(F32)
                        to = dst[32 * term:32 * term + 32].bitcast(F32)
                        to = (to.rearrange("p (c j r) s -> p j c r s", c=C, j=4) if dst is q_st[par]
                              else to.rearrange("p (c j) s -> p j c s", c=C))
                        sp.dma_start(to[:, j], rows).then_inc(d_stack[half], 16)

        def maxima(n, par):
            sp.wait_ge(mrow_done, n + 1)
            sp.dma_start(q_st[par][96:97].bitcast(F32), max_row[:].bitcast(F32)).then_inc(d_max, 16)

        for n in range(2):
            for half in range(2):
                stack(n, n, half)
        maxima(0, 0)

        def staged(n, par):
            sp.wait_ge(proj_v, n - 1)
            sp.dma_start(xs[par][:], t["xT"][bass.ds(n, 1)].rearrange("o (k p) s -> p (o k) s", p=P)
                         if not isinstance(n, int) else t["xT"][n].rearrange("(k p) s -> p k s", p=P)).then_inc(d_xs[par], 16)

        def full(n, par, more_max, more_proj):
            at_least(sp, d_x, n * 16)
            sp.dma_start(X[:, :, bass.ds(n * S, S)] if not isinstance(n, int) else X[:, :, n * S:n * S + S],
                         t["xT"][bass.ds(n, 1)].rearrange("o (k p) s -> p (o k) s", p=P)
                         if not isinstance(n, int) else t["xT"][n].rearrange("(k p) s -> p k s", p=P)).then_inc(d_x, 16)
            if more_proj:
                staged(n + 2, par)
                stack(n + 2, par, 0)
            if more_max:
                maxima(n + 1, 1 - par)
            if more_proj:
                stack(n + 2, par, 1)

        full(0, 0, True, NB > 2)
        if NB > 2:
            if NB > 4:
                with pairs(sp, 1, NB - 3) as n:
                    full(n, 1, True, True)
                    full(n + 1, 0, True, True)
            full(NB - 3, 1, True, True)
            full(NB - 2, 0, True, False)
        full(NB - 1, 1, False, False)

    @block.gpsimd
    def _(pool):
        for half in stack_free:
            pool.sem_inc(half, 2)
        for i in range(2):
            pool.memset(k_st[i][96:97].bitcast(F32), 1.0).then_inc(zero_done, 1)
            pool.wait_ge(zero_done, 2 * i + 1)
            pool.memset(v_pad[i][:], 0.0).then_inc(zero_done, 1)
            pool.wait_ge(zero_done, 2 * i + 2)
        pool.dma_start(idx_i[:], t["idx"].rearrange("(k p) j -> p k j", p=P)).then_inc(d_small, 16)
        pool.dma_start(val_u[:], t["valid"].rearrange("(k p) j -> p k j", p=P)).then_inc(d_small, 16)
        pool.dma_start(msk_u[:, 0], t["mask"].rearrange("(k p) s -> p k s", p=P)).then_inc(d_small, 16)
        pool.dma_start(msk_u[:, 1], t["maskT"].rearrange("(k p) s -> p k s", p=P)).then_inc(d_small, 16)
        pool.dma_start(u_all[:], t["u"].partition_broadcast(P)).then_inc(d_small, 16)
        for i, name in enumerate(("bq", "bk", "bv", "bo")):
            pool.dma_start(bias[:, i], t[name]).then_inc(d_small, 16)
        pool.wait_ge(mix_done, 1)
        pool.wait_ge(setup_done, 1)

        def body(n, par):
            at_least(pool, w_ready, n)
            at_least(pool, m_ready, n)
            if isinstance(n, int):
                pool.tensor_copy(mixn[par][:], mix[:, n]).then_inc(pool_mix, 1)
            else:
                pool.tensor_copy(mixn[par][:], mix[:, bass.ds(n, 1)].rearrange("p o f -> p (o f)")).then_inc(pool_mix, 1)
            pool.wait_ge(pool_mix, n + 1)
            m = mixn[par]
            pool.tensor_tensor(w_cnt[:], cnt_t[:], m[:, 0:1].unsqueeze(2).to_broadcast([P, C, S]), ALU.mult).then_inc(pool_step, 1)
            pool.tensor_scalar(w_off[:], off_t[:], m[:, 2:3], m[:, 1:2], ALU.mult, ALU.add).then_inc(pool_step, 1)
            pool.tensor_scalar(m_off[:], off[:], m[:, 3:4], None, ALU.mult).then_inc(pool_step, 1)
            pool.tensor_scalar(m_abs[:], absent[:], m[:, 0:1], None, ALU.mult).then_inc(pool_step, 1)
            pool.wait_ge(pool_step, n * 4 + 4)
            if not (isinstance(n, int) and n < 2):
                pool.wait_ge(p_done, (n - 1) * GROUPS)
            pool.tensor_tensor(w_t[par][:], w_off[:], w_cnt[:], ALU.add).then_inc(w_ready, 1)
            if not (isinstance(n, int) and n < 2):
                pool.wait_ge(s_done, (n - 1) * GROUPS)
            pool.tensor_tensor(add_m[par][:], m_off[:], m_abs[:], ALU.add).then_inc(m_ready, 1)

        body(0, 0)
        body(1, 1)
        if NB > 2:
            with pairs(pool, 2, NB) as n:
                body(n, 0)
                body(n + 1, 1)

    @block.vector
    def _(dve):
        done = [0]

        def link(ins):
            done[0] += 1
            ins.then_inc(g_step, 1)
            dve.wait_ge(g_step, done[0])

        dve.wait_ge(d_w, 16 * N_W)
        dve.wait_ge(d_small, 16 * 9)
        dve.tensor_scalar(wq[:], wq[:], 0.25, None, ALU.mult).then_inc(s_ready, 1)
        for par in range(2):
            dve.tensor_scalar(bq_s[:, :, par], bias[:, 0], par_mask[:, par:par + 1], 0.25, ALU.mult, ALU.mult).then_inc(s_ready, 1)

        link(dve.tensor_copy(idx_f[:], idx_i[:]))
        link(dve.tensor_copy(val_f[:], val_u[:]))
        link(dve.tensor_scalar(idx_f[:], idx_f[:], 1.0, None, ALU.add))
        link(dve.tensor_tensor(idx_f[:], idx_f[:], val_f[:], ALU.mult))
        link(dve.tensor_scalar(idx_f[:], idx_f[:], -1.0, None, ALU.add))
        link(dve.memset(cnt[:], 0.0))
        base = done[0]
        for j in range(K_SPARSE):
            for k in range(C):
                if j:
                    dve.wait_ge(g_step, base + (j - 1) * C + k + 1)
                dve.scalar_tensor_tensor(out=cnt[:, k], in0=iota[:], scalar=idx_f[:, k, j:j + 1], in1=cnt[:, k],
                                         op0=ALU.is_equal, op1=ALU.add).then_inc(g_step, 1)
        done[0] = base + C * K_SPARSE
        dve.wait_ge(g_step, done[0])
        link(dve.tensor_scalar(absent[:], cnt[:], 0.0, NEG, ALU.is_equal, ALU.mult))
        link(dve.tensor_copy(off[:], msk_u[:, 0]))
        link(dve.tensor_copy(off_t[:], msk_u[:, 1]))
        link(dve.tensor_scalar(off[:], off[:], -1.0, 1.0, ALU.mult, ALU.add))
        link(dve.tensor_scalar(off_t[:], off_t[:], -1.0, 1.0, ALU.mult, ALU.add))
        dve.wait_ge(a_step, 1)
        dve.tensor_scalar(lam[:], lam[:], 10.0, None, ALU.mult).then_inc(g_ready, 1)
        dve.wait_ge(g_ready, 1)
        dve.wait_ge(a_step, 2)
        link(dve.tensor_scalar(mix[:, :, 0], lam[:], 1.0, None, ALU.is_ge))
        link(dve.tensor_scalar(mix[:, :, 1], mix[:, :, 0], -1.0, 1.0, ALU.mult, ALU.add))
        link(dve.tensor_scalar(decay[:], decay[:], -1.0, None, ALU.add))
        link(dve.tensor_tensor(mix[:, :, 2], mix[:, :, 1], decay[:], ALU.mult))
        link(dve.tensor_scalar(lam[:], lam[:], 1.0, -1.0, ALU.min, ALU.mult))
        dve.tensor_tensor(mix[:, :, 3], mix[:, :, 1], lam[:], ALU.mult).then_inc(mix_done, 1)
        dve.wait_ge(setup_pe, 1)
        for k in range(C):
            dve.tensor_copy(cnt_t[:, k], bank0[:, k]).then_inc(g_step, 1)
        dve.tensor_tensor(bo_all[:], ps_den[:, 0:C], bias[:, 3], ALU.add).then_inc(s_ready, 1)
        done[0] += 2
        dve.wait_ge(g_step, done[0])
        dve.wait_ge(s_ready, 4)
        dve.sem_inc(setup_done, 1)

        def low_parts(n):
            dve.wait_ge(qf_done, n + 1)
            dve.wait_ge(qhi_done, n + 1)
            if not (isinstance(n, int) and n == 0):
                for half in d_stack:
                    dve.wait_ge(half, n * 16 * STACK_DMAS)
            dve.tensor_tensor(q_lo[:], q_full[:], q_hi[:].bitcast(F32), ALU.subtract).then_inc(qlo_done, 1)
            dve.wait_ge(khi_done, n + 1)
            for k in range(C):
                ins = dve.scalar_tensor_tensor(out=k_lo[:, k], in0=bank1[:, k], scalar=bias[:, 1, k:k + 1],
                                               in1=k_hi[:, k].bitcast(F32), op0=ALU.add, op1=ALU.subtract)
            ins.then_inc(klo_done, 1)

        def row_max(n, g):
            quad, qc = rows_group(g)
            dve.wait_ge(s_done, n * GROUPS + g + 1)
            if g == 0:
                at_least(dve, mt_done, n)
            dve.tensor_reduce(neg_max[:, qc, 4 * quad:4 * quad + 4],
                              ps_s[:].rearrange("p b (h k) -> p (b h) k", h=2), AX.X, ALU.max, negate=True).then_inc(red_done, 1)

        def weigh(n, par, g):
            kc = g % 2
            dve.wait_ge(exp_done, n * GROUPS + g + 1)
            if g == 0:
                dve.wait_ge(w_ready, n + 1)
            buf = e[g % E_BUFS]
            dve.scalar_tensor_tensor(out=buf[:], in0=buf[:], scalar=BIG,
                                     in1=w_t[par][:, kc].unsqueeze(1).to_broadcast([P, 4, S]),
                                     op0=ALU.min, op1=ALU.mult).then_inc(p_done, 1)

        def reciprocal(n):
            dve.wait_ge(pv_done, (n + 1) * GROUPS)
            at_least(dve, rep_done, n)
            dve.reciprocal(r_den[:], ps_den[:, 0:S]).then_inc(rden_done, 1)

        def normalize(n):
            dve.wait_ge(rrep_done, n + 1)
            at_least(dve, wo_done, n)
            dve.tensor_tensor(att[:], ps_o[:], r_rep[:], ALU.mult).then_inc(att_done, 1)

        def residual(n):
            dve.wait_ge(wo_done, n + 1)
            dve.wait_ge(d_x, 16 * (n + 1))
            for k in range(C):
                xo = X[:, k, n * S:n * S + S] if isinstance(n, int) else X[:, k, bass.ds(n * S, S)]
                ins = dve.scalar_tensor_tensor(out=xo, in0=bank0[:, k], scalar=bo_all[:, k:k + 1], in1=xo,
                                               op0=ALU.add, op1=ALU.add)
            ins.then_inc(x1_done, 1)

        def body(n, par, first, last, proj):
            for g in range(GROUPS):
                if not last:
                    row_max(n + 1, g)
                weigh(n, par, g)
                if g == 0 and not first:
                    normalize(n - 1)
                if g == 1 and not first:
                    residual(n - 1)
                if g == 3 and proj:
                    low_parts(n + 2)
            reciprocal(n)

        low_parts(0)
        low_parts(1)
        for g in range(GROUPS):
            row_max(0, g)
        body(0, 0, True, False, NB > 2)
        if NB > 2:
            if NB > 4:
                with pairs(dve, 1, NB - 3) as n:
                    body(n, 1, False, False, True)
                    body(n + 1, 0, False, False, True)
            body(NB - 3, 1, False, False, True)
            body(NB - 2, 0, False, False, False)
        body(NB - 1, 1, False, True, False)
        normalize(NB - 1)
        residual(NB - 1)
        dve.wait_ge(x1_done, NB)

    @block.scalar
    def _(act):
        act.wait_ge(d_small, 16 * 9)
        act.activation(lam[:], u_all[:], ACT.Exp, scale=-5.0).then_inc(a_step, 1)
        act.wait_ge(g_ready, 1)
        act.activation(decay[:], lam[:], ACT.Exp, scale=-1.0).then_inc(a_step, 1)
        act.wait_ge(setup_done, 1)
        act.wait_ge(zero_done, 4)

        def high_parts(n):
            if not (isinstance(n, int) and n == 0):
                for half in d_stack:
                    act.wait_ge(half, n * 16 * STACK_DMAS)
                act.wait_ge(qlo_done, n)
            act.wait_ge(proj_q, n + 1)
            for k in range(C):
                for r in range(2):
                    ins = act.activation(q_full[:, k, r], bank0[:, k], ACT.Identity,
                                         bias=bq_s[:, k, r:r + 1], scale=par_mask[:, r:r + 1])
            ins.then_inc(qf_done, 1)
            act.wait_ge(qf_done, n + 1)
            act.activation(q_hi[:], q_full[:], ACT.Copy).then_inc(qhi_done, 1)
            act.wait_ge(proj_k, n + 1)
            for k in range(C):
                ins = act.activation(k_hi[:, k], bank1[:, k], ACT.Identity, bias=bias[:, 1, k:k + 1])
            ins.then_inc(khi_done, 1)

        def values(n, par):
            act.wait_ge(proj_v, n + 1)
            if not (isinstance(n, int) and n < 2):
                act.wait_ge(pv_done, (n - 1) * GROUPS)
            for k in range(C):
                for half in range(2):
                    src = bank0[:, k].rearrange("p (c h j d) -> p c h j d", c=C, h=2, j=4)[:, :, half]
                    dst = v_pad[par][:, k].rearrange("p (c h j) w -> p c h j w", c=C, h=2)[:, :, half, :, 16 * half:16 * half + 16]
                    ins = act.activation(dst, src, ACT.Copy)
            ins.then_inc(v_done, 1)

        def exps(n, g):
            act.wait_ge(t_done, n * GROUPS + g + 1)
            if not (isinstance(n, int) and n == 0 and g < E_BUFS):
                act.wait_ge(pv_done, n * GROUPS + g - E_BUFS + 1)
            act.activation(e[g % E_BUFS][:].rearrange("p (b h) s -> p b (h s)", b=2), ps_t[:], ACT.Exp).then_inc(exp_done, 1)

        def max_rows(n):
            act.wait_ge(mt_done, n + 1)
            if not (isinstance(n, int) and n == 0):
                act.wait_ge(d_max, 16 * n)
            act.activation(max_row[:], bank1[0:HEADS, 0], ACT.Copy).then_inc(mrow_done, 1)

        def spread(n):
            act.wait_ge(rep_done, n + 1)
            at_least(act, att_done, n)
            act.activation(r_rep[:], bank1[:], ACT.Copy).then_inc(rrep_done, 1)

        def body(n, par, first, last, proj):
            for g in range(GROUPS):
                exps(n, g)
                if g == 0 and not first:
                    spread(n - 1)
                if g == 2 and proj:
                    high_parts(n + 2)
            if not last:
                max_rows(n + 1)
            if proj:
                values(n + 2, par)

        high_parts(0)
        values(0, 0)
        high_parts(1)
        values(1, 1)
        max_rows(0)
        body(0, 0, True, False, NB > 2)
        if NB > 2:
            if NB > 4:
                with pairs(act, 1, NB - 3) as n:
                    body(n, 1, False, False, True)
                    body(n + 1, 0, False, False, True)
            body(NB - 3, 1, False, False, True)
            body(NB - 2, 0, False, False, False)
        body(NB - 1, 1, False, True, False)
        spread(NB - 1)

    @block.tensor
    def _(pe):
        pe.wait_ge(g_step, 6 + C * K_SPARSE)
        for qc in range(C):
            for kc in range(C):
                pe.transpose(bank0[:, kc, qc * P:qc * P + P], cnt[:, qc, kc * P:kc * P + P], ident[:])
        for m in range(C):
            for k in range(C):
                ins = pe.matmul(ps_den[:, m:m + 1], wo[:, k, m * P:m * P + P], bias[:, 2, k:k + 1],
                                start=(k == 0), stop=(k == C - 1))
        ins.then_inc(setup_pe, 1)
        pe.wait_ge(setup_done, 1)

        def project(n, par):
            pe.wait_ge(d_xs[par], landed(n, par))
            if not (isinstance(n, int) and n < 2):
                at_least(pe, x1_done, n - 2)
                pe.wait_ge(v_done, n)
            elif n == 1:
                pe.wait_ge(v_done, 1)
            for m in range(C):
                for k in range(C):
                    ins = pe.matmul(bank0[:, m], wq[:, k, m * P:m * P + P], xs[par][:, k], start=(k == 0), stop=(k == C - 1))
            ins.then_inc(proj_q, 1)
            if isinstance(n, int) and n == 1:
                pe.wait_ge(klo_done, 1)
            elif isinstance(n, int) and n == 2:
                pe.wait_ge(mrow_done, 1)
            elif not (isinstance(n, int) and n == 0):
                pe.wait_ge(rrep_done, n - 2)
            for m in range(C):
                for k in range(C):
                    ins = pe.matmul(bank1[:, m], wk[:, k, m * P:m * P + P], xs[par][:, k], start=(k == 0), stop=(k == C - 1))
            ins.then_inc(proj_k, 1)
            pe.wait_ge(qf_done, n + 1)
            for m in range(C):
                for k in range(C):
                    ins = pe.matmul(bank0[:, m], xs[par][:, k, m * P:m * P + P], wv[:, k], start=(k == 0), stop=(k == C - 1))
            ins.then_inc(proj_v, 1)

        def score_rows(n, par, g):
            quad, qc = rows_group(g)
            if g == 0:
                pe.wait_ge(m_ready, n + 1)
            if g % 4 == 0:
                pe.wait_ge(d_stack[g // 4], (n + 1) * 16 * STACK_DMAS)
            at_least(pe, red_done, n * GROUPS + g)
            for b in range(2):
                pe.matmul(ps_s[:, b].rearrange("p (h k) -> p h k", h=2), ident_bf[:],
                          add_m[par][:, qc].unsqueeze(1).to_broadcast([P, 2, S]), start=True, stop=False)
                for r in range(2):
                    slot = 4 * quad + 2 * b + r
                    ins = pe.matmul(ps_s[:, b, r * S:r * S + S], q_st[par][0:96, slot, qc * P:qc * P + P],
                                    k_st[par][0:96, slot // 2], start=False, stop=(r == 1))
            ins.then_inc(s_done, 1)

        def score_cols(n, par, g):
            quad, kc = rows_group(g)
            if g == 0:
                pe.wait_ge(d_max, 16 * (n + 1))
            at_least(pe, exp_done, n * GROUPS + g)
            for b in range(2):
                pair = 2 * quad + b
                ins = pe.matmul(ps_t[:, b].rearrange("p (h s) -> p h s", h=2), k_st[par][0:97, pair, kc * P:kc * P + P],
                                q_st[par][0:97, 2 * pair:2 * pair + 2], start=True, stop=True)
            ins.then_inc(t_done, 1)

        def mix_values(n, par, g):
            quad, kc = rows_group(g)
            pe.wait_ge(p_done, n * GROUPS + g + 1)
            if g == 0:
                pe.wait_ge(v_done, n + 1)
                at_least(pe, att_done, n)
                at_least(pe, rden_done, n)
            for j in range(4):
                ins = pe.matmul(ps_o[32 * j:32 * j + 32, quad // 2], v_pad[par][:, kc, 4 * quad + j], e[g % E_BUFS][:, j],
                          start=(g == 0), stop=(g == GROUPS - 1), tile_position=(0, 32 * j), skip_group_check=True)
            if g % 4 == 2:
                ins.then_inc(stack_free[g // 4], 1)
            for j in range(4):
                ins = pe.matmul(ps_den[32 * j:32 * j + 32, 0:S], sel_den[:, quad], e[g % E_BUFS][:, j],
                                start=(g == 0), stop=(g == GROUPS - 1), tile_position=(0, 32 * j))
            ins.then_inc(pv_done, 1)

        def transpose_max(n):
            pe.wait_ge(red_done, (n + 1) * GROUPS)
            if isinstance(n, int) and n + 1 >= NB:
                at_least(pe, rrep_done, NB - 2)
                pe.wait_ge(klo_done, NB)
                pe.wait_ge(mrow_done, n)
            else:
                pe.wait_ge(klo_done, n + 2)
            for qc in range(C):
                ins = pe.transpose(bank1[0:HEADS, 0, qc * P:qc * P + P], neg_max[:, qc], ident[:])
            ins.then_inc(mt_done, 1)

        def spread(n):
            pe.wait_ge(rden_done, n + 1)
            if isinstance(n, int) and n == NB - 1:
                pe.wait_ge(rrep_done, n)
            else:
                pe.wait_ge(mrow_done, n + 2)
            for c in range(C):
                ins = pe.matmul(bank1[:, c], sel_rep[:, c], r_den[:], start=True, stop=True)
            ins.then_inc(rep_done, 1)

        def project_out(n):
            pe.wait_ge(att_done, n + 1)
            if isinstance(n, int) and n + 3 > NB:
                at_least(pe, x1_done, n)
            else:
                pe.wait_ge(v_done, n + 3)
            for m in range(C):
                for k in range(C):
                    ins = pe.matmul(bank0[:, m], wo[:, k, m * P:m * P + P], att[:, k], start=(k == 0), stop=(k == C - 1))
            ins.then_inc(wo_done, 1)

        def body(n, par, first, last, proj):
            for g in range(GROUPS):
                if not last:
                    score_rows(n + 1, 1 - par, g)
                score_cols(n, par, g)
                if g == 0 and not first:
                    spread(n - 1)
                if g > 0:
                    mix_values(n, par, g - 1)
                if g == 1 and not first:
                    project_out(n - 1)
                if g == 2 and proj:
                    project(n + 2, par)
            if not last:
                transpose_max(n + 1)
            mix_values(n, par, GROUPS - 1)

        project(0, 0)
        project(1, 1)
        for g in range(GROUPS):
            score_rows(0, 0, g)
        transpose_max(0)
        body(0, 0, True, False, NB > 2)
        if NB > 2:
            if NB > 4:
                with pairs(pe, 1, NB - 3) as n:
                    body(n, 1, False, False, True)
                    body(n + 1, 0, False, False, True)
            body(NB - 3, 1, False, False, True)
            body(NB - 2, 0, False, False, False)
        body(NB - 1, 1, False, True, False)
        spread(NB - 1)
        project_out(NB - 1)

TRACES = 32
HID1 = 64
STEP = 8
CHUNKS = S // STEP
LATE = 16
TABLE = CHUNKS + LATE


def trace_layer(nc, sem_ctx, ctx, t, X, NB, consts):
    def sb(name, shape, dt=F32):
        return ctx.enter_context(nc.sbuf_tensor("b_" + name, shape, dt))

    def ps(name, shape, dt=F32):
        return ctx.enter_context(nc.psum_tensor("b_" + name, shape, dt))

    def sem(name):
        return sem_ctx.enter_context(nc.semaphore("b_" + name))

    ident = consts["ident"]
    wg = sb("wg", [P, 2 * C, D])
    wn1 = sb("wn1", [P, C, HID1])
    wn2 = sb("wn2", [HID1 + 1, TRACES])
    wn2_3 = sb("wn2_3", [HID1 + 1, 3 * TRACES])
    wsoma, wtemp, wout = sb("wsoma", [P, C, D]), sb("wtemp", [P, C, D]), sb("wout", [P, C, D])
    bg_h, bsoma, btemp_h, gamma, beta = (sb(n, [P, C]) for n in ("bg", "bsoma", "btemp", "gamma", "beta"))
    bn1 = sb("bn1", [HID1, 1])
    tau_c = sb("tau_c", [P, 1])
    tau_col = sb("tau_col", [P, 1])
    tau_row = sb("tau_row", [P, TRACES])
    sp_c, sp_col, sp_row = sb("sp_c", [P, 1]), sb("sp_col", [P, 1]), sb("sp_row", [P, TRACES])
    alpha_c = sb("alpha_c", [P, 1])
    lag_n = sb("lag_n", [P, TABLE])
    lag_on = sb("lag_on", [P, TABLE])
    ramp = sb("ramp", [P, 32])
    own = sb("own", [P, 32])
    table = sb("table", [P, TABLE, TRACES])
    spread_w = sb("spread_w", [P, 32])
    power = sb("power", [P, STEP])
    blend_t = sb("blend_t", [P, C, TRACES])
    bl_max = sb("bl_max", [P, C])
    bl_sum = sb("bl_sum", [P, C])
    bl_inv = sb("bl_inv", [P, C])
    bl_rep = sb("bl_rep", [P, C, 4, TRACES])
    w_rep = sb("w_rep", [P, D])
    w_lag = sb("w_lag", [P, STEP, D])
    w_st = sb("w_st", [P, STEP, D], F32R)
    mean_w = sb("mean_w", [P, C])
    mean_mat = sb("mean_mat", [P, P])
    eps = sb("eps", [P, 1])

    ctx_e = sb("ctx_e", [P, C, S])
    th_g = sb("th_g", [P, C, S])
    gated = [sb(f"gated{i}", [P, C, S]) for i in range(2)]
    gated_t = [sb(f"gated_t{i}", [P, C, D]) for i in range(2)]
    h1 = sb("h1", [HID1 + 1, S])
    th_m = sb("th_m", [3 * TRACES, S])
    mod_f = sb("mod_f", [3 * TRACES, S])
    mod_st = [sb(f"mod_st{i}", [3 * TRACES, S], F32R) for i in range(2)]
    th_t = sb("th_t", [P, C, TRACES])
    mod_t = sb("mod_t", [P, C, TRACES])
    decayed = [sb(f"decayed{i}", [P, TABLE, TRACES]) for i in range(2)]
    state = [sb(f"state{i}", [P, 2, D]) for i in range(2)]
    inner = sb("inner", [P, C, S])
    prod = [sb(f"prod{i}", [P, C, S]) for i in range(2)]
    outer_t = sb("outer_t", [P, C, D])
    temporal = sb("temporal", [P, C, S])
    th_o = sb("th_o", [P, C, S])
    soma = sb("soma", [P, C, S])
    mixed = sb("mixed", [P, C, S])
    square = sb("square", [P, C, S])
    std = sb("std", [P, S])
    rstd = sb("rstd", [P, S])
    normed = sb("normed", [P, C, S])
    scaled = sb("scaled", [P, C, S])

    pA = ps("pA", [P, C, S])
    pB = ps("pB", [P, 2, S])
    pS = [ps(f"pS{i}", [P, 2, D]) for i in range(2)]
    pL = [ps(f"pL{i}", [P, C, S]) for i in range(2)]
    pY = ps("pY", [P, C, S])
    pZ = ps("pZ", [P, C, S])

    d_in, v_step, a_set, a_bl, pe_set, set_done = (sem(n) for n in ("d_in", "v_step", "a_set", "a_bl", "pe_set", "set_done"))
    ctx_done, wg_done, thg_done, gated_done = (sem(n) for n in ("ctx", "wg", "thg", "gated"))
    h1_done, gelu1_done, mod_done, thm_done, modst_done, vmod = (sem(n) for n in ("h1", "gelu1", "mod", "thm", "modst", "vmod"))
    modt_done, tht_done, modt_ready, dec_done = (sem(n) for n in ("modt", "tht", "modt_ready", "dec"))
    gt_done, gtev_done = sem("gt"), sem("gtev")
    st_done, sw_done, yin_done, yev_done, ytr_done = (sem(n) for n in ("st", "sw", "yin", "yev", "ytr"))
    lag_done, prod_done, inner_done, temp_done = (sem(n) for n in ("lag", "prod", "inner", "temp"))
    soma_mm, soma_done, gate_mm, tho_done, mixed_done = (sem(n) for n in ("soma_mm", "soma", "gate_mm", "tho", "mixed"))
    out_mm, sq_done, var_mm, std_done, rstd_done, normed_done, scaled_done, x2_done = (
        sem(n) for n in ("out_mm", "sq", "var_mm", "std", "rstd", "normed", "scaled", "x2"))

    LOADS = ("wg", "wn1", "wn2", "wn2_3", "wsoma", "wtemp", "wout", "bg", "bn1", "bsoma", "btemp", "gamma", "beta",
             "tau_c", "tau_col", "tau_row", "lag_n", "lag_on", "ramp", "own", "blend_t")
    tiles = dict(zip(LOADS, (wg, wn1, wn2, wn2_3, wsoma, wtemp, wout, bg_h, bn1, bsoma, btemp_h, gamma, beta,
                             tau_c, tau_col, tau_row, lag_n, lag_on, ramp, own, blend_t)))

    def xn(n, k=None):
        at = slice(n * S, n * S + S) if isinstance(n, int) else bass.ds(n * S, S)
        return X[:, :, at] if k is None else X[:, k, at]

    def rows(w):
        return w[:].rearrange("p c s -> p (c s)")

    block = ctx.enter_context(nc.Block())

    def loop(eng, body):
        body(0, 0, True, False)
        if NB > 2:
            with pairs(eng, 1, NB - 1) as n:
                body(n, 1, True, True)
                body(n + 1, 0, True, True)
        body(NB - 1, 1, False, True)

    @block.sync
    def _(sp):
        for name in LOADS:
            src = t[name]
            if name in ("wg", "wn1", "wsoma", "wtemp", "wout", "blend_t"):
                src = src.rearrange("(k p) e -> p k e", p=P)
            if name in ("tau_c", "tau_row"):
                src = src.partition_broadcast(P)
            sp.dma_start(tiles[name][:], src).then_inc(d_in, 16)

    @block.gpsimd
    def _(pool):
        pool.memset(h1[HID1:HID1 + 1], 1.0).then_inc(set_done, 1)
        pool.wait_ge(set_done, 2)

        def decays(n, par):
            pool.wait_ge(modt_ready, n + 1)
            if not (isinstance(n, int) and n < 2):
                pool.wait_ge(st_done, (n - 1) * 4)
            for k, lo, cnt in ((0, 0, CHUNKS), (1, CHUNKS, LATE)):
                ins = pool.tensor_tensor(decayed[par][:, lo:lo + cnt], table[:, lo:lo + cnt],
                                         mod_t[:, k].unsqueeze(1).to_broadcast([P, cnt, TRACES]), ALU.mult)
            ins.then_inc(dec_done, 1)

        def residual(n):
            pool.wait_ge(scaled_done, n + 1)
            pool.tensor_tensor(xn(n), scaled[:], xn(n), ALU.add).then_inc(x2_done, 1)

        def body(n, par, has_a, has_c):
            if has_c:
                residual(n - 1)
            if has_a:
                decays(n + 1, 1 - par)

        decays(0, 0)
        loop(pool, body)
        residual(NB - 1)
        pool.wait_ge(x2_done, NB)

    @block.vector
    def _(dve):
        done = [0]

        def link(ins):
            done[0] += 1
            ins.then_inc(v_step, 1)
            dve.wait_ge(v_step, done[0])

        dve.wait_ge(d_in, 16 * len(LOADS))
        link(dve.memset(eps[:], 1e-5))
        link(dve.memset(mean_mat[:], 1.0 / D))
        for tau in (tau_c, tau_col, tau_row):
            link(dve.tensor_scalar(tau[:], tau[:], 80.0, None, ALU.min))
        link(dve.tensor_reduce(bl_max[:], blend_t[:], AX.X, ALU.max, negate=True))
        dve.wait_ge(a_set, 1)
        for sp_, tau in ((sp_c, tau_c), (sp_col, tau_col), (sp_row, tau_row)):
            link(dve.tensor_scalar(sp_[:], tau[:], 1.0, None, ALU.add))
        dve.wait_ge(a_set, 2)
        for sp_ in (sp_c, sp_col, sp_row):
            link(dve.tensor_scalar(sp_[:], sp_[:], -1.0, None, ALU.mult))
        link(dve.tensor_tensor(table[:], lag_n[:].unsqueeze(2).to_broadcast([P, TABLE, TRACES]),
                               sp_row[:].unsqueeze(1).to_broadcast([P, TABLE, TRACES]), ALU.mult))
        link(dve.tensor_scalar(spread_w[:], ramp[:], sp_col[:], None, ALU.mult))
        link(dve.tensor_scalar(power[:], ramp[:, 0:STEP], -1.0, sp_col[:], ALU.add, ALU.mult))
        dve.wait_ge(a_bl, C)
        link(dve.tensor_reduce(bl_sum[:], blend_t[:], AX.X, ALU.add))
        link(dve.reciprocal(bl_inv[:], bl_sum[:]))
        for k in range(C):
            link(dve.tensor_scalar(blend_t[:, k], blend_t[:, k], bl_inv[:, k:k + 1], 0.5, ALU.mult, ALU.mult))
        link(dve.tensor_copy(bl_rep[:], blend_t[:].unsqueeze(2).to_broadcast([P, C, 4, TRACES])))
        link(dve.tensor_reduce(mean_w[:], wout[:], AX.X, ALU.add))
        link(dve.tensor_scalar(mean_w[:], mean_w[:], -1.0 / D, None, ALU.mult))
        for k in range(C):
            link(dve.tensor_scalar(wout[:, k], wout[:, k], mean_w[:, k:k + 1], 0.5, ALU.add, ALU.mult))
        link(dve.tensor_scalar(bg_h[:], bg_h[:], 0.5, None, ALU.mult))
        link(dve.tensor_scalar(btemp_h[:], btemp_h[:], 0.5, None, ALU.mult))
        dve.wait_ge(a_set, 3)
        link(dve.tensor_tensor(table[:], table[:], lag_on[:].unsqueeze(2).to_broadcast([P, TABLE, TRACES]), ALU.mult))
        link(dve.tensor_tensor(spread_w[:], spread_w[:], own[:], ALU.mult))
        dve.wait_ge(pe_set, 1)
        link(dve.tensor_copy(w_rep[:], pA[:, 0]))
        for lag in range(STEP):
            link(dve.tensor_scalar(w_lag[:, lag], w_rep[:], power[:, lag:lag + 1], None, ALU.mult))
        link(dve.tensor_copy(w_st[:], w_lag[:]))
        low = slice(2 * TRACES, 3 * TRACES)
        link(dve.tensor_tensor(w_st[low], w_lag[low], w_st[low].bitcast(F32), ALU.subtract))
        dve.sem_inc(set_done, 1)

        def context(n):
            at_least(dve, wg_done, n)
            for k in range(C):
                ins = dve.tensor_tensor_scan(ctx_e[:, k], alpha_c[:].to_broadcast([P, S]), xn(n, k), 0.0, ALU.mult, ALU.add)
            ins.then_inc(ctx_done, 1)

        def gating(n, par):
            dve.wait_ge(thg_done, n + 1)
            if not (isinstance(n, int) and n < 2):
                dve.wait_ge(inner_done, (STEP - 1) * (n - 1))
                dve.wait_ge(gt_done, n - 1)
            dve.scalar_tensor_tensor(out=gated[par][:], in0=th_g[:], scalar=1.0, in1=xn(n), op0=ALU.add, op1=ALU.mult)\
               .then_inc(gated_done, 1)

        def modulation(n, par):
            dve.wait_ge(thm_done, n + 1)
            if not (isinstance(n, int) and n < 2):
                dve.wait_ge(lag_done, (n - 1) * STEP)
            dve.tensor_scalar(mod_st[par][:], th_m[:], 0.5, 1.0, ALU.mult, ALU.add).then_inc(vmod, 1)
            low = slice(TRACES, 2 * TRACES)
            dve.tensor_scalar(mod_f[low], th_m[low], 0.5, 1.0, ALU.mult, ALU.add).then_inc(vmod, 1)
            dve.wait_ge(vmod, 2 * n + 2)
            dve.tensor_tensor(mod_st[par][low], mod_f[low], mod_st[par][low].bitcast(F32), ALU.subtract).then_inc(modst_done, 1)

        def states(n, q):
            dve.wait_ge(st_done, 4 * n + q + 1)
            if not (isinstance(n, int) and n == 0 and q < 2):
                dve.wait_ge(yin_done, 4 * n + q - 1)
            dve.tensor_tensor(state[q % 2][:], pS[q % 2][:], w_rep[:].unsqueeze(1).to_broadcast([P, 2, D]), ALU.mult)\
               .then_inc(sw_done, 1)

        def lag_sum(n, par, lag):
            dve.wait_ge(lag_done, STEP * n + lag + 1)
            m = rows(pL[lag % 2]).rearrange("p (a j) -> p a j", j=STEP)
            g = rows(gated[par]).rearrange("p (a j) -> p a j", j=STEP)
            if lag == 0:
                at_least(dve, temp_done, n)
                dve.tensor_tensor(rows(inner), rows(gated[par]), rows(pL[0]), ALU.mult).then_inc(prod_done, 1)
                return
            pr = rows(prod[lag % 2]).rearrange("p (a j) -> p a j", j=STEP)[:, :, 0:STEP - lag]
            dve.tensor_tensor(pr, g[:, :, 0:STEP - lag], m[:, :, 0:STEP - lag], ALU.mult).then_inc(prod_done, 1)
            dve.wait_ge(prod_done, STEP * n + lag + 1)
            if lag > 1:
                dve.wait_ge(inner_done, (STEP - 1) * n + lag - 1)
            y = rows(inner).rearrange("p (a j) -> p a j", j=STEP)[:, :, lag:STEP]
            dve.tensor_tensor(y, y, pr, ALU.add).then_inc(inner_done, 1)

        def total(n):
            dve.wait_ge(ytr_done, n + 1)
            dve.wait_ge(inner_done, (STEP - 1) * (n + 1))
            at_least(dve, gate_mm, n)
            dve.tensor_tensor(temporal[:], inner[:], pY[:], ALU.add).then_inc(temp_done, 1)

        def mixing(n):
            dve.wait_ge(tho_done, n + 1)
            dve.wait_ge(soma_done, n + 1)
            at_least(dve, out_mm, n)
            dve.scalar_tensor_tensor(out=mixed[:], in0=th_o[:], scalar=1.0, in1=soma[:], op0=ALU.add, op1=ALU.mult)\
               .then_inc(mixed_done, 1)

        def norm(n):
            dve.wait_ge(std_done, n + 1)
            at_least(dve, normed_done, n)
            dve.reciprocal(rstd[:], std[:]).then_inc(rstd_done, 1)
            dve.wait_ge(rstd_done, n + 1)
            at_least(dve, scaled_done, n)
            dve.tensor_tensor(normed[:], pZ[:], rstd[:].unsqueeze(1).to_broadcast([P, C, S]), ALU.mult).then_inc(normed_done, 1)

        def body(n, par, has_a, has_c):
            if has_a:
                context(n + 1)
            states(n, 0)
            states(n, 1)
            lag_sum(n, par, 0)
            if has_c:
                mixing(n - 1)
            lag_sum(n, par, 1)
            states(n, 2)
            if has_a:
                gating(n + 1, 1 - par)
            lag_sum(n, par, 2)
            lag_sum(n, par, 3)
            states(n, 3)
            if has_c:
                norm(n - 1)
            lag_sum(n, par, 4)
            if has_a:
                modulation(n + 1, 1 - par)
            for lag in (5, 6, 7):
                lag_sum(n, par, lag)
            total(n)

        context(0)
        gating(0, 0)
        modulation(0, 0)
        loop(dve, body)
        mixing(NB - 1)
        norm(NB - 1)

    @block.scalar
    def _(act):
        act.wait_ge(v_step, 6)
        for tau in (tau_c, tau_col):
            act.activation(tau[:], tau[:], ACT.Exp)
        act.activation(tau_row[:], tau_row[:], ACT.Exp).then_inc(a_set, 1)
        act.wait_ge(v_step, 9)
        for sp_ in (sp_c, sp_col):
            act.activation(sp_[:], sp_[:], ACT.Ln)
        act.activation(sp_row[:], sp_row[:], ACT.Ln).then_inc(a_set, 1)
        for k in range(C):
            act.activation(blend_t[:, k], blend_t[:, k], ACT.Exp, bias=bl_max[:, k:k + 1]).then_inc(a_bl, 1)
        act.wait_ge(v_step, 15)
        act.activation(alpha_c[:], sp_c[:], ACT.Exp)
        act.activation(table[:], table[:], ACT.Exp)
        act.activation(spread_w[:], spread_w[:], ACT.Exp)
        act.activation(power[:], power[:], ACT.Exp).then_inc(a_set, 1)
        act.wait_ge(set_done, 2)

        def input_gate(n):
            act.wait_ge(wg_done, n + 1)
            at_least(act, gated_done, n)
            for m in range(C):
                ins = act.activation(th_g[:, m], pA[:, m], ACT.Tanh, bias=bg_h[:, m:m + 1], scale=0.5)
            ins.then_inc(thg_done, 1)

        def hidden(n):
            act.wait_ge(h1_done, n + 1)
            at_least(act, modt_done, n)
            act.activation(h1[0:HID1], pB[0:HID1, 0], ACT.Gelu, bias=bn1[:]).then_inc(gelu1_done, 1)

        def mod_rows(n):
            act.wait_ge(mod_done, n + 1)
            at_least(act, modst_done, n)
            act.activation(th_m[:], pB[0:3 * TRACES, 1], ACT.Tanh, scale=0.5).then_inc(thm_done, 1)

        def mod_cols(n):
            act.wait_ge(modt_done, n + 1)
            act.activation(th_t[:], pB[:, 0, 0:C * TRACES].rearrange("p (c d) -> p c d", c=C), ACT.Tanh, scale=0.5)\
               .then_inc(tht_done, 1)
            act.wait_ge(tht_done, n + 1)
            at_least(act, dec_done, n)
            act.activation(mod_t[:], th_t[:], ACT.Copy, scale=0.5, bias=1.0).then_inc(modt_ready, 1)

        def turned(n, par):
            act.wait_ge(gt_done, n + 1)
            if not (isinstance(n, int) and n < 2):
                act.wait_ge(st_done, (n - 1) * 4)
            act.activation(gated_t[par][:], pA[:], ACT.Copy).then_inc(gtev_done, 1)

        def spread_out(n):
            act.wait_ge(yin_done, 4 * (n + 1))
            at_least(act, ytr_done, n)
            act.activation(outer_t[:], pY[:], ACT.Copy).then_inc(yev_done, 1)

        def somas(n):
            act.wait_ge(soma_mm, n + 1)
            at_least(act, mixed_done, n)
            for m in range(C):
                ins = act.activation(soma[:, m], pZ[:, m], ACT.Gelu, bias=bsoma[:, m:m + 1])
            ins.then_inc(soma_done, 1)

        def output_gate(n):
            act.wait_ge(gate_mm, n + 1)
            at_least(act, mixed_done, n)
            for m in range(C):
                ins = act.activation(th_o[:, m], pY[:, m], ACT.Tanh, bias=btemp_h[:, m:m + 1], scale=0.5)
            ins.then_inc(tho_done, 1)

        def squares(n):
            act.wait_ge(out_mm, n + 1)
            at_least(act, var_mm, n)
            act.activation(square[:], pZ[:], ACT.Square).then_inc(sq_done, 1)

        def deviation(n):
            act.wait_ge(var_mm, n + 1)
            at_least(act, rstd_done, n)
            act.activation(std[:], pY[:, 0], ACT.Sqrt, bias=eps[:]).then_inc(std_done, 1)

        def scaling(n):
            act.wait_ge(normed_done, n + 1)
            at_least(act, x2_done, n)
            for m in range(C):
                ins = act.activation(scaled[:, m], normed[:, m], ACT.Identity, bias=beta[:, m:m + 1], scale=gamma[:, m:m + 1])
            ins.then_inc(scaled_done, 1)

        def body(n, par, has_a, has_c):
            if has_c:
                output_gate(n - 1)
                squares(n - 1)
            if has_a:
                input_gate(n + 1)
            if has_c:
                deviation(n - 1)
            if has_a:
                hidden(n + 1)
                mod_rows(n + 1)
                mod_cols(n + 1)
            spread_out(n)
            if has_c:
                scaling(n - 1)
            if has_a:
                turned(n + 1, 1 - par)
            somas(n)

        input_gate(0)
        hidden(0)
        mod_rows(0)
        mod_cols(0)
        turned(0, 0)
        loop(act, body)
        output_gate(NB - 1)
        squares(NB - 1)
        deviation(NB - 1)
        scaling(NB - 1)

    @block.tensor
    def _(pe):
        pe.wait_ge(v_step, 20)
        for k in range(C):
            ins = pe.transpose(pA[:, 0, k * P:k * P + P], bl_rep[:, k].rearrange("p r d -> p (r d)"), ident[:])
        ins.then_inc(pe_set, 1)
        pe.wait_ge(set_done, 2)

        def gate_in(n):
            at_least(pe, tht_done, n)
            at_least(pe, thm_done, n)
            pe.wait_ge(ctx_done, n + 1)
            at_least(pe, gtev_done, n)
            for m in range(C):
                for k in range(2 * C):
                    rhs = xn(n, k) if k < C else ctx_e[:, k - C]
                    ins = pe.matmul(pA[:, m], wg[:, k, m * P:m * P + P], rhs, start=(k == 0), stop=(k == 2 * C - 1))
            ins.then_inc(wg_done, 1)

        def hidden(n):
            for k in range(C):
                ins = pe.matmul(pB[0:HID1, 0], wn1[:, k], xn(n, k), start=(k == 0), stop=(k == C - 1))
            ins.then_inc(h1_done, 1)

        def modulate(n):
            pe.wait_ge(gelu1_done, n + 1)
            pe.matmul(pB[0:3 * TRACES, 1], wn2_3[:], h1[:], start=True, stop=True).then_inc(mod_done, 1)
            pe.wait_ge(thm_done, n + 1)
            for k in range(C):
                ins = pe.matmul(pB[:, 0, k * TRACES:k * TRACES + TRACES], h1[:, k * P:k * P + P], wn2[:], start=True, stop=True)
            ins.then_inc(modt_done, 1)

        def turn(n, par):
            pe.wait_ge(gated_done, n + 1)
            pe.wait_ge(thg_done, n + 1)
            for k in range(C):
                for c in range(C):
                    ins = pe.transpose(pA[:, k, c * P:c * P + P], gated[par][:, c, k * P:k * P + P], ident[:])
            ins.then_inc(gt_done, 1)

        def states(n, par, q):
            if q == 0:
                pe.wait_ge(dec_done, n + 1)
                pe.wait_ge(gtev_done, n + 1)
            if not (isinstance(n, int) and n == 0 and q < 2):
                pe.wait_ge(sw_done, 4 * n + q - 1)
            for i in range(2):
                g = 2 * q + i
                late = g >= 4
                columns = (4 * g, CHUNKS + 4 * g - LATE) if late else (4 * g,)
                for k, lo in enumerate(columns):
                    ins = pe.matmul(pS[q % 2][:, i], decayed[par][:, lo:lo + 4].rearrange("p a d -> p (a d)"),
                                    gated_t[par][:, k], start=(k == 0), stop=(k == len(columns) - 1))
            ins.then_inc(st_done, 1)

        def spread(n, q):
            pe.wait_ge(sw_done, 4 * n + q + 1)
            if q == 0:
                at_least(pe, std_done, n)
            for i in range(2):
                j = (2 * q + i) % 4
                ins = pe.matmul(pY[32 * j:32 * j + 32, q // 2], spread_w[:], state[q % 2][:, i],
                                start=True, stop=True, tile_position=(0, 32 * j))
            ins.then_inc(yin_done, 1)

        def turn_back(n):
            pe.wait_ge(yev_done, n + 1)
            for k in range(C):
                for c in range(C):
                    ins = pe.transpose(pY[:, c, k * P:k * P + P], outer_t[:, k, c * P:c * P + P], ident[:])
            ins.then_inc(ytr_done, 1)

        def lags(n, par, lag):
            if lag == 0:
                pe.wait_ge(modst_done, n + 1)
            if not (isinstance(n, int) and n == 0 and lag < 2):
                pe.wait_ge(prod_done, STEP * n + lag - 1)
            for c in range(C):
                ins = pe.matmul(pL[lag % 2][:, c], w_st[0:3 * TRACES, lag, c * P:c * P + P], mod_st[par][:],
                                start=True, stop=True)
            ins.then_inc(lag_done, 1)

        def soma_in(n):
            at_least(pe, normed_done, n)
            for m in range(C):
                for k in range(C):
                    ins = pe.matmul(pZ[:, m], wsoma[:, k, m * P:m * P + P], xn(n, k), start=(k == 0), stop=(k == C - 1))
            ins.then_inc(soma_mm, 1)

        def gate_out(n):
            pe.wait_ge(temp_done, n + 1)
            for m in range(C):
                for k in range(C):
                    ins = pe.matmul(pY[:, m], wtemp[:, k, m * P:m * P + P], temporal[:, k], start=(k == 0), stop=(k == C - 1))
            ins.then_inc(gate_mm, 1)

        def output(n):
            pe.wait_ge(mixed_done, n + 1)
            for m in range(C):
                for k in range(C):
                    ins = pe.matmul(pZ[:, m], wout[:, k, m * P:m * P + P], mixed[:, k], start=(k == 0), stop=(k == C - 1))
            ins.then_inc(out_mm, 1)

        def mean_square(n):
            pe.wait_ge(sq_done, n + 1)
            pe.wait_ge(tho_done, n + 1)
            for k in range(C):
                ins = pe.matmul(pY[:, 0], mean_mat[:], square[:, k], start=(k == 0), stop=(k == C - 1))
            ins.then_inc(var_mm, 1)

        def body(n, par, has_a, has_c):
            states(n, par, 0)
            states(n, par, 1)
            lags(n, par, 0)
            lags(n, par, 1)
            if has_c:
                output(n - 1)
            if has_a:
                gate_in(n + 1)
            if has_c:
                mean_square(n - 1)
            lags(n, par, 2)
            if has_a:
                hidden(n + 1)
            spread(n, 0)
            states(n, par, 2)
            lags(n, par, 3)
            spread(n, 1)
            states(n, par, 3)
            lags(n, par, 4)
            if has_a:
                modulate(n + 1)
            spread(n, 2)
            lags(n, par, 5)
            spread(n, 3)
            lags(n, par, 6)
            lags(n, par, 7)
            if has_a:
                turn(n + 1, 1 - par)
            turn_back(n)
            soma_in(n)
            gate_out(n)

        gate_in(0)
        hidden(0)
        modulate(0)
        turn(0, 0)
        loop(pe, body)
        output(NB - 1)
        mean_square(NB - 1)

HIDDEN = 1024
HC = HIDDEN // P
ROUNDS = HC // 2
SHARED = 192
EXPERTS = 8
STAGES = 6


def expert_and_final(nc, sem_ctx, ctx, t, X, NB, consts):
    def sb(name, shape, dt=F32):
        return ctx.enter_context(nc.sbuf_tensor("c_" + name, shape, dt))

    def ps(name, shape, dt=F32):
        return ctx.enter_context(nc.psum_tensor("c_" + name, shape, dt))

    def sem(name):
        return sem_ctx.enter_context(nc.semaphore("c_" + name))

    ident = consts["ident"]
    w1 = sb("w1", [P, C, HIDDEN])
    b1 = sb("b1", [P, HC])
    w2a = sb("w2a", [P, HC, P])
    w2b = [sb(f"w2b{i}", [P, HC, P]) for i in range(2)]
    b2 = [sb(f"b2{i}", [P, C]) for i in range(2)]
    expert_i = sb("expert_i", [1, NB], I32)
    stage_i = sb("stage_i", [1, NB], I32)
    embed_all = sb("embed_all", [P, STAGES, S])
    embed = [sb(f"embed{i}", [P, S]) for i in range(2)]
    key_t = [sb(f"key_t{i}", [P, C, S]) for i in range(2)]
    value = [sb(f"value{i}", [P, C, D]) for i in range(2)]
    hid = [sb(f"hid{i}", [P, 2, S]) for i in range(2)]
    query = sb("query", [P, C, S])
    neg_max = sb("neg_max", [P, C])
    row_sum = sb("row_sum", [P, C])
    row_inv = sb("row_inv", [P, C])
    prob = sb("prob", [P, C, S])
    prob_t = sb("prob_t", [P, C, S])
    y = [sb(f"y{i}", [P, C, S]) for i in range(2)]

    pH = [ps(f"pH{i}", [P, 2, S]) for i in range(2)]
    pO, pS, pT, pV = (ps(n, [P, C, S]) for n in ("pO", "pS", "pT", "pV"))

    d_in = sem("d_in")
    d_exp, d_bias, d_emb, d_key, d_val, stored = ([sem(f"{n}{i}") for i in range(2)]
                                                  for n in ("d_exp", "d_bias", "d_emb", "d_key", "d_val", "stored"))
    hid_mm, hid_done, out_mm, x3_done = (sem(n) for n in ("hid_mm", "hid", "out_mm", "x3"))
    query_done, s_mm, max_done, exp_done, inv_done, prob_done = (sem(n) for n in ("query", "s_mm", "max", "exp", "inv", "prob"))
    t_mm, pt_done, v_mm, y_done = (sem(n) for n in ("t_mm", "pt", "v_mm", "y"))

    def xn(n, k):
        at = slice(n * S, n * S + S) if isinstance(n, int) else bass.ds(n * S, S)
        return X[:, k, at]

    def batch_of(src, n):
        if isinstance(n, int):
            return src[n]
        return src[bass.ds(n, 1)]

    LOADS = 12
    block = ctx.enter_context(nc.Block())

    def loop(eng, body):
        body(0, 0, False, NB == 1)
        if NB > 2:
            with pairs(eng, 1, NB - 1) as n:
                body(n, 1, True, False)
                body(n + 1, 0, True, False)
        body(NB - 1, 1, True, True)

    @block.sync
    def _(sp):
        sp.dma_start(expert_i[:], t["expert"]).then_inc(d_in, 16)
        sp.dma_start(stage_i[:], t["stage"]).then_inc(d_in, 16)
        sp.dma_start(w1[:], t["w1"].rearrange("(k p) e -> p k e", p=P)).then_inc(d_in, 16)
        sp.dma_start(b1[:], t["b1"]).then_inc(d_in, 16)
        w2 = t["w2"].rearrange("(k p) e -> p k e", p=P)
        sp.dma_start(w2a[:], w2[:, :, 0:P]).then_inc(d_in, 16)
        for i in range(2):
            sp.dma_start(w2b[i][:, :, 0:SHARED - P], w2[:, :, P:SHARED]).then_inc(d_in, 16)
            sp.dma_start(b2[i][:, 0:1], t["b2"][0:P]).then_inc(d_in, 16)
            sp.dma_start(b2[i][0:SHARED - P, 1:2], t["b2"][P:SHARED]).then_inc(d_in, 16)
        sp.dma_start(embed_all[:], t["embed"].partition_broadcast(P)).then_inc(d_in, 16)
        sp.wait_ge(d_in, 16 * LOADS)

        def load(n, par):
            at = slice(n, n + 1) if isinstance(n, int) else bass.ds(n, 1)
            expert = sp.value_load(expert_i[0:1, at], min_val=0, max_val=EXPERTS - 1)
            stage = sp.value_load(stage_i[0:1, at], min_val=0, max_val=STAGES - 1)
            if not (isinstance(n, int) and n < 2):
                sp.wait_ge(out_mm, (n - 1) * ROUNDS)
            sp.dma_start(w2b[par][:, :, SHARED - P:P], t["we"][bass.ds(expert, 1)].rearrange("o p k e -> p (o k) e")).then_inc(d_exp[par], 16)
            if not (isinstance(n, int) and n < 2):
                sp.wait_ge(x3_done, n - 1)
            sp.dma_start(b2[par][SHARED - P:P, 1:2], t["be"][bass.ds(expert, 1)].rearrange("o p f -> p (o f)")).then_inc(d_bias[par], 16)
            if not (isinstance(n, int) and n < 2):
                sp.wait_ge(query_done, n - 1)
            sp.dma_start(embed[par][:], embed_all[:, bass.ds(stage, 1)].rearrange("p o f -> p (o f)")).then_inc(d_emb[par], 16)
            if not (isinstance(n, int) and n < 2):
                sp.wait_ge(s_mm, n - 1)
            src = batch_of(t["keyT"], n)
            sp.dma_start(key_t[par][:], src.rearrange("(k p) s -> p k s", p=P) if isinstance(n, int)
                         else src.rearrange("o (k p) s -> p (o k) s", p=P)).then_inc(d_key[par], 16)
            if not (isinstance(n, int) and n < 2):
                sp.wait_ge(v_mm, n - 1)
            src = batch_of(t["key"], n)
            sp.dma_start(value[par][:], src.rearrange("(k p) s -> p k s", p=P) if isinstance(n, int)
                         else src.rearrange("o (k p) s -> p (o k) s", p=P)).then_inc(d_val[par], 16)

        def body(n, par, has_3, last):
            if not last:
                load(n + 1, 1 - par)

        load(0, 0)
        loop(sp, body)

    @block.gpsimd
    def _(pool):
        def store(n, par):
            pool.wait_ge(y_done, n + 1)
            dst = batch_of(t["out"], n)
            pool.dma_start(dst.rearrange("(k p) s -> p k s", p=P) if isinstance(n, int)
                           else dst.rearrange("o (k p) s -> p (o k) s", p=P), y[par][:]).then_inc(stored[par], 16)

        def body(n, par, has_3, last):
            if has_3:
                store(n - 1, 1 - par)

        loop(pool, body)
        store(NB - 1, 1)
        for par in range(2):
            pool.wait_ge(stored[par], landed(NB - 2 + par, par))

    @block.vector
    def _(dve):
        def residual(n, par):
            dve.wait_ge(out_mm, ROUNDS * (n + 1))
            dve.wait_ge(d_bias[par], landed(n, par))
            for k in range(C):
                ins = dve.scalar_tensor_tensor(out=xn(n, k), in0=pO[:, k], scalar=b2[par][:, k:k + 1], in1=xn(n, k),
                                               op0=ALU.add, op1=ALU.add)
            ins.then_inc(x3_done, 1)

        def queries(n, par):
            dve.wait_ge(x3_done, n + 1)
            dve.wait_ge(d_emb[par], landed(n, par))
            at_least(dve, s_mm, n)
            at = slice(n * S, n * S + S) if isinstance(n, int) else bass.ds(n * S, S)
            dve.tensor_tensor(query[:], X[:, :, at], embed[par][:].unsqueeze(1).to_broadcast([P, C, S]), ALU.add)\
               .then_inc(query_done, 1)

        def maxima(n):
            dve.wait_ge(s_mm, n + 1)
            dve.tensor_reduce(neg_max[:], pS[:], AX.X, ALU.max, negate=True).then_inc(max_done, 1)

        def normalize(n):
            dve.wait_ge(exp_done, n + 1)
            at_least(dve, prob_done, C * n)
            dve.reciprocal(row_inv[:], row_sum[:]).then_inc(inv_done, 1)
            dve.wait_ge(inv_done, n + 1)
            for k in range(C):
                dve.tensor_scalar(prob[:, k], prob[:, k], row_inv[:, k:k + 1], None, ALU.mult).then_inc(prob_done, 1)

        def final(n, par):
            dve.wait_ge(v_mm, n + 1)
            if not (isinstance(n, int) and n < 2):
                dve.wait_ge(stored[par], landed(n - 2, par))
            at = slice(n * S, n * S + S) if isinstance(n, int) else bass.ds(n * S, S)
            dve.tensor_tensor(y[par][:], pV[:], X[:, :, at], ALU.add).then_inc(y_done, 1)

        def body(n, par, has_3, last):
            if has_3:
                maxima(n - 1)
                normalize(n - 1)
                final(n - 1, 1 - par)
            residual(n, par)
            queries(n, par)

        loop(dve, body)
        maxima(NB - 1)
        normalize(NB - 1)
        final(NB - 1, 1)

    @block.scalar
    def _(act):
        act.wait_ge(d_in, 16 * LOADS)

        def hidden(n, r):
            act.wait_ge(hid_mm, ROUNDS * n + r + 1)
            if not (isinstance(n, int) and n == 0 and r < 2):
                act.wait_ge(out_mm, ROUNDS * n + r - 1)
            for i in range(2):
                ins = act.activation(hid[r % 2][:, i], pH[r % 2][:, i], ACT.Gelu, bias=b1[:, 2 * r + i:2 * r + i + 1])
            ins.then_inc(hid_done, 1)

        def exps(n):
            act.wait_ge(max_done, n + 1)
            at_least(act, t_mm, n)
            at_least(act, inv_done, n)
            for k in range(C):
                ins = act.activation(prob[:, k], pS[:, k], ACT.Exp, bias=neg_max[:, k:k + 1], accum_out=row_sum[:, k:k + 1])
            ins.then_inc(exp_done, 1)

        def turned(n):
            act.wait_ge(t_mm, n + 1)
            at_least(act, v_mm, n)
            act.activation(prob_t[:], pT[:], ACT.Copy).then_inc(pt_done, 1)

        def body(n, par, has_3, last):
            hidden(n, 0)
            hidden(n, 1)
            if has_3:
                exps(n - 1)
            hidden(n, 2)
            hidden(n, 3)
            if has_3:
                turned(n - 1)

        loop(act, body)
        exps(NB - 1)
        turned(NB - 1)

    @block.tensor
    def _(pe):
        pe.wait_ge(d_in, 16 * LOADS)

        def hidden(n, r):
            if not (isinstance(n, int) and n == 0 and r < 2):
                pe.wait_ge(hid_done, ROUNDS * n + r - 1)
            for i in range(2):
                m = 2 * r + i
                for k in range(C):
                    ins = pe.matmul(pH[r % 2][:, i], w1[:, k, m * P:m * P + P], xn(n, k), start=(k == 0), stop=(k == C - 1))
            ins.then_inc(hid_mm, 1)

        def output(n, par, r):
            pe.wait_ge(hid_done, ROUNDS * n + r + 1)
            if r == 0:
                pe.wait_ge(d_exp[par], landed(n, par))
                at_least(pe, x3_done, n)
            for i in range(2):
                m = 2 * r + i
                for half, w in enumerate((w2a, w2b[par])):
                    ins = pe.matmul(pO[:, half], w[:, m], hid[r % 2][:, i], start=(m == 0 and half == 0),
                                    stop=(m == HC - 1 and half == 1), skip_group_check=True)
            ins.then_inc(out_mm, 1)

        def scores(n, par):
            pe.wait_ge(query_done, n + 1)
            pe.wait_ge(d_key[par], landed(n, par))
            at_least(pe, exp_done, n)
            for m in range(C):
                for k in range(C):
                    ins = pe.matmul(pS[:, m], query[:, k, m * P:m * P + P], key_t[par][:, k], start=(k == 0), stop=(k == C - 1))
            ins.then_inc(s_mm, 1)

        def turn(n):
            pe.wait_ge(prob_done, C * (n + 1))
            at_least(pe, pt_done, n)
            for k in range(C):
                for m in range(C):
                    ins = pe.transpose(pT[:, m, k * P:k * P + P], prob[:, k, m * P:m * P + P], ident[:])
            ins.then_inc(t_mm, 1)

        def mix_values(n, par):
            pe.wait_ge(pt_done, n + 1)
            pe.wait_ge(d_val[par], landed(n, par))
            at_least(pe, y_done, n)
            for m in range(C):
                for k in range(C):
                    ins = pe.matmul(pV[:, m], value[par][:, k, m * P:m * P + P], prob_t[:, k], start=(k == 0), stop=(k == C - 1))
            ins.then_inc(v_mm, 1)

        def body(n, par, has_3, last):
            hidden(n, 0)
            hidden(n, 1)
            if has_3:
                scores(n - 1, 1 - par)
            output(n, par, 0)
            hidden(n, 2)
            output(n, par, 1)
            hidden(n, 3)
            output(n, par, 2)
            if has_3:
                turn(n - 1)
            output(n, par, 3)
            if has_3:
                mix_values(n - 1, 1 - par)

        loop(pe, body)
        scores(NB - 1, 1)
        turn(NB - 1)
        mix_values(NB - 1, 1)


def build_program(nc, t):
    NB = t["xT"].shape[0]
    with ExitStack() as whole:
        X = whole.enter_context(nc.sbuf_tensor("x_all", [P, C, NB * S], F32))
        shapes = {"ident": [P, P], "iota": [P, S], "sel_den": [P, 4, 32], "sel_rep": [P, C, P], "par_mask": [P, 2]}
        consts = {name: whole.enter_context(nc.sbuf_tensor(name, shape, F32)) for name, shape in shapes.items()}
        consts["ident_bf"] = whole.enter_context(nc.sbuf_tensor("ident_bf", [P, P], BF16))
        const_loaded = whole.enter_context(nc.semaphore("const_loaded"))
        const_cast = whole.enter_context(nc.semaphore("const_cast"))

        with nc.Block() as block:
            @block.sync
            def _(sp):
                for name in shapes:
                    sp.dma_start(consts[name][:], t[name]).then_inc(const_loaded, 16)
                sp.wait_ge(const_loaded, 16 * len(shapes))

            @block.vector
            def _(dve):
                dve.wait_ge(const_loaded, 16 * len(shapes))
                dve.tensor_copy(consts["ident_bf"][:], consts["ident"][:]).then_inc(const_cast, 1)
                dve.wait_ge(const_cast, 1)

        for layer in (attention_layer, trace_layer, expert_and_final):
            with ExitStack() as tiles:
                layer(nc, whole, tiles, t, X, NB, consts)



def shape_constants():
    import numpy as np
    p, o, i = np.arange(P), np.arange(P), np.arange(32)
    f = np.float32
    sel_den = np.stack([np.tile((i % 4 == q).astype(f), (P, 1)) for q in range(4)], 1)
    source = [32 * (o // 32) + 2 * c + o % 32 // 16 for c in range(C)]
    sel_rep = np.stack([(p[:, None] == s[None]).astype(f) for s in source], 1)
    before = np.concatenate([STEP * np.arange(CHUNKS)[None] - 1 - p[:, None],
                             STEP * np.arange(LATE, CHUNKS)[None] - 1 - P - p[:, None]], 1)
    return {
        "ident": np.eye(P, dtype=f), "iota": np.tile(np.arange(S, dtype=f), (P, 1)),
        "sel_den": sel_den, "sel_rep": sel_rep,
        "par_mask": np.stack([p // DH % 2 == 0, p // DH % 2 == 1], 1).astype(f),
        "lag_n": np.maximum(before, 0).astype(f), "lag_on": (before >= 0).astype(f),
        "ramp": np.tile((i % STEP + 1).astype(f), (P, 1)),
        "own": (p[:, None] // 32 == i[None] // STEP).astype(f),
    }


def layouts(a):
    import numpy as np

    def turned(w):
        return w.T

    def column(b):
        return b.reshape(-1, P).T

    def head_rows(w):
        return w.reshape((C, 2, 4, DH) + w.shape[1:]).swapaxes(1, 2).reshape(w.shape)

    l0, l1, l2 = ({k[8:]: v for k, v in a.items() if k.startswith(p)} for p in ("L0_cond_", "L1_cond_", "L2_cond_"))
    wn2 = np.concatenate([turned(a["cond_256"]), a["condB_bn2"][None]])
    out = {
        "xT": a["x"].transpose(0, 2, 1),
        "wq": turned(l0["Wq"]), "wk": turned(l0["Wk"]), "wv": turned(l0["Wv"]), "wo": head_rows(turned(l0["Wo"])),
        "bq": column(l0["bq"]), "bk": column(l0["bk"]), "bv": column(head_rows(l0["bv"])), "bo": column(l0["bo"]),
        "idx": a["itok_Sx32_0_1023"], "valid": a["mask_Sx32_bk1"],
        "mask": a["mask_SxS_bk0"], "maskT": turned(a["mask_SxS_bk0"]),
        "u": a["condB_uprev"],
        "wg": turned(l1["Wg"]), "wn1": turned(l1["Wn1"]), "wn2": wn2, "wn2_3": np.tile(wn2, (1, 3)),
        "wsoma": turned(l1["Wsoma"]), "wtemp": turned(l1["Wtemp"]), "wout": turned(l1["Wout"]),
        "bg": column(l1["bg"]), "bn1": l1["bn1"].reshape(-1, 1), "bsoma": column(l1["bsoma"]),
        "btemp": column(l1["btemp"]), "gamma": column(l1["gamma"]), "beta": column(l1["beta"]),
        "tau_c": l1["tau_ctx"].reshape(1), "tau_col": np.tile(a["condB_tauraws"], P // TRACES).reshape(P, 1),
        "tau_row": a["condB_tauraws"], "blend_t": turned(a["cond_1024"]),
        "w1": l2["W1"], "b1": column(l2["b1"]), "w2": l2["W2"], "b2": l2["b2"].reshape(-1, 1),
        "we": l2["We"].reshape(EXPERTS, HC, P, -1).swapaxes(1, 2), "be": l2["be"][:, :, None],
        "embed": a["L3_cond_braak_embed"], "expert": a["itok_B_0_7"][None], "stage": a["itok_B_0_5"][None],
        "key": a["fside_BxSxS_0"], "keyT": a["fside_BxSxS_0"].transpose(0, 2, 1),
    }
    out.update(shape_constants())
    return out


def kernel(**inputs):
    import numpy as np
    import concourse.bacc as bacc
    from concourse.bass_utils import run_bass_kernel_spmd

    data = layouts({name: np.asarray(a) for name, a in inputs.items()})
    nc = bacc.Bacc("TRN2", target_bir_lowering=False, num_devices=1)
    arrays, t = {}, {}
    for name, a in data.items():
        a = np.ascontiguousarray(a)
        arrays[f"in_{name}"] = a
        t[name] = nc.dram_tensor(f"in_{name}", a.shape, mybir.dt.from_np(a.dtype), kind="ExternalInput").ap()
    shape = data["xT"].shape
    t["out"] = nc.dram_tensor("out_0", shape, F32, kind="ExternalOutput").ap()
    build_program(nc, t)
    result = run_bass_kernel_spmd(nc, [arrays], core_ids=[0])
    return result.results[0]["out_0"].transpose(0, 2, 1)
```

```python
from contextlib import contextmanager, ExitStack

import concourse.bass as bass
from concourse import mybir

F32 = mybir.dt.float32
F32R = mybir.dt.float32r
BF16 = mybir.dt.bfloat16
I32 = mybir.dt.int32
U8 = mybir.dt.uint8
ALU = mybir.AluOpType
ACT = mybir.ActivationFunctionType
AX = mybir.AxisListType

P = 128
S = 256
D = 256
C = D // P
HEADS, DH = 16, 16
K_SPARSE = 32
NEG = -1.0e30
BIG = 3.0e38
GROUPS = 8
TERMS = 3
E_BUFS = 4


def at_least(eng, sem, value):
    if isinstance(value, int) and value <= 0:
        return
    eng.wait_ge(sem, value)


def rows_group(g):
    half, c, rows = g // 4, g // 2 % 2, g % 2
    return 2 * c + half, rows


def landed(n, par):
    return 8 * (n - par) + 16


@contextmanager
def pairs(eng, first, end):
    with eng.Fori(0, (end - first) // 2) as i:
        yield i * 2 + first


def attention_layer(nc, sem_ctx, ctx, t, X, NB, consts):
    def sb(name, shape, dt):
        return ctx.enter_context(nc.sbuf_tensor("a_" + name, shape, dt))

    def ps(name, shape, dt=F32):
        return ctx.enter_context(nc.psum_tensor("a_" + name, shape, dt))

    def sem(name):
        return sem_ctx.enter_context(nc.semaphore("a_" + name))

    ident, ident_bf, iota, sel_den, sel_rep = consts["ident"], consts["ident_bf"], consts["iota"], consts["sel_den"], consts["sel_rep"]

    wq, wk, wv, wo = (sb(n, [P, C, D], F32) for n in ("wq", "wk", "wv", "wo"))
    bias = sb("bias", [P, 4, C], F32)
    bq_s = sb("bq_s", [P, C, 2], F32)
    bo_all = sb("bo_all", [P, C], F32)
    par_mask = consts["par_mask"]
    xs = [sb(f"xs{i}", [P, C, S], F32) for i in range(2)]
    q_hi = sb("q_hi", [P, C, 2, S], F32R)
    q_lo = sb("q_lo", [P, C, 2, S], F32R)
    q_full = sb("q_full", [P, C, 2, S], F32)
    k_hi = sb("k_hi", [P, C, S], F32R)
    k_lo = sb("k_lo", [P, C, S], F32R)
    k_full = sb("k_full", [P, C, S], F32)
    delta = sb("delta", [P, C, S], F32)
    q_st = [sb(f"q_st{i}", [P, HEADS, S], F32R) for i in range(2)]
    k_st = [sb(f"k_st{i}", [P, HEADS // 2, S], F32R) for i in range(2)]
    v_pad = [sb(f"v_pad{i}", [P, C, HEADS, 32], F32) for i in range(2)]
    e = [sb(f"e{i}", [P, 4, S], F32) for i in range(E_BUFS)]
    neg_max = sb("neg_max", [P, C, HEADS], F32)
    max_row = sb("max_row", [HEADS, S], F32R)
    r_den = sb("r_den", [P, S], F32)
    r_rep = sb("r_rep", [P, C, S], F32)
    att = sb("att", [P, C, S], F32)
    u_all = sb("u_all", [P, NB], F32)
    lam = sb("lam", [P, NB], F32)
    decay = sb("decay", [P, NB], F32)
    mix = sb("mix", [P, NB, 4], F32)
    mix_m, mix_w = sb("mix_m", [P, 4], F32), sb("mix_w", [P, 4], F32)
    idx_i = sb("idx_i", [P, C, K_SPARSE], I32)
    idx_f = sb("idx_f", [P, C, K_SPARSE], F32)
    val_u = sb("val_u", [P, C, K_SPARSE], U8)
    val_f = sb("val_f", [P, C, K_SPARSE], F32)
    cnt = sb("cnt", [P, C, S], F32)
    cnt_t = sb("cnt_t", [P, C, S], F32)
    absent = sb("absent", [P, C, S], F32)
    msk_u = sb("msk_u", [P, 2, C, S], U8)
    off = sb("off", [P, C, S], F32)
    off_t = sb("off_t", [P, C, S], F32)
    w_off, w_cnt, m_off, m_abs = (sb(n, [P, C, S], F32) for n in ("w_off", "w_cnt", "m_off", "m_abs"))
    w_t = [sb(f"w_t{i}", [P, C, S], F32) for i in range(2)]
    add_m = [sb(f"add_m{i}", [P, C, S], BF16) for i in range(2)]

    ps_s = [ps(f"s{b}", [P, 2, S]) for b in range(2)]
    ps_t = [ps(f"t{b}", [P, 2, S]) for b in range(2)]
    ps_o = ps("o", [P, C, S])
    ps_den = ps("den", [P, 512])
    bank0 = ps("bank0", [P, C, S])
    bank1 = ps("bank1", [P, C, S])

    d_w, d_small = sem("d_w"), sem("d_small")
    g_ready, g_step, s_ready, a_step = sem("g_ready"), sem("g_step"), sem("s_ready"), sem("a_step")
    setup_pe, setup_done = sem("setup_pe"), sem("setup_done")
    d_xs, d_x = [sem("d_xs0"), sem("d_xs1")], sem("d_x")
    stack_free = [sem("stack_free0"), sem("stack_free1")]
    proj_q, proj_k, proj_v = sem("proj_q"), sem("proj_k"), sem("proj_v")
    qf_done, qhi_done, qlo_done, khi_done, klo_done, v_done = (sem(n) for n in ("qf", "qhi", "qlo", "khi", "klo", "v"))
    d_stack, d_max = [sem("d_stack0"), sem("d_stack1")], sem("d_max")
    s_done, red_done = sem("s_done"), sem("red_done")
    t_done, exp_done, p_done, pv_done = sem("t_done"), sem("exp_done"), sem("p_done"), sem("pv_done")
    mt_done, mrow_done = sem("mt_done"), sem("mrow_done")
    rden_done, rep_done, rrep_done, att_done, wo_done, x1_done = (sem(n) for n in ("rden", "rep", "rrep", "att", "wo", "x1"))
    mix_done, mixm_done, mixw_done, m_step, w_step, w_ready, m_ready = (
        sem(n) for n in ("mix", "mixm", "mixw", "m_step", "w_step", "w_ready", "m_ready"))
    kf_done, delta_done = sem("kf"), sem("delta")
    zero_done = sem("zero")

    def batches(eng, body):
        body(0, 0, True, True, False)
        body(1, 1, True, True, True)
        if NB > 4:
            with pairs(eng, 2, NB - 2) as n:
                body(n, 0, True, True, True)
                body(n + 1, 1, True, True, True)
        body(NB - 2, 0, False, True, True)
        body(NB - 1, 1, False, False, True)

    N_W = 4
    STACK_DMAS = 2 * TERMS * 2

    block = ctx.enter_context(nc.Block())

    @block.sync
    def _(sp):
        for w, name in ((wq, "wq"), (wk, "wk"), (wv, "wv"), (wo, "wo")):
            sp.dma_start(w[:], t[name].rearrange("(k p) e -> p k e", p=P)).then_inc(d_w, 16)
        for n in range(2):
            sp.dma_start(xs[n][:], t["xT"][n].rearrange("(k p) s -> p k s", p=P)).then_inc(d_xs[n], 16)

        def stack(n, par, half):
            sp.wait_ge(stack_free[half], n + 1)
            for done, dst, src, terms in ((khi_done, k_st[par], k_hi, (0, 1)), (qhi_done, q_st[par], q_hi, (0, 2)),
                                          (klo_done, k_st[par], k_lo, (2,)), (qlo_done, q_st[par], q_lo, (1,))):
                sp.wait_ge(done, n + 1)
                for term in terms:
                    for j in (2 * half, 2 * half + 1):
                        rows = src[32 * j:32 * j + 32].bitcast(F32)
                        to = dst[32 * term:32 * term + 32].bitcast(F32)
                        to = (to.rearrange("p (c j r) s -> p j c r s", c=C, j=4) if dst is q_st[par]
                              else to.rearrange("p (c j) s -> p j c s", c=C))
                        sp.dma_start(to[:, j], rows).then_inc(d_stack[half], 16)

        def maxima(n, par):
            sp.wait_ge(mrow_done, n + 1)
            sp.dma_start(q_st[par][96:97].bitcast(F32), max_row[:].bitcast(F32)).then_inc(d_max, 16)

        stack(0, 0, 0)
        stack(0, 0, 1)
        stack(1, 1, 0)
        maxima(0, 0)

        def staged(n, par):
            sp.wait_ge(proj_v, n - 1)
            sp.dma_start(xs[par][:], t["xT"][bass.ds(n, 1)].rearrange("o (k p) s -> p (o k) s", p=P)
                         if not isinstance(n, int) else t["xT"][n].rearrange("(k p) s -> p k s", p=P)).then_inc(d_xs[par], 16)

        def body(n, par, proj, maxi, finish):
            if proj:
                staged(n + 2, par)
            if maxi:
                stack(n + 1, 1 - par, 1)
            at_least(sp, d_x, n * 16)
            sp.dma_start(X[:, :, bass.ds(n * S, S)] if not isinstance(n, int) else X[:, :, n * S:n * S + S],
                         t["xT"][bass.ds(n, 1)].rearrange("o (k p) s -> p (o k) s", p=P)
                         if not isinstance(n, int) else t["xT"][n].rearrange("(k p) s -> p k s", p=P)).then_inc(d_x, 16)
            if proj:
                stack(n + 2, par, 0)
            if maxi:
                maxima(n + 1, 1 - par)

        batches(sp, body)

    @block.gpsimd
    def _(pool):
        for half in stack_free:
            pool.sem_inc(half, 2)
        for i in range(2):
            pool.memset(k_st[i][96:97].bitcast(F32), 1.0).then_inc(zero_done, 1)
            pool.wait_ge(zero_done, 2 * i + 1)
            pool.memset(v_pad[i][:], 0.0).then_inc(zero_done, 1)
            pool.wait_ge(zero_done, 2 * i + 2)
        pool.dma_start(idx_i[:], t["idx"].rearrange("(k p) j -> p k j", p=P)).then_inc(d_small, 16)
        pool.dma_start(val_u[:], t["valid"].rearrange("(k p) j -> p k j", p=P)).then_inc(d_small, 16)
        pool.dma_start(msk_u[:, 0], t["mask"].rearrange("(k p) s -> p k s", p=P)).then_inc(d_small, 16)
        pool.dma_start(msk_u[:, 1], t["maskT"].rearrange("(k p) s -> p k s", p=P)).then_inc(d_small, 16)
        pool.dma_start(u_all[:], t["u"].partition_broadcast(P)).then_inc(d_small, 16)
        for i, name in enumerate(("bq", "bk", "bv", "bo")):
            pool.dma_start(bias[:, i], t[name]).then_inc(d_small, 16)
        pool.wait_ge(mix_done, 1)
        pool.wait_ge(setup_done, 1)

        def masks(n, par):
            pool.tensor_copy(mix_m[:], mix[:, n] if isinstance(n, int) else mix[:, bass.ds(n, 1)].rearrange("p o f -> p (o f)"))\
                .then_inc(mixm_done, 1)
            at_least(pool, m_ready, n)
            pool.wait_ge(mixm_done, n + 1)
            pool.tensor_tensor(m_abs[:], absent[:], mix_m[:, 0:1].unsqueeze(2).to_broadcast([P, C, S]), ALU.mult).then_inc(m_step, 1)
            pool.tensor_scalar(m_off[:], off[:], mix_m[:, 3:4], None, ALU.mult).then_inc(m_step, 1)
            pool.wait_ge(m_step, n * 2 + 2)
            if not (isinstance(n, int) and n < 2):
                pool.wait_ge(s_done, (n - 1) * 2 * GROUPS)
            pool.tensor_tensor(add_m[par][:], m_off[:], m_abs[:], ALU.add).then_inc(m_ready, 1)

        def weights(n, par):
            pool.tensor_copy(mix_w[:], mix[:, n] if isinstance(n, int) else mix[:, bass.ds(n, 1)].rearrange("p o f -> p (o f)"))\
                .then_inc(mixw_done, 1)
            at_least(pool, w_ready, n)
            pool.wait_ge(mixw_done, n + 1)
            pool.tensor_tensor(w_cnt[:], cnt_t[:], mix_w[:, 0:1].unsqueeze(2).to_broadcast([P, C, S]), ALU.mult).then_inc(w_step, 1)
            pool.tensor_scalar(w_off[:], off_t[:], mix_w[:, 2:3], mix_w[:, 1:2], ALU.mult, ALU.add).then_inc(w_step, 1)
            pool.wait_ge(w_step, n * 2 + 2)
            if not (isinstance(n, int) and n < 2):
                pool.wait_ge(p_done, (n - 1) * GROUPS)
            pool.tensor_tensor(w_t[par][:], w_off[:], w_cnt[:], ALU.add).then_inc(w_ready, 1)

        def low_parts(n):
            pool.wait_ge(khi_done, n + 1)
            pool.tensor_tensor(k_lo[:], k_full[:], k_hi[:].bitcast(F32), ALU.subtract).then_inc(klo_done, 1)
            pool.wait_ge(qhi_done, n + 1)
            pool.tensor_tensor(q_lo[:], q_full[:], q_hi[:].bitcast(F32), ALU.subtract).then_inc(qlo_done, 1)

        def residual(n):
            pool.wait_ge(delta_done, n + 1)
            pool.wait_ge(d_x, 16 * (n + 1))
            xo = X[:, :, n * S:n * S + S] if isinstance(n, int) else X[:, :, bass.ds(n * S, S)]
            pool.tensor_tensor(xo, delta[:], xo, ALU.add).then_inc(x1_done, 1)

        def body(n, par, proj, maxi, finish):
            if proj:
                masks(n + 2, par)
            if maxi:
                weights(n + 1, 1 - par)
            if proj:
                low_parts(n + 2)
            if finish:
                residual(n - 1)

        masks(0, 0)
        weights(0, 0)
        masks(1, 1)
        low_parts(0)
        low_parts(1)
        batches(pool, body)
        residual(NB - 1)
        pool.wait_ge(x1_done, NB)

    @block.vector
    def _(dve):
        done = [0]

        def link(ins):
            done[0] += 1
            ins.then_inc(g_step, 1)
            dve.wait_ge(g_step, done[0])

        dve.wait_ge(d_w, 16 * N_W)
        dve.wait_ge(d_small, 16 * 9)
        dve.tensor_scalar(wq[:], wq[:], 0.25, None, ALU.mult).then_inc(s_ready, 1)
        for par in range(2):
            dve.tensor_scalar(bq_s[:, :, par], bias[:, 0], par_mask[:, par:par + 1], 0.25, ALU.mult, ALU.mult).then_inc(s_ready, 1)

        link(dve.tensor_copy(idx_f[:], idx_i[:]))
        link(dve.tensor_copy(val_f[:], val_u[:]))
        link(dve.tensor_scalar(idx_f[:], idx_f[:], 1.0, None, ALU.add))
        link(dve.tensor_tensor(idx_f[:], idx_f[:], val_f[:], ALU.mult))
        link(dve.tensor_scalar(idx_f[:], idx_f[:], -1.0, None, ALU.add))
        link(dve.memset(cnt[:], 0.0))
        base = done[0]
        for j in range(K_SPARSE):
            for k in range(C):
                if j:
                    dve.wait_ge(g_step, base + (j - 1) * C + k + 1)
                dve.scalar_tensor_tensor(out=cnt[:, k], in0=iota[:], scalar=idx_f[:, k, j:j + 1], in1=cnt[:, k],
                                         op0=ALU.is_equal, op1=ALU.add).then_inc(g_step, 1)
        done[0] = base + C * K_SPARSE
        dve.wait_ge(g_step, done[0])
        link(dve.tensor_scalar(absent[:], cnt[:], 0.0, NEG, ALU.is_equal, ALU.mult))
        link(dve.tensor_copy(off[:], msk_u[:, 0]))
        link(dve.tensor_copy(off_t[:], msk_u[:, 1]))
        link(dve.tensor_scalar(off[:], off[:], -1.0, 1.0, ALU.mult, ALU.add))
        link(dve.tensor_scalar(off_t[:], off_t[:], -1.0, 1.0, ALU.mult, ALU.add))
        dve.wait_ge(a_step, 1)
        dve.tensor_scalar(lam[:], lam[:], 10.0, None, ALU.mult).then_inc(g_ready, 1)
        dve.wait_ge(g_ready, 1)
        dve.wait_ge(a_step, 2)
        link(dve.tensor_scalar(mix[:, :, 0], lam[:], 1.0, None, ALU.is_ge))
        link(dve.tensor_scalar(mix[:, :, 1], mix[:, :, 0], -1.0, 1.0, ALU.mult, ALU.add))
        link(dve.tensor_scalar(decay[:], decay[:], -1.0, None, ALU.add))
        link(dve.tensor_tensor(mix[:, :, 2], mix[:, :, 1], decay[:], ALU.mult))
        link(dve.tensor_scalar(lam[:], lam[:], 1.0, -1.0, ALU.min, ALU.mult))
        dve.tensor_tensor(mix[:, :, 3], mix[:, :, 1], lam[:], ALU.mult).then_inc(mix_done, 1)
        dve.wait_ge(setup_pe, 1)
        for k in range(C):
            dve.tensor_copy(cnt_t[:, k], bank0[:, k]).then_inc(g_step, 1)
        dve.tensor_tensor(bo_all[:], ps_den[:, 0:C], bias[:, 3], ALU.add).then_inc(s_ready, 1)
        done[0] += 2
        dve.wait_ge(g_step, done[0])
        dve.wait_ge(s_ready, 4)
        dve.sem_inc(setup_done, 1)

        def row_max(n, g):
            quad, qc = rows_group(g)
            if g == 0:
                at_least(dve, mt_done, n)
            for b in range(2):
                dve.wait_ge(s_done, 2 * (n * GROUPS + g) + b + 1)
                head = 4 * quad + 2 * b
                dve.tensor_reduce(neg_max[:, qc, head:head + 2], ps_s[b][:], AX.X, ALU.max, negate=True).then_inc(red_done, 1)

        def weigh(n, par, g):
            kc = g % 2
            dve.wait_ge(exp_done, 2 * (n * GROUPS + g + 1))
            if g == 0:
                dve.wait_ge(w_ready, n + 1)
            buf = e[g % E_BUFS]
            dve.scalar_tensor_tensor(out=buf[:], in0=buf[:], scalar=BIG,
                                     in1=w_t[par][:, kc].unsqueeze(1).to_broadcast([P, 4, S]),
                                     op0=ALU.min, op1=ALU.mult).then_inc(p_done, 1)

        def reciprocal(n):
            dve.wait_ge(pv_done, (n + 1) * GROUPS)
            at_least(dve, rep_done, n)
            dve.reciprocal(r_den[:], ps_den[:, 0:S]).then_inc(rden_done, 1)

        def normalize(n):
            dve.wait_ge(rrep_done, n + 1)
            at_least(dve, wo_done, n)
            dve.tensor_tensor(att[:], ps_o[:], r_rep[:], ALU.mult).then_inc(att_done, 1)

        def body(n, par, proj, maxi, finish):
            for g in range(GROUPS):
                if maxi:
                    row_max(n + 1, g)
                if g == 0 and finish:
                    normalize(n - 1)
                weigh(n, par, g)
            reciprocal(n)

        for g in range(GROUPS):
            row_max(0, g)
        batches(dve, body)
        normalize(NB - 1)

    @block.scalar
    def _(act):
        act.wait_ge(d_small, 16 * 9)
        act.activation(lam[:], u_all[:], ACT.Exp, scale=-5.0).then_inc(a_step, 1)
        act.wait_ge(g_ready, 1)
        act.activation(decay[:], lam[:], ACT.Exp, scale=-1.0).then_inc(a_step, 1)
        act.wait_ge(setup_done, 1)
        act.wait_ge(zero_done, 4)

        def whole_q(n):
            if not (isinstance(n, int) and n == 0):
                act.wait_ge(qlo_done, n)
            act.wait_ge(proj_q, n + 1)
            for k in range(C):
                for r in range(2):
                    ins = act.activation(q_full[:, k, r], bank0[:, k], ACT.Identity,
                                         bias=bq_s[:, k, r:r + 1], scale=par_mask[:, r:r + 1])
            ins.then_inc(qf_done, 1)

        def high_q(n):
            if not (isinstance(n, int) and n == 0):
                for half in d_stack:
                    act.wait_ge(half, n * 16 * STACK_DMAS)
            act.wait_ge(qf_done, n + 1)
            act.activation(q_hi[:], q_full[:], ACT.Copy).then_inc(qhi_done, 1)

        def whole_k(n):
            act.wait_ge(proj_k, n + 1)
            at_least(act, klo_done, n)
            for k in range(C):
                ins = act.activation(k_full[:, k], bank1[:, k], ACT.Identity, bias=bias[:, 1, k:k + 1])
            ins.then_inc(kf_done, 1)

        def high_k(n):
            if not (isinstance(n, int) and n == 0):
                for half in d_stack:
                    act.wait_ge(half, n * 16 * STACK_DMAS)
            act.wait_ge(kf_done, n + 1)
            act.activation(k_hi[:], k_full[:], ACT.Copy).then_inc(khi_done, 1)

        def projected(n):
            act.wait_ge(wo_done, n + 1)
            at_least(act, x1_done, n)
            for k in range(C):
                ins = act.activation(delta[:, k], bank0[:, k], ACT.Identity, bias=bo_all[:, k:k + 1])
            ins.then_inc(delta_done, 1)

        def values(n, par):
            act.wait_ge(proj_v, n + 1)
            if not (isinstance(n, int) and n < 2):
                act.wait_ge(pv_done, (n - 1) * GROUPS)
            for k in range(C):
                for half in range(2):
                    src = bank0[:, k].rearrange("p (c h j d) -> p c h j d", c=C, h=2, j=4)[:, :, half]
                    dst = v_pad[par][:, k].rearrange("p (c h j) w -> p c h j w", c=C, h=2)[:, :, half, :, 16 * half:16 * half + 16]
                    ins = act.activation(dst, src, ACT.Copy)
            ins.then_inc(v_done, 1)

        def exps(n, g):
            if not (isinstance(n, int) and n == 0 and g < E_BUFS):
                act.wait_ge(pv_done, n * GROUPS + g - E_BUFS + 1)
            for b in range(2):
                act.wait_ge(t_done, 2 * (n * GROUPS + g) + b + 1)
                act.activation(e[g % E_BUFS][:, 2 * b:2 * b + 2], ps_t[b][:], ACT.Exp).then_inc(exp_done, 1)

        def max_rows(n):
            act.wait_ge(mt_done, n + 1)
            if not (isinstance(n, int) and n == 0):
                act.wait_ge(d_max, 16 * n)
            act.activation(max_row[:], bank1[0:HEADS, 0], ACT.Copy).then_inc(mrow_done, 1)

        def spread(n):
            act.wait_ge(rep_done, n + 1)
            at_least(act, att_done, n)
            act.activation(r_rep[:], bank1[:], ACT.Copy).then_inc(rrep_done, 1)

        def body(n, par, proj, maxi, finish):
            for g in range(GROUPS):
                exps(n, g)
                if g == 0 and finish:
                    spread(n - 1)
                if proj:
                    if g == 0:
                        whole_q(n + 2)
                    elif g == 1:
                        whole_k(n + 2)
                    elif g == 2:
                        high_k(n + 2)
                    elif g == 3:
                        high_q(n + 2)
                if g == 4 and finish:
                    projected(n - 1)
            if maxi:
                max_rows(n + 1)
            if proj:
                values(n + 2, par)

        for n in range(2):
            whole_q(n)
            whole_k(n)
            values(n, n)
            high_k(n)
            high_q(n)
        max_rows(0)
        batches(act, body)
        spread(NB - 1)
        projected(NB - 1)

    @block.tensor
    def _(pe):
        pe.wait_ge(g_step, 6 + C * K_SPARSE)
        for qc in range(C):
            for kc in range(C):
                pe.transpose(bank0[:, kc, qc * P:qc * P + P], cnt[:, qc, kc * P:kc * P + P], ident[:])
        for m in range(C):
            for k in range(C):
                ins = pe.matmul(ps_den[:, m:m + 1], wo[:, k, m * P:m * P + P], bias[:, 2, k:k + 1],
                                start=(k == 0), stop=(k == C - 1))
        ins.then_inc(setup_pe, 1)
        pe.wait_ge(setup_done, 1)

        def project_q(n, par):
            pe.wait_ge(d_xs[par], landed(n, par))
            at_least(pe, v_done, n)
            for m in range(C):
                for k in range(C):
                    ins = pe.matmul(bank0[:, m], wq[:, k, m * P:m * P + P], xs[par][:, k], start=(k == 0), stop=(k == C - 1))
            ins.then_inc(proj_q, 1)

        def project_k(n, par):
            if isinstance(n, int) and n == 1:
                pe.wait_ge(kf_done, 1)
            elif isinstance(n, int) and n == 2:
                pe.wait_ge(mrow_done, 1)
            elif not (isinstance(n, int) and n == 0):
                pe.wait_ge(rrep_done, n - 2)
            for m in range(C):
                for k in range(C):
                    ins = pe.matmul(bank1[:, m], wk[:, k, m * P:m * P + P], xs[par][:, k], start=(k == 0), stop=(k == C - 1))
            ins.then_inc(proj_k, 1)

        def project_v(n, par):
            pe.wait_ge(qf_done, n + 1)
            if not (isinstance(n, int) and n < 3):
                pe.wait_ge(delta_done, n - 2)
            for m in range(C):
                for k in range(C):
                    ins = pe.matmul(bank0[:, m], xs[par][:, k, m * P:m * P + P], wv[:, k], start=(k == 0), stop=(k == C - 1))
            ins.then_inc(proj_v, 1)

        def score_rows(n, par, g):
            quad, qc = rows_group(g)
            if g == 0:
                pe.wait_ge(m_ready, n + 1)
            if g % 4 == 0:
                pe.wait_ge(d_stack[g // 4], (n + 1) * 16 * STACK_DMAS)
            for b in range(2):
                if not (isinstance(n, int) and n == 0 and g == 0):
                    pe.wait_ge(red_done, 2 * (n * GROUPS + g) + b - 1)
                pe.matmul(ps_s[b][:], ident_bf[:], add_m[par][:, qc].unsqueeze(1).to_broadcast([P, 2, S]), start=True, stop=False)
                for r in range(2):
                    slot = 4 * quad + 2 * b + r
                    ins = pe.matmul(ps_s[b][:, r], q_st[par][0:96, slot, qc * P:qc * P + P],
                                    k_st[par][0:96, slot // 2], start=False, stop=(r == 1))
                ins.then_inc(s_done, 1)

        def score_cols(n, par, g):
            quad, kc = rows_group(g)
            if g == 0:
                pe.wait_ge(d_max, 16 * (n + 1))
            for b in range(2):
                if not (isinstance(n, int) and n == 0 and g == 0):
                    pe.wait_ge(exp_done, 2 * (n * GROUPS + g) + b - 1)
                pair = 2 * quad + b
                pe.matmul(ps_t[b][:], k_st[par][0:97, pair, kc * P:kc * P + P],
                          q_st[par][0:97, 2 * pair:2 * pair + 2], start=True, stop=True).then_inc(t_done, 1)

        def mix_values(n, par, g):
            quad, kc = rows_group(g)
            pe.wait_ge(p_done, n * GROUPS + g + 1)
            if g == 0:
                pe.wait_ge(v_done, n + 1)
                at_least(pe, att_done, n)
                at_least(pe, rden_done, n)
            for j in range(4):
                ins = pe.matmul(ps_o[32 * j:32 * j + 32, quad // 2], v_pad[par][:, kc, 4 * quad + j], e[g % E_BUFS][:, j],
                          start=(g == 0), stop=(g == GROUPS - 1), tile_position=(0, 32 * j), skip_group_check=True)
            if g % 4 == 2:
                ins.then_inc(stack_free[g // 4], 1)
            for j in range(4):
                ins = pe.matmul(ps_den[32 * j:32 * j + 32, 0:S], sel_den[:, quad], e[g % E_BUFS][:, j],
                                start=(g == 0), stop=(g == GROUPS - 1), tile_position=(0, 32 * j))
            ins.then_inc(pv_done, 1)

        def transpose_max(n):
            pe.wait_ge(red_done, (n + 1) * 2 * GROUPS)
            if isinstance(n, int) and n + 1 >= NB:
                at_least(pe, rrep_done, NB - 2)
                pe.wait_ge(kf_done, NB)
                pe.wait_ge(mrow_done, n)
            else:
                pe.wait_ge(kf_done, n + 2)
            for qc in range(C):
                ins = pe.transpose(bank1[0:HEADS, 0, qc * P:qc * P + P], neg_max[:, qc], ident[:])
            ins.then_inc(mt_done, 1)

        def spread(n):
            pe.wait_ge(rden_done, n + 1)
            if isinstance(n, int) and n == NB - 1:
                pe.wait_ge(rrep_done, n)
            else:
                pe.wait_ge(mrow_done, n + 2)
            for c in range(C):
                ins = pe.matmul(bank1[:, c], sel_rep[:, c], r_den[:], start=True, stop=True)
            ins.then_inc(rep_done, 1)

        def project_out(n):
            pe.wait_ge(att_done, n + 1)
            if isinstance(n, int) and n + 4 > NB:
                pe.wait_ge(v_done, NB)
                at_least(pe, delta_done, n)
            else:
                pe.wait_ge(qf_done, n + 4)
            for m in range(C):
                for k in range(C):
                    ins = pe.matmul(bank0[:, m], wo[:, k, m * P:m * P + P], att[:, k], start=(k == 0), stop=(k == C - 1))
            ins.then_inc(wo_done, 1)

        def body(n, par, proj, maxi, finish):
            for g in range(GROUPS):
                if maxi:
                    score_rows(n + 1, 1 - par, g)
                score_cols(n, par, g)
                if g == 0 and finish:
                    spread(n - 1)
                if g == 0 and proj:
                    project_q(n + 2, par)
                if g > 0:
                    mix_values(n, par, g - 1)
                if g == 1 and proj:
                    project_k(n + 2, par)
                if g == 2 and finish:
                    project_out(n - 1)
            if maxi:
                transpose_max(n + 1)
            if proj:
                project_v(n + 2, par)
            mix_values(n, par, GROUPS - 1)

        for n in range(2):
            project_q(n, n)
            project_k(n, n)
            project_v(n, n)
        for g in range(GROUPS):
            score_rows(0, 0, g)
        transpose_max(0)
        batches(pe, body)
        spread(NB - 1)
        project_out(NB - 1)

TRACES = 32
HID1 = 64
STEP = 8
CHUNKS = S // STEP
LATE = 16
TABLE = CHUNKS + LATE


def trace_layer(nc, sem_ctx, ctx, t, X, NB, consts):
    def sb(name, shape, dt=F32):
        return ctx.enter_context(nc.sbuf_tensor("b_" + name, shape, dt))

    def ps(name, shape, dt=F32):
        return ctx.enter_context(nc.psum_tensor("b_" + name, shape, dt))

    def sem(name):
        return sem_ctx.enter_context(nc.semaphore("b_" + name))

    ident = consts["ident"]
    wg = sb("wg", [P, 2 * C, D])
    wn1 = sb("wn1", [P, C, HID1])
    wn2 = sb("wn2", [HID1 + 1, TRACES])
    wn2_3 = sb("wn2_3", [HID1 + 1, 3 * TRACES])
    wsoma, wtemp, wout = sb("wsoma", [P, C, D]), sb("wtemp", [P, C, D]), sb("wout", [P, C, D])
    bg_h, bsoma, btemp_h, gamma, beta = (sb(n, [P, C]) for n in ("bg", "bsoma", "btemp", "gamma", "beta"))
    bn1 = sb("bn1", [HID1, 1])
    tau_c = sb("tau_c", [P, 1])
    tau_col = sb("tau_col", [P, 1])
    tau_row = sb("tau_row", [P, TRACES])
    sp_c, sp_col, sp_row = sb("sp_c", [P, 1]), sb("sp_col", [P, 1]), sb("sp_row", [P, TRACES])
    alpha_c = sb("alpha_c", [P, 1])
    lag_n = sb("lag_n", [P, TABLE])
    lag_on = sb("lag_on", [P, TABLE])
    ramp = sb("ramp", [P, 32])
    own = sb("own", [P, 32])
    table = sb("table", [P, TABLE, TRACES])
    spread_w = sb("spread_w", [P, 32])
    power = sb("power", [P, STEP])
    blend_t = sb("blend_t", [P, C, TRACES])
    bl_max = sb("bl_max", [P, C])
    bl_sum = sb("bl_sum", [P, C])
    bl_inv = sb("bl_inv", [P, C])
    bl_rep = sb("bl_rep", [P, C, 4, TRACES])
    w_rep = sb("w_rep", [P, D])
    w_lag = sb("w_lag", [P, STEP, D])
    w_st = sb("w_st", [P, STEP, D], F32R)
    mean_w = sb("mean_w", [P, C])
    mean_mat = sb("mean_mat", [P, P])
    eps = sb("eps", [P, 1])

    ctx_e = sb("ctx_e", [P, C, S])
    th_g = sb("th_g", [P, C, S])
    gated = [sb(f"gated{i}", [P, C, S]) for i in range(2)]
    gated_t = [sb(f"gated_t{i}", [P, C, D]) for i in range(2)]
    h1 = sb("h1", [HID1 + 1, S])
    th_m = sb("th_m", [3 * TRACES, S])
    mod_f = sb("mod_f", [3 * TRACES, S])
    mod_st = [sb(f"mod_st{i}", [3 * TRACES, S], F32R) for i in range(2)]
    th_t = sb("th_t", [P, C, TRACES])
    mod_t = sb("mod_t", [P, C, TRACES])
    decayed = [sb(f"decayed{i}", [P, TABLE, TRACES]) for i in range(2)]
    state = [sb(f"state{i}", [P, 2, D]) for i in range(2)]
    inner = sb("inner", [P, C, S])
    prod = [sb(f"prod{i}", [P, C, S]) for i in range(2)]
    outer_t = sb("outer_t", [P, C, D])
    temporal = sb("temporal", [P, C, S])
    th_o = sb("th_o", [P, C, S])
    soma = sb("soma", [P, C, S])
    mixed = sb("mixed", [P, C, S])
    square = sb("square", [P, C, S])
    std = sb("std", [P, S])
    rstd = sb("rstd", [P, S])
    normed = sb("normed", [P, C, S])
    scaled = sb("scaled", [P, C, S])

    pA = ps("pA", [P, C, S])
    pB = ps("pB", [P, 2, S])
    pS = [ps(f"pS{i}", [P, 2, D]) for i in range(2)]
    pL = [ps(f"pL{i}", [P, C, S]) for i in range(2)]
    pY = ps("pY", [P, C, S])
    pZ = ps("pZ", [P, C, S])

    d_in, v_step, a_set, a_bl, pe_set, set_done = (sem(n) for n in ("d_in", "v_step", "a_set", "a_bl", "pe_set", "set_done"))
    ctx_done, wg_done, thg_done, gated_done = (sem(n) for n in ("ctx", "wg", "thg", "gated"))
    h1_done, gelu1_done, mod_done, thm_done, modst_done, vmod = (sem(n) for n in ("h1", "gelu1", "mod", "thm", "modst", "vmod"))
    modt_done, tht_done, modt_ready, dec_done = (sem(n) for n in ("modt", "tht", "modt_ready", "dec"))
    gt_done, gtev_done = sem("gt"), sem("gtev")
    st_done, sw_done, yin_done, yev_done, ytr_done = (sem(n) for n in ("st", "sw", "yin", "yev", "ytr"))
    lag_done, prod_done, inner_done, temp_done = (sem(n) for n in ("lag", "prod", "inner", "temp"))
    soma_mm, soma_done, gate_mm, tho_done, mixed_done = (sem(n) for n in ("soma_mm", "soma", "gate_mm", "tho", "mixed"))
    out_mm, sq_done, var_mm, std_done, rstd_done, normed_done, scaled_done, x2_done = (
        sem(n) for n in ("out_mm", "sq", "var_mm", "std", "rstd", "normed", "scaled", "x2"))

    LOADS = ("wg", "wn1", "wn2", "wn2_3", "wsoma", "wtemp", "wout", "bg", "bn1", "bsoma", "btemp", "gamma", "beta",
             "tau_c", "tau_col", "tau_row", "lag_n", "lag_on", "ramp", "own", "blend_t")
    tiles = dict(zip(LOADS, (wg, wn1, wn2, wn2_3, wsoma, wtemp, wout, bg_h, bn1, bsoma, btemp_h, gamma, beta,
                             tau_c, tau_col, tau_row, lag_n, lag_on, ramp, own, blend_t)))

    def xn(n, k=None):
        at = slice(n * S, n * S + S) if isinstance(n, int) else bass.ds(n * S, S)
        return X[:, :, at] if k is None else X[:, k, at]

    def rows(w):
        return w[:].rearrange("p c s -> p (c s)")

    block = ctx.enter_context(nc.Block())

    def loop(eng, body):
        body(0, 0, True, False)
        if NB > 2:
            with pairs(eng, 1, NB - 1) as n:
                body(n, 1, True, True)
                body(n + 1, 0, True, True)
        body(NB - 1, 1, False, True)

    @block.sync
    def _(sp):
        for name in LOADS:
            src = t[name]
            if name in ("wg", "wn1", "wsoma", "wtemp", "wout", "blend_t"):
                src = src.rearrange("(k p) e -> p k e", p=P)
            if name in ("tau_c", "tau_row"):
                src = src.partition_broadcast(P)
            sp.dma_start(tiles[name][:], src).then_inc(d_in, 16)

    @block.gpsimd
    def _(pool):
        pool.memset(h1[HID1:HID1 + 1], 1.0).then_inc(set_done, 1)
        pool.wait_ge(set_done, 2)

        def decays(n, par):
            pool.wait_ge(modt_ready, n + 1)
            if not (isinstance(n, int) and n < 2):
                pool.wait_ge(st_done, (n - 1) * 4)
            for k, lo, cnt in ((0, 0, CHUNKS), (1, CHUNKS, LATE)):
                ins = pool.tensor_tensor(decayed[par][:, lo:lo + cnt], table[:, lo:lo + cnt],
                                         mod_t[:, k].unsqueeze(1).to_broadcast([P, cnt, TRACES]), ALU.mult)
            ins.then_inc(dec_done, 1)

        def residual(n):
            pool.wait_ge(scaled_done, n + 1)
            pool.tensor_tensor(xn(n), scaled[:], xn(n), ALU.add).then_inc(x2_done, 1)

        def body(n, par, has_a, has_c):
            if has_a:
                decays(n + 1, 1 - par)
            if has_c:
                residual(n - 1)

        decays(0, 0)
        loop(pool, body)
        residual(NB - 1)
        pool.wait_ge(x2_done, NB)

    @block.vector
    def _(dve):
        done = [0]

        def link(ins):
            done[0] += 1
            ins.then_inc(v_step, 1)
            dve.wait_ge(v_step, done[0])

        dve.wait_ge(d_in, 16 * len(LOADS))
        link(dve.memset(eps[:], 1e-5))
        link(dve.memset(mean_mat[:], 1.0 / D))
        for tau in (tau_c, tau_col, tau_row):
            link(dve.tensor_scalar(tau[:], tau[:], 80.0, None, ALU.min))
        link(dve.tensor_reduce(bl_max[:], blend_t[:], AX.X, ALU.max, negate=True))
        dve.wait_ge(a_set, 1)
        for sp_, tau in ((sp_c, tau_c), (sp_col, tau_col), (sp_row, tau_row)):
            link(dve.tensor_scalar(sp_[:], tau[:], 1.0, None, ALU.add))
        dve.wait_ge(a_set, 2)
        for sp_ in (sp_c, sp_col, sp_row):
            link(dve.tensor_scalar(sp_[:], sp_[:], -1.0, None, ALU.mult))
        link(dve.tensor_tensor(table[:], lag_n[:].unsqueeze(2).to_broadcast([P, TABLE, TRACES]),
                               sp_row[:].unsqueeze(1).to_broadcast([P, TABLE, TRACES]), ALU.mult))
        link(dve.tensor_scalar(spread_w[:], ramp[:], sp_col[:], None, ALU.mult))
        link(dve.tensor_scalar(power[:], ramp[:, 0:STEP], -1.0, sp_col[:], ALU.add, ALU.mult))
        dve.wait_ge(a_bl, C)
        link(dve.tensor_reduce(bl_sum[:], blend_t[:], AX.X, ALU.add))
        link(dve.reciprocal(bl_inv[:], bl_sum[:]))
        for k in range(C):
            link(dve.tensor_scalar(blend_t[:, k], blend_t[:, k], bl_inv[:, k:k + 1], 0.5, ALU.mult, ALU.mult))
        link(dve.tensor_copy(bl_rep[:], blend_t[:].unsqueeze(2).to_broadcast([P, C, 4, TRACES])))
        link(dve.tensor_reduce(mean_w[:], wout[:], AX.X, ALU.add))
        link(dve.tensor_scalar(mean_w[:], mean_w[:], -1.0 / D, None, ALU.mult))
        for k in range(C):
            link(dve.tensor_scalar(wout[:, k], wout[:, k], mean_w[:, k:k + 1], 0.5, ALU.add, ALU.mult))
        link(dve.tensor_scalar(bg_h[:], bg_h[:], 0.5, None, ALU.mult))
        link(dve.tensor_scalar(btemp_h[:], btemp_h[:], 0.5, None, ALU.mult))
        dve.wait_ge(a_set, 3)
        link(dve.tensor_tensor(table[:], table[:], lag_on[:].unsqueeze(2).to_broadcast([P, TABLE, TRACES]), ALU.mult))
        link(dve.tensor_tensor(spread_w[:], spread_w[:], own[:], ALU.mult))
        dve.wait_ge(pe_set, 1)
        link(dve.tensor_copy(w_rep[:], pA[:, 0]))
        for lag in range(STEP):
            link(dve.tensor_scalar(w_lag[:, lag], w_rep[:], power[:, lag:lag + 1], None, ALU.mult))
        link(dve.tensor_copy(w_st[:], w_lag[:]))
        low = slice(2 * TRACES, 3 * TRACES)
        link(dve.tensor_tensor(w_st[low], w_lag[low], w_st[low].bitcast(F32), ALU.subtract))
        dve.sem_inc(set_done, 1)

        def context(n):
            at_least(dve, wg_done, C * n)
            for k in range(C):
                ins = dve.tensor_tensor_scan(ctx_e[:, k], alpha_c[:].to_broadcast([P, S]), xn(n, k), 0.0, ALU.mult, ALU.add)
            ins.then_inc(ctx_done, 1)

        def gating(n, par):
            dve.wait_ge(thg_done, n + 1)
            if not (isinstance(n, int) and n < 2):
                dve.wait_ge(inner_done, (STEP - 1) * (n - 1))
                dve.wait_ge(gt_done, n - 1)
            dve.scalar_tensor_tensor(out=gated[par][:], in0=th_g[:], scalar=1.0, in1=xn(n), op0=ALU.add, op1=ALU.mult)\
               .then_inc(gated_done, 1)

        def modulation(n, par):
            dve.wait_ge(thm_done, n + 1)
            if not (isinstance(n, int) and n < 2):
                dve.wait_ge(lag_done, (n - 1) * STEP)
            dve.tensor_scalar(mod_st[par][:], th_m[:], 0.5, 1.0, ALU.mult, ALU.add).then_inc(vmod, 1)
            low = slice(TRACES, 2 * TRACES)
            dve.tensor_scalar(mod_f[low], th_m[low], 0.5, 1.0, ALU.mult, ALU.add).then_inc(vmod, 1)
            dve.wait_ge(vmod, 2 * n + 2)
            dve.tensor_tensor(mod_st[par][low], mod_f[low], mod_st[par][low].bitcast(F32), ALU.subtract).then_inc(modst_done, 1)

        def states(n, q):
            dve.wait_ge(st_done, 4 * n + q + 1)
            if not (isinstance(n, int) and n == 0 and q < 2):
                dve.wait_ge(yin_done, 4 * n + q - 1)
            dve.tensor_tensor(state[q % 2][:], pS[q % 2][:], w_rep[:].unsqueeze(1).to_broadcast([P, 2, D]), ALU.mult)\
               .then_inc(sw_done, 1)

        def lag_sum(n, par, lag):
            dve.wait_ge(lag_done, STEP * n + lag + 1)
            m = rows(pL[lag % 2]).rearrange("p (a j) -> p a j", j=STEP)
            g = rows(gated[par]).rearrange("p (a j) -> p a j", j=STEP)
            if lag == 0:
                at_least(dve, temp_done, n)
                dve.tensor_tensor(rows(inner), rows(gated[par]), rows(pL[0]), ALU.mult).then_inc(prod_done, 1)
                return
            pr = rows(prod[lag % 2]).rearrange("p (a j) -> p a j", j=STEP)[:, :, 0:STEP - lag]
            dve.tensor_tensor(pr, g[:, :, 0:STEP - lag], m[:, :, 0:STEP - lag], ALU.mult).then_inc(prod_done, 1)
            dve.wait_ge(prod_done, STEP * n + lag + 1)
            if lag > 1:
                dve.wait_ge(inner_done, (STEP - 1) * n + lag - 1)
            y = rows(inner).rearrange("p (a j) -> p a j", j=STEP)[:, :, lag:STEP]
            dve.tensor_tensor(y, y, pr, ALU.add).then_inc(inner_done, 1)

        def total(n):
            dve.wait_ge(ytr_done, n + 1)
            dve.wait_ge(inner_done, (STEP - 1) * (n + 1))
            at_least(dve, gate_mm, n)
            dve.tensor_tensor(temporal[:], inner[:], pY[:], ALU.add).then_inc(temp_done, 1)

        def mixing(n):
            dve.wait_ge(tho_done, n + 1)
            dve.wait_ge(soma_done, n + 1)
            at_least(dve, out_mm, n)
            dve.scalar_tensor_tensor(out=mixed[:], in0=th_o[:], scalar=1.0, in1=soma[:], op0=ALU.add, op1=ALU.mult)\
               .then_inc(mixed_done, 1)

        def norm(n):
            dve.wait_ge(std_done, n + 1)
            at_least(dve, normed_done, n)
            dve.reciprocal(rstd[:], std[:]).then_inc(rstd_done, 1)
            dve.wait_ge(rstd_done, n + 1)
            at_least(dve, scaled_done, n)
            dve.tensor_tensor(normed[:], pZ[:], rstd[:].unsqueeze(1).to_broadcast([P, C, S]), ALU.mult).then_inc(normed_done, 1)

        def body(n, par, has_a, has_c):
            if has_c:
                mixing(n - 1)
            states(n, 0)
            lag_sum(n, par, 0)
            lag_sum(n, par, 1)
            if has_a:
                context(n + 1)
            states(n, 1)
            lag_sum(n, par, 2)
            if has_a:
                modulation(n + 1, 1 - par)
            if has_c:
                norm(n - 1)
            lag_sum(n, par, 3)
            states(n, 2)
            lag_sum(n, par, 4)
            lag_sum(n, par, 5)
            if has_a:
                gating(n + 1, 1 - par)
            states(n, 3)
            lag_sum(n, par, 6)
            lag_sum(n, par, 7)
            total(n)

        context(0)
        gating(0, 0)
        modulation(0, 0)
        loop(dve, body)
        mixing(NB - 1)
        norm(NB - 1)

    @block.scalar
    def _(act):
        act.wait_ge(v_step, 6)
        for tau in (tau_c, tau_col):
            act.activation(tau[:], tau[:], ACT.Exp)
        act.activation(tau_row[:], tau_row[:], ACT.Exp).then_inc(a_set, 1)
        act.wait_ge(v_step, 9)
        for sp_ in (sp_c, sp_col):
            act.activation(sp_[:], sp_[:], ACT.Ln)
        act.activation(sp_row[:], sp_row[:], ACT.Ln).then_inc(a_set, 1)
        for k in range(C):
            act.activation(blend_t[:, k], blend_t[:, k], ACT.Exp, bias=bl_max[:, k:k + 1]).then_inc(a_bl, 1)
        act.wait_ge(v_step, 15)
        act.activation(alpha_c[:], sp_c[:], ACT.Exp)
        act.activation(table[:], table[:], ACT.Exp)
        act.activation(spread_w[:], spread_w[:], ACT.Exp)
        act.activation(power[:], power[:], ACT.Exp).then_inc(a_set, 1)
        act.wait_ge(set_done, 2)

        def input_gate(n):
            act.wait_ge(wg_done, C * (n + 1))
            at_least(act, gated_done, n)
            for m in range(C):
                ins = act.activation(th_g[:, m], pA[:, m], ACT.Tanh, bias=bg_h[:, m:m + 1], scale=0.5)
            ins.then_inc(thg_done, 1)

        def hidden(n):
            act.wait_ge(h1_done, n + 1)
            at_least(act, modt_done, n)
            act.activation(h1[0:HID1], pB[0:HID1, 0], ACT.Gelu, bias=bn1[:]).then_inc(gelu1_done, 1)

        def mod_rows(n):
            act.wait_ge(mod_done, n + 1)
            at_least(act, modst_done, n)
            act.activation(th_m[:], pB[0:3 * TRACES, 1], ACT.Tanh, scale=0.5).then_inc(thm_done, 1)

        def mod_cols(n):
            act.wait_ge(modt_done, n + 1)
            act.activation(th_t[:], pB[:, 0, 0:C * TRACES].rearrange("p (c d) -> p c d", c=C), ACT.Tanh, scale=0.5)\
               .then_inc(tht_done, 1)
            act.wait_ge(tht_done, n + 1)
            at_least(act, dec_done, n)
            act.activation(mod_t[:], th_t[:], ACT.Copy, scale=0.5, bias=1.0).then_inc(modt_ready, 1)

        def turned(n, par):
            act.wait_ge(gt_done, n + 1)
            if not (isinstance(n, int) and n < 2):
                act.wait_ge(st_done, (n - 1) * 4)
            act.activation(gated_t[par][:], pA[:], ACT.Copy).then_inc(gtev_done, 1)

        def spread_out(n):
            act.wait_ge(yin_done, 4 * (n + 1))
            at_least(act, ytr_done, n)
            act.activation(outer_t[:], pY[:], ACT.Copy).then_inc(yev_done, 1)

        def somas(n):
            act.wait_ge(soma_mm, n + 1)
            at_least(act, mixed_done, n)
            for m in range(C):
                ins = act.activation(soma[:, m], pZ[:, m], ACT.Gelu, bias=bsoma[:, m:m + 1])
            ins.then_inc(soma_done, 1)

        def output_gate(n):
            act.wait_ge(gate_mm, n + 1)
            at_least(act, mixed_done, n)
            for m in range(C):
                ins = act.activation(th_o[:, m], pY[:, m], ACT.Tanh, bias=btemp_h[:, m:m + 1], scale=0.5)
            ins.then_inc(tho_done, 1)

        def squares(n):
            act.wait_ge(out_mm, n + 1)
            at_least(act, var_mm, n)
            act.activation(square[:], pZ[:], ACT.Square).then_inc(sq_done, 1)

        def deviation(n):
            act.wait_ge(var_mm, n + 1)
            at_least(act, rstd_done, n)
            act.activation(std[:], pY[:, 0], ACT.Sqrt, bias=eps[:]).then_inc(std_done, 1)

        def scaling(n):
            act.wait_ge(normed_done, n + 1)
            at_least(act, x2_done, n)
            for m in range(C):
                ins = act.activation(scaled[:, m], normed[:, m], ACT.Identity, bias=beta[:, m:m + 1], scale=gamma[:, m:m + 1])
            ins.then_inc(scaled_done, 1)

        def body(n, par, has_a, has_c):
            if has_c:
                output_gate(n - 1)
            if has_a:
                hidden(n + 1)
            if has_c:
                squares(n - 1)
            if has_a:
                mod_rows(n + 1)
                mod_cols(n + 1)
            if has_c:
                deviation(n - 1)
            if has_a:
                input_gate(n + 1)
            if has_c:
                scaling(n - 1)
            spread_out(n)
            somas(n)
            if has_a:
                turned(n + 1, 1 - par)

        hidden(0)
        input_gate(0)
        mod_rows(0)
        mod_cols(0)
        turned(0, 0)
        loop(act, body)
        output_gate(NB - 1)
        squares(NB - 1)
        deviation(NB - 1)
        scaling(NB - 1)

    @block.tensor
    def _(pe):
        pe.wait_ge(v_step, 20)
        for k in range(C):
            ins = pe.transpose(pA[:, 0, k * P:k * P + P], bl_rep[:, k].rearrange("p r d -> p (r d)"), ident[:])
        ins.then_inc(pe_set, 1)
        pe.wait_ge(set_done, 2)

        def gate_in(n, m):
            if m == 0:
                pe.wait_ge(ctx_done, n + 1)
                at_least(pe, gtev_done, n)
            for k in range(2 * C):
                rhs = xn(n, k) if k < C else ctx_e[:, k - C]
                ins = pe.matmul(pA[:, m], wg[:, k, m * P:m * P + P], rhs, start=(k == 0), stop=(k == 2 * C - 1))
            ins.then_inc(wg_done, 1)

        def hidden(n):
            for k in range(C):
                ins = pe.matmul(pB[0:HID1, 0], wn1[:, k], xn(n, k), start=(k == 0), stop=(k == C - 1))
            ins.then_inc(h1_done, 1)

        def modulate(n):
            pe.wait_ge(gelu1_done, n + 1)
            pe.matmul(pB[0:3 * TRACES, 1], wn2_3[:], h1[:], start=True, stop=True).then_inc(mod_done, 1)
            pe.wait_ge(thm_done, n + 1)
            for k in range(C):
                ins = pe.matmul(pB[:, 0, k * TRACES:k * TRACES + TRACES], h1[:, k * P:k * P + P], wn2[:], start=True, stop=True)
            ins.then_inc(modt_done, 1)

        def turn(n, par):
            pe.wait_ge(tht_done, n + 1)
            pe.wait_ge(thg_done, n + 1)
            pe.wait_ge(gated_done, n + 1)
            for k in range(C):
                for c in range(C):
                    ins = pe.transpose(pA[:, k, c * P:c * P + P], gated[par][:, c, k * P:k * P + P], ident[:])
            ins.then_inc(gt_done, 1)

        def states(n, par, q):
            if q == 0:
                pe.wait_ge(dec_done, n + 1)
                pe.wait_ge(gtev_done, n + 1)
            if not (isinstance(n, int) and n == 0 and q < 2):
                pe.wait_ge(sw_done, 4 * n + q - 1)
            for i in range(2):
                g = 2 * q + i
                late = g >= 4
                columns = (4 * g, CHUNKS + 4 * g - LATE) if late else (4 * g,)
                for k, lo in enumerate(columns):
                    ins = pe.matmul(pS[q % 2][:, i], decayed[par][:, lo:lo + 4].rearrange("p a d -> p (a d)"),
                                    gated_t[par][:, k], start=(k == 0), stop=(k == len(columns) - 1))
            ins.then_inc(st_done, 1)

        def spread(n, q):
            pe.wait_ge(sw_done, 4 * n + q + 1)
            if q == 0:
                at_least(pe, std_done, n)
            for i in range(2):
                j = (2 * q + i) % 4
                ins = pe.matmul(pY[32 * j:32 * j + 32, q // 2], spread_w[:], state[q % 2][:, i],
                                start=True, stop=True, tile_position=(0, 32 * j))
            ins.then_inc(yin_done, 1)

        def turn_back(n):
            pe.wait_ge(yev_done, n + 1)
            for k in range(C):
                for c in range(C):
                    ins = pe.transpose(pY[:, c, k * P:k * P + P], outer_t[:, k, c * P:c * P + P], ident[:])
            ins.then_inc(ytr_done, 1)

        def lags(n, par, lag):
            if lag == 0:
                pe.wait_ge(modst_done, n + 1)
            if not (isinstance(n, int) and n == 0 and lag < 2):
                pe.wait_ge(prod_done, STEP * n + lag - 1)
            for c in range(C):
                ins = pe.matmul(pL[lag % 2][:, c], w_st[0:3 * TRACES, lag, c * P:c * P + P], mod_st[par][:],
                                start=True, stop=True)
            ins.then_inc(lag_done, 1)

        def soma_in(n):
            at_least(pe, normed_done, n)
            for m in range(C):
                for k in range(C):
                    ins = pe.matmul(pZ[:, m], wsoma[:, k, m * P:m * P + P], xn(n, k), start=(k == 0), stop=(k == C - 1))
            ins.then_inc(soma_mm, 1)

        def gate_out(n):
            pe.wait_ge(temp_done, n + 1)
            for m in range(C):
                for k in range(C):
                    ins = pe.matmul(pY[:, m], wtemp[:, k, m * P:m * P + P], temporal[:, k], start=(k == 0), stop=(k == C - 1))
            ins.then_inc(gate_mm, 1)

        def output(n):
            pe.wait_ge(mixed_done, n + 1)
            for m in range(C):
                for k in range(C):
                    ins = pe.matmul(pZ[:, m], wout[:, k, m * P:m * P + P], mixed[:, k], start=(k == 0), stop=(k == C - 1))
            ins.then_inc(out_mm, 1)

        def mean_square(n):
            pe.wait_ge(sq_done, n + 1)
            pe.wait_ge(tho_done, n + 1)
            for k in range(C):
                ins = pe.matmul(pY[:, 0], mean_mat[:], square[:, k], start=(k == 0), stop=(k == C - 1))
            ins.then_inc(var_mm, 1)

        def body(n, par, has_a, has_c):
            if has_a:
                hidden(n + 1)
            states(n, par, 0)
            lags(n, par, 0)
            lags(n, par, 1)
            if has_c:
                output(n - 1)
            states(n, par, 1)
            if has_a:
                modulate(n + 1)
            if has_c:
                mean_square(n - 1)
            lags(n, par, 2)
            if has_a:
                gate_in(n + 1, 0)
            spread(n, 0)
            lags(n, par, 3)
            states(n, par, 2)
            spread(n, 1)
            lags(n, par, 4)
            if has_a:
                gate_in(n + 1, 1)
            lags(n, par, 5)
            states(n, par, 3)
            spread(n, 2)
            lags(n, par, 6)
            spread(n, 3)
            lags(n, par, 7)
            soma_in(n)
            turn_back(n)
            if has_a:
                turn(n + 1, 1 - par)
            gate_out(n)

        hidden(0)
        gate_in(0, 0)
        gate_in(0, 1)
        modulate(0)
        turn(0, 0)
        loop(pe, body)
        output(NB - 1)
        mean_square(NB - 1)

HIDDEN = 1024
HC = HIDDEN // P
ROUNDS = HC // 2
SHARED = 192
EXPERTS = 8
STAGES = 6


def expert_and_final(nc, sem_ctx, ctx, t, X, NB, consts):
    def sb(name, shape, dt=F32):
        return ctx.enter_context(nc.sbuf_tensor("c_" + name, shape, dt))

    def ps(name, shape, dt=F32):
        return ctx.enter_context(nc.psum_tensor("c_" + name, shape, dt))

    def sem(name):
        return sem_ctx.enter_context(nc.semaphore("c_" + name))

    ident = consts["ident"]
    w1 = sb("w1", [P, C, HIDDEN])
    b1 = sb("b1", [P, HC])
    w2a = sb("w2a", [P, HC, P])
    w2b = [sb(f"w2b{i}", [P, HC, P]) for i in range(2)]
    b2 = [sb(f"b2{i}", [P, C]) for i in range(2)]
    expert_i = sb("expert_i", [1, NB], I32)
    stage_i = sb("stage_i", [1, NB], I32)
    embed_all = sb("embed_all", [P, STAGES, S])
    embed = [sb(f"embed{i}", [P, S]) for i in range(2)]
    key_t = [sb(f"key_t{i}", [P, C, S]) for i in range(2)]
    value = [sb(f"value{i}", [P, C, D]) for i in range(2)]
    hid = [sb(f"hid{i}", [P, 2, S]) for i in range(2)]
    query = sb("query", [P, C, S])
    neg_max = sb("neg_max", [P, C])
    row_sum = sb("row_sum", [P, C])
    row_inv = sb("row_inv", [P, C])
    prob = sb("prob", [P, C, S])
    prob_t = sb("prob_t", [P, C, S])
    y = [sb(f"y{i}", [P, C, S]) for i in range(2)]

    pH = [ps(f"pH{i}", [P, 2, S]) for i in range(2)]
    pO, pS, pT, pV = (ps(n, [P, C, S]) for n in ("pO", "pS", "pT", "pV"))

    d_in = sem("d_in")
    d_exp, d_bias, d_emb, d_key, d_val, stored = ([sem(f"{n}{i}") for i in range(2)]
                                                  for n in ("d_exp", "d_bias", "d_emb", "d_key", "d_val", "stored"))
    hid_mm, hid_done, out_mm, x3_done = (sem(n) for n in ("hid_mm", "hid", "out_mm", "x3"))
    query_done, s_mm, max_done, exp_done, inv_done, prob_done = (sem(n) for n in ("query", "s_mm", "max", "exp", "inv", "prob"))
    t_mm, pt_done, v_mm, y_done = (sem(n) for n in ("t_mm", "pt", "v_mm", "y"))

    def xn(n, k):
        at = slice(n * S, n * S + S) if isinstance(n, int) else bass.ds(n * S, S)
        return X[:, k, at]

    def batch_of(src, n):
        if isinstance(n, int):
            return src[n]
        return src[bass.ds(n, 1)]

    LOADS = 12
    block = ctx.enter_context(nc.Block())

    def loop(eng, body):
        body(0, 0, False, NB == 1)
        if NB > 2:
            with pairs(eng, 1, NB - 1) as n:
                body(n, 1, True, False)
                body(n + 1, 0, True, False)
        body(NB - 1, 1, True, True)

    @block.sync
    def _(sp):
        sp.dma_start(expert_i[:], t["expert"]).then_inc(d_in, 16)
        sp.dma_start(stage_i[:], t["stage"]).then_inc(d_in, 16)
        sp.dma_start(w1[:], t["w1"].rearrange("(k p) e -> p k e", p=P)).then_inc(d_in, 16)
        sp.dma_start(b1[:], t["b1"]).then_inc(d_in, 16)
        w2 = t["w2"].rearrange("(k p) e -> p k e", p=P)
        sp.dma_start(w2a[:], w2[:, :, 0:P]).then_inc(d_in, 16)
        for i in range(2):
            sp.dma_start(w2b[i][:, :, 0:SHARED - P], w2[:, :, P:SHARED]).then_inc(d_in, 16)
            sp.dma_start(b2[i][:, 0:1], t["b2"][0:P]).then_inc(d_in, 16)
            sp.dma_start(b2[i][0:SHARED - P, 1:2], t["b2"][P:SHARED]).then_inc(d_in, 16)
        sp.dma_start(embed_all[:], t["embed"].partition_broadcast(P)).then_inc(d_in, 16)
        sp.wait_ge(d_in, 16 * LOADS)

        def load(n, par):
            at = slice(n, n + 1) if isinstance(n, int) else bass.ds(n, 1)
            expert = sp.value_load(expert_i[0:1, at], min_val=0, max_val=EXPERTS - 1)
            stage = sp.value_load(stage_i[0:1, at], min_val=0, max_val=STAGES - 1)
            if not (isinstance(n, int) and n < 2):
                sp.wait_ge(out_mm, (n - 1) * ROUNDS)
            sp.dma_start(w2b[par][:, :, SHARED - P:P], t["we"][bass.ds(expert, 1)].rearrange("o p k e -> p (o k) e")).then_inc(d_exp[par], 16)
            if not (isinstance(n, int) and n < 2):
                sp.wait_ge(x3_done, n - 1)
            sp.dma_start(b2[par][SHARED - P:P, 1:2], t["be"][bass.ds(expert, 1)].rearrange("o p f -> p (o f)")).then_inc(d_bias[par], 16)
            if not (isinstance(n, int) and n < 2):
                sp.wait_ge(query_done, n - 1)
            sp.dma_start(embed[par][:], embed_all[:, bass.ds(stage, 1)].rearrange("p o f -> p (o f)")).then_inc(d_emb[par], 16)
            if not (isinstance(n, int) and n < 2):
                sp.wait_ge(s_mm, n - 1)
            src = batch_of(t["keyT"], n)
            sp.dma_start(key_t[par][:], src.rearrange("(k p) s -> p k s", p=P) if isinstance(n, int)
                         else src.rearrange("o (k p) s -> p (o k) s", p=P)).then_inc(d_key[par], 16)
            if not (isinstance(n, int) and n < 2):
                sp.wait_ge(v_mm, n - 1)
            src = batch_of(t["key"], n)
            sp.dma_start(value[par][:], src.rearrange("(k p) s -> p k s", p=P) if isinstance(n, int)
                         else src.rearrange("o (k p) s -> p (o k) s", p=P)).then_inc(d_val[par], 16)

        def body(n, par, has_3, last):
            if not last:
                load(n + 1, 1 - par)

        load(0, 0)
        loop(sp, body)

    @block.gpsimd
    def _(pool):
        def store(n, par):
            pool.wait_ge(y_done, n + 1)
            dst = batch_of(t["out"], n)
            pool.dma_start(dst.rearrange("(k p) s -> p k s", p=P) if isinstance(n, int)
                           else dst.rearrange("o (k p) s -> p (o k) s", p=P), y[par][:]).then_inc(stored[par], 16)

        def body(n, par, has_3, last):
            if has_3:
                store(n - 1, 1 - par)

        loop(pool, body)
        store(NB - 1, 1)
        for par in range(2):
            pool.wait_ge(stored[par], landed(NB - 2 + par, par))

    @block.vector
    def _(dve):
        def residual(n, par):
            dve.wait_ge(out_mm, ROUNDS * (n + 1))
            dve.wait_ge(d_bias[par], landed(n, par))
            for k in range(C):
                ins = dve.scalar_tensor_tensor(out=xn(n, k), in0=pO[:, k], scalar=b2[par][:, k:k + 1], in1=xn(n, k),
                                               op0=ALU.add, op1=ALU.add)
            ins.then_inc(x3_done, 1)

        def queries(n, par):
            dve.wait_ge(x3_done, n + 1)
            dve.wait_ge(d_emb[par], landed(n, par))
            at_least(dve, s_mm, n)
            at = slice(n * S, n * S + S) if isinstance(n, int) else bass.ds(n * S, S)
            dve.tensor_tensor(query[:], X[:, :, at], embed[par][:].unsqueeze(1).to_broadcast([P, C, S]), ALU.add)\
               .then_inc(query_done, 1)

        def maxima(n):
            dve.wait_ge(s_mm, n + 1)
            dve.tensor_reduce(neg_max[:], pS[:], AX.X, ALU.max, negate=True).then_inc(max_done, 1)

        def normalize(n):
            dve.wait_ge(exp_done, n + 1)
            at_least(dve, prob_done, C * n)
            dve.reciprocal(row_inv[:], row_sum[:]).then_inc(inv_done, 1)
            dve.wait_ge(inv_done, n + 1)
            for k in range(C):
                dve.tensor_scalar(prob[:, k], prob[:, k], row_inv[:, k:k + 1], None, ALU.mult).then_inc(prob_done, 1)

        def final(n, par):
            dve.wait_ge(v_mm, n + 1)
            if not (isinstance(n, int) and n < 2):
                dve.wait_ge(stored[par], landed(n - 2, par))
            at = slice(n * S, n * S + S) if isinstance(n, int) else bass.ds(n * S, S)
            dve.tensor_tensor(y[par][:], pV[:], X[:, :, at], ALU.add).then_inc(y_done, 1)

        def body(n, par, has_3, last):
            if has_3:
                maxima(n - 1)
                normalize(n - 1)
                final(n - 1, 1 - par)
            residual(n, par)
            queries(n, par)

        loop(dve, body)
        maxima(NB - 1)
        normalize(NB - 1)
        final(NB - 1, 1)

    @block.scalar
    def _(act):
        act.wait_ge(d_in, 16 * LOADS)

        def hidden(n, r):
            act.wait_ge(hid_mm, ROUNDS * n + r + 1)
            if not (isinstance(n, int) and n == 0 and r < 2):
                act.wait_ge(out_mm, ROUNDS * n + r - 1)
            for i in range(2):
                ins = act.activation(hid[r % 2][:, i], pH[r % 2][:, i], ACT.Gelu, bias=b1[:, 2 * r + i:2 * r + i + 1])
            ins.then_inc(hid_done, 1)

        def exps(n):
            act.wait_ge(max_done, n + 1)
            at_least(act, t_mm, n)
            at_least(act, inv_done, n)
            for k in range(C):
                ins = act.activation(prob[:, k], pS[:, k], ACT.Exp, bias=neg_max[:, k:k + 1], accum_out=row_sum[:, k:k + 1])
            ins.then_inc(exp_done, 1)

        def turned(n):
            act.wait_ge(t_mm, n + 1)
            at_least(act, v_mm, n)
            act.activation(prob_t[:], pT[:], ACT.Copy).then_inc(pt_done, 1)

        def body(n, par, has_3, last):
            hidden(n, 0)
            hidden(n, 1)
            if has_3:
                exps(n - 1)
            hidden(n, 2)
            hidden(n, 3)
            if has_3:
                turned(n - 1)

        loop(act, body)
        exps(NB - 1)
        turned(NB - 1)

    @block.tensor
    def _(pe):
        pe.wait_ge(d_in, 16 * LOADS)

        def hidden(n, r):
            if not (isinstance(n, int) and n == 0 and r < 2):
                pe.wait_ge(hid_done, ROUNDS * n + r - 1)
            for i in range(2):
                m = 2 * r + i
                for k in range(C):
                    ins = pe.matmul(pH[r % 2][:, i], w1[:, k, m * P:m * P + P], xn(n, k), start=(k == 0), stop=(k == C - 1))
            ins.then_inc(hid_mm, 1)

        def output(n, par, r):
            pe.wait_ge(hid_done, ROUNDS * n + r + 1)
            if r == 0:
                pe.wait_ge(d_exp[par], landed(n, par))
                at_least(pe, x3_done, n)
            for i in range(2):
                m = 2 * r + i
                for half, w in enumerate((w2a, w2b[par])):
                    ins = pe.matmul(pO[:, half], w[:, m], hid[r % 2][:, i], start=(m == 0 and half == 0),
                                    stop=(m == HC - 1 and half == 1), skip_group_check=True)
            ins.then_inc(out_mm, 1)

        def scores(n, par):
            pe.wait_ge(query_done, n + 1)
            pe.wait_ge(d_key[par], landed(n, par))
            at_least(pe, exp_done, n)
            for m in range(C):
                for k in range(C):
                    ins = pe.matmul(pS[:, m], query[:, k, m * P:m * P + P], key_t[par][:, k], start=(k == 0), stop=(k == C - 1))
            ins.then_inc(s_mm, 1)

        def turn(n):
            pe.wait_ge(prob_done, C * (n + 1))
            at_least(pe, pt_done, n)
            for k in range(C):
                for m in range(C):
                    ins = pe.transpose(pT[:, m, k * P:k * P + P], prob[:, k, m * P:m * P + P], ident[:])
            ins.then_inc(t_mm, 1)

        def mix_values(n, par):
            pe.wait_ge(pt_done, n + 1)
            pe.wait_ge(d_val[par], landed(n, par))
            at_least(pe, y_done, n)
            for m in range(C):
                for k in range(C):
                    ins = pe.matmul(pV[:, m], value[par][:, k, m * P:m * P + P], prob_t[:, k], start=(k == 0), stop=(k == C - 1))
            ins.then_inc(v_mm, 1)

        def body(n, par, has_3, last):
            hidden(n, 0)
            hidden(n, 1)
            if has_3:
                scores(n - 1, 1 - par)
            output(n, par, 0)
            hidden(n, 2)
            output(n, par, 1)
            hidden(n, 3)
            output(n, par, 2)
            if has_3:
                turn(n - 1)
            output(n, par, 3)
            if has_3:
                mix_values(n - 1, 1 - par)

        loop(pe, body)
        scores(NB - 1, 1)
        turn(NB - 1)
        mix_values(NB - 1, 1)


def build_program(nc, t):
    NB = t["xT"].shape[0]
    with ExitStack() as whole:
        X = whole.enter_context(nc.sbuf_tensor("x_all", [P, C, NB * S], F32))
        shapes = {"ident": [P, P], "iota": [P, S], "sel_den": [P, 4, 32], "sel_rep": [P, C, P], "par_mask": [P, 2]}
        consts = {name: whole.enter_context(nc.sbuf_tensor(name, shape, F32)) for name, shape in shapes.items()}
        consts["ident_bf"] = whole.enter_context(nc.sbuf_tensor("ident_bf", [P, P], BF16))
        const_loaded = whole.enter_context(nc.semaphore("const_loaded"))
        const_cast = whole.enter_context(nc.semaphore("const_cast"))

        with nc.Block() as block:
            @block.sync
            def _(sp):
                for name in shapes:
                    sp.dma_start(consts[name][:], t[name]).then_inc(const_loaded, 16)
                sp.wait_ge(const_loaded, 16 * len(shapes))

            @block.vector
            def _(dve):
                dve.wait_ge(const_loaded, 16 * len(shapes))
                dve.tensor_copy(consts["ident_bf"][:], consts["ident"][:]).then_inc(const_cast, 1)
                dve.wait_ge(const_cast, 1)

        for layer in (attention_layer, trace_layer, expert_and_final):
            with ExitStack() as tiles:
                layer(nc, whole, tiles, t, X, NB, consts)



def shape_constants():
    import numpy as np
    p, o, i = np.arange(P), np.arange(P), np.arange(32)
    f = np.float32
    sel_den = np.stack([np.tile((i % 4 == q).astype(f), (P, 1)) for q in range(4)], 1)
    source = [32 * (o // 32) + 2 * c + o % 32 // 16 for c in range(C)]
    sel_rep = np.stack([(p[:, None] == s[None]).astype(f) for s in source], 1)
    before = np.concatenate([STEP * np.arange(CHUNKS)[None] - 1 - p[:, None],
                             STEP * np.arange(LATE, CHUNKS)[None] - 1 - P - p[:, None]], 1)
    return {
        "ident": np.eye(P, dtype=f), "iota": np.tile(np.arange(S, dtype=f), (P, 1)),
        "sel_den": sel_den, "sel_rep": sel_rep,
        "par_mask": np.stack([p // DH % 2 == 0, p // DH % 2 == 1], 1).astype(f),
        "lag_n": np.maximum(before, 0).astype(f), "lag_on": (before >= 0).astype(f),
        "ramp": np.tile((i % STEP + 1).astype(f), (P, 1)),
        "own": (p[:, None] // 32 == i[None] // STEP).astype(f),
    }


def layouts(a):
    import numpy as np

    def turned(w):
        return w.T

    def column(b):
        return b.reshape(-1, P).T

    def head_rows(w):
        return w.reshape((C, 2, 4, DH) + w.shape[1:]).swapaxes(1, 2).reshape(w.shape)

    l0, l1, l2 = ({k[8:]: v for k, v in a.items() if k.startswith(p)} for p in ("L0_cond_", "L1_cond_", "L2_cond_"))
    wn2 = np.concatenate([turned(a["cond_256"]), a["condB_bn2"][None]])
    out = {
        "xT": a["x"].transpose(0, 2, 1),
        "wq": turned(l0["Wq"]), "wk": turned(l0["Wk"]), "wv": turned(l0["Wv"]), "wo": head_rows(turned(l0["Wo"])),
        "bq": column(l0["bq"]), "bk": column(l0["bk"]), "bv": column(head_rows(l0["bv"])), "bo": column(l0["bo"]),
        "idx": a["itok_Sx32_0_1023"], "valid": a["mask_Sx32_bk1"],
        "mask": a["mask_SxS_bk0"], "maskT": turned(a["mask_SxS_bk0"]),
        "u": a["condB_uprev"],
        "wg": turned(l1["Wg"]), "wn1": turned(l1["Wn1"]), "wn2": wn2, "wn2_3": np.tile(wn2, (1, 3)),
        "wsoma": turned(l1["Wsoma"]), "wtemp": turned(l1["Wtemp"]), "wout": turned(l1["Wout"]),
        "bg": column(l1["bg"]), "bn1": l1["bn1"].reshape(-1, 1), "bsoma": column(l1["bsoma"]),
        "btemp": column(l1["btemp"]), "gamma": column(l1["gamma"]), "beta": column(l1["beta"]),
        "tau_c": l1["tau_ctx"].reshape(1), "tau_col": np.tile(a["condB_tauraws"], P // TRACES).reshape(P, 1),
        "tau_row": a["condB_tauraws"], "blend_t": turned(a["cond_1024"]),
        "w1": l2["W1"], "b1": column(l2["b1"]), "w2": l2["W2"], "b2": l2["b2"].reshape(-1, 1),
        "we": l2["We"].reshape(EXPERTS, HC, P, -1).swapaxes(1, 2), "be": l2["be"][:, :, None],
        "embed": a["L3_cond_braak_embed"], "expert": a["itok_B_0_7"][None], "stage": a["itok_B_0_5"][None],
        "key": a["fside_BxSxS_0"], "keyT": a["fside_BxSxS_0"].transpose(0, 2, 1),
    }
    out.update(shape_constants())
    return out


def kernel(**inputs):
    import numpy as np
    import concourse.bacc as bacc
    from concourse.bass_utils import run_bass_kernel_spmd

    data = layouts({name: np.asarray(a) for name, a in inputs.items()})
    nc = bacc.Bacc("TRN2", target_bir_lowering=False, num_devices=1)
    arrays, t = {}, {}
    for name, a in data.items():
        a = np.ascontiguousarray(a)
        arrays[f"in_{name}"] = a
        t[name] = nc.dram_tensor(f"in_{name}", a.shape, mybir.dt.from_np(a.dtype), kind="ExternalInput").ap()
    shape = data["xT"].shape
    t["out"] = nc.dram_tensor("out_0", shape, F32, kind="ExternalOutput").ap()
    build_program(nc, t)
    result = run_bass_kernel_spmd(nc, [arrays], core_ids=[0])
    return result.results[0]["out_0"].transpose(0, 2, 1)
```

```python
from contextlib import contextmanager, ExitStack

import concourse.bass as bass
from concourse import mybir

F32 = mybir.dt.float32
F32R = mybir.dt.float32r
BF16 = mybir.dt.bfloat16
I32 = mybir.dt.int32
U8 = mybir.dt.uint8
ALU = mybir.AluOpType
ACT = mybir.ActivationFunctionType
AX = mybir.AxisListType

P = 128
S = 256
D = 256
C = D // P
HEADS, DH = 16, 16
K_SPARSE = 32
NEG = -1.0e30
BIG = 3.0e38
GROUPS = 8
TERMS = 3
E_BUFS = 4


def at_least(eng, sem, value):
    if isinstance(value, int) and value <= 0:
        return
    eng.wait_ge(sem, value)


def rows_group(g):
    half, c, rows = g // 4, g // 2 % 2, g % 2
    return 2 * c + half, rows


def landed(n, par):
    return 8 * (n - par) + 16


@contextmanager
def pairs(eng, first, end):
    with eng.Fori(0, (end - first) // 2) as i:
        yield i * 2 + first


def attention_layer(nc, sem_ctx, ctx, t, X, NB, consts):
    def sb(name, shape, dt):
        return ctx.enter_context(nc.sbuf_tensor("a_" + name, shape, dt))

    def ps(name, shape, dt=F32):
        return ctx.enter_context(nc.psum_tensor("a_" + name, shape, dt))

    def sem(name):
        return sem_ctx.enter_context(nc.semaphore("a_" + name))

    ident, ident_bf, iota = consts["ident"], consts["ident_bf"], consts["iota"]
    sel_sum, sel_rep = consts["sel_sum"], consts["sel_rep"]

    wq, wk, wv, wo = (sb(n, [P, C, D], F32) for n in ("wq", "wk", "wv", "wo"))
    bias = sb("bias", [P, 4, C], F32)
    bq = sb("bq", [P, C], F32)
    bq_s = sb("bq_s", [P, C, 2], F32)
    bo_all = sb("bo_all", [P, C], F32)
    par_mask = consts["par_mask"]
    xs = [sb(f"xs{i}", [P, C, S], F32) for i in range(2)]
    q_hi = sb("q_hi", [P, C, 2, S], F32R)
    q_lo = sb("q_lo", [P, C, 2, S], F32R)
    q_full = sb("q_full", [P, C, 2, S], F32)
    k_hi = sb("k_hi", [P, C, S], F32R)
    k_lo = sb("k_lo", [P, C, S], F32R)
    k_full = sb("k_full", [P, C, S], F32)
    delta = sb("delta", [P, C, S], F32)
    q_st = [sb(f"q_st{i}", [P, HEADS, S], F32R) for i in range(2)]
    k_st = [sb(f"k_st{i}", [P, HEADS // 2, S], F32R) for i in range(2)]
    v_pad = [sb(f"v_pad{i}", [P, C, HEADS, 32], F32) for i in range(2)]
    e = [sb(f"e{i}", [P, 4, S], F32) for i in range(E_BUFS)]
    neg_max = sb("neg_max", [P, C, HEADS], F32)
    max_row = sb("max_row", [HEADS, S], F32R)
    raw_v = [sb(f"raw{half}", [P, C, S], F32) for half in range(2)]
    even = sb("even", [P, C, S], F32)
    r_den = sb("r_den", [P, P], F32)
    r_rep = sb("r_rep", [P, C, S], F32)
    att = sb("att", [P, C, S], F32)
    u_all = sb("u_all", [P, NB], F32)
    lam = sb("lam", [P, NB], F32)
    decay = sb("decay", [P, NB], F32)
    mix = sb("mix", [P, NB, 4], F32)
    mix_m, mix_w = sb("mix_m", [P, 4], F32), sb("mix_w", [P, 4], F32)
    idx_i = sb("idx_i", [P, C, K_SPARSE], I32)
    idx_f = e[3][:, 0:C, 0:K_SPARSE]
    val_u = sb("val_u", [P, C, K_SPARSE], U8)
    val_f = e[3][:, C:2 * C, 0:K_SPARSE]
    cnt = e[2][:, 0:C]
    cnt_t = sb("cnt_t", [P, C, S], F32)
    absent = sb("absent", [P, C, S], F32)
    msk_u = sb("msk_u", [P, 2, C, S], U8)
    off = sb("off", [P, C, S], F32)
    off_t = sb("off_t", [P, C, S], F32)
    t_off, t_sparse = sb("t_off", [P, C, S], F32), sb("t_sparse", [P, C, S], F32)
    w_t = [sb(f"w_t{i}", [P, C, S], F32) for i in range(2)]
    add_m = [sb(f"add_m{i}", [P, C, S], BF16) for i in range(2)]

    ps_s = [ps(f"s{b}", [P, 2, S]) for b in range(2)]
    ps_t = [ps(f"t{b}", [P, 2, S]) for b in range(2)]
    ps_v = [ps(f"v{half}", [P, C, S]) for half in range(2)]
    bank0 = ps("bank0", [P, C, S])
    bank1 = ps("bank1", [P, C, S])

    d_idx, d_u, d_mask, d_w, d_b = (sem(n) for n in ("d_idx", "d_u", "d_mask", "d_w", "d_b"))
    lam_done, g_step, scaled, lam_exp, decay_exp = (sem(n) for n in ("lam", "g_step", "scaled", "lam_exp", "decay_exp"))
    bo_mm, bo_done, cnt_mm, setup_done = sem("bo_mm"), sem("bo"), sem("cnt_mm"), sem("setup_done")
    d_xs, d_x = [sem("d_xs0"), sem("d_xs1")], sem("d_x")
    stack_free = [sem("stack_free0"), sem("stack_free1")]
    proj_q, proj_k, proj_v = sem("proj_q"), sem("proj_k"), sem("proj_v")
    qf_done, qhi_done, qlo_done, khi_done, klo_done, v_done = (sem(n) for n in ("qf", "qhi", "qlo", "khi", "klo", "v"))
    d_stack, d_max = [sem("d_stack0"), sem("d_stack1")], sem("d_max")
    s_done, red_done = sem("s_done"), sem("red_done")
    t_done, exp_done, p_done, pv_done = sem("t_done"), sem("exp_done"), sem("p_done"), sem("pv_done")
    mt_done, mrow_done = sem("mt_done"), sem("mrow_done")
    rden_done, rep_done, rrep_done, att_done, wo_done, x1_done = (sem(n) for n in ("rden", "rep", "rrep", "att", "wo", "x1"))
    mix_done, mixm_done, mixw_done, m_step, w_step, w_ready, m_ready = (
        sem(n) for n in ("mix", "mixm", "mixw", "m_step", "w_step", "w_ready", "m_ready"))
    kf_done, delta_done = sem("kf"), sem("delta")
    zero_done = sem("zero")
    raw_done, even_done, comb_done, sum_done = (sem(n) for n in ("raw", "even", "comb", "sum"))

    def batches(eng, body):
        body(0, 0, True, True, False)
        body(1, 1, True, True, True)
        if NB > 4:
            with pairs(eng, 2, NB - 2) as n:
                body(n, 0, True, True, True)
                body(n + 1, 1, True, True, True)
        body(NB - 2, 0, False, True, True)
        body(NB - 1, 1, False, False, True)

    STACK_DMAS = 2 * TERMS * 2

    block = ctx.enter_context(nc.Block())

    @block.sync
    def _(sp):
        sp.dma_start(idx_i[:], t["idx"].rearrange("(k p) j -> p k j", p=P)).then_inc(d_idx, 16)
        sp.dma_start(val_u[:], t["valid"].rearrange("(k p) j -> p k j", p=P)).then_inc(d_idx, 16)
        sp.dma_start(u_all[:], t["u"].partition_broadcast(P)).then_inc(d_u, 16)
        for i, name in enumerate(("bq", "bk", "bv", "bo")):
            sp.dma_start(bias[:, i], t[name]).then_inc(d_b, 16)
        for w, name in ((wq, "wq"), (wk, "wk"), (wv, "wv"), (wo, "wo")):
            sp.dma_start(w[:], t[name].rearrange("(k p) e -> p k e", p=P)).then_inc(d_w, 16)
        for n in range(2):
            sp.dma_start(xs[n][:], t["xT"][n].rearrange("(k p) s -> p k s", p=P)).then_inc(d_xs[n], 16)
        sp.dma_start(msk_u[:, 0], t["mask"].rearrange("(k p) s -> p k s", p=P)).then_inc(d_mask, 16)
        sp.dma_start(msk_u[:, 1], t["maskT"].rearrange("(k p) s -> p k s", p=P)).then_inc(d_mask, 16)

        def stack(n, par, half):
            sp.wait_ge(stack_free[half], n + 1)
            for done, dst, src, terms in ((khi_done, k_st[par], k_hi, (0, 1)), (qhi_done, q_st[par], q_hi, (0, 2)),
                                          (klo_done, k_st[par], k_lo, (2,)), (qlo_done, q_st[par], q_lo, (1,))):
                sp.wait_ge(done, n + 1)
                for term in terms:
                    for j in (2 * half, 2 * half + 1):
                        rows = src[32 * j:32 * j + 32].bitcast(F32)
                        to = dst[32 * term:32 * term + 32].bitcast(F32)
                        to = (to.rearrange("p (c j r) s -> p j c r s", c=C, j=4) if dst is q_st[par]
                              else to.rearrange("p (c j) s -> p j c s", c=C))
                        sp.dma_start(to[:, j], rows).then_inc(d_stack[half], 16)

        def maxima(n, par):
            sp.wait_ge(mrow_done, n + 1)
            sp.dma_start(q_st[par][96:97].bitcast(F32), max_row[:].bitcast(F32)).then_inc(d_max, 16)

        stack(0, 0, 0)
        stack(0, 0, 1)
        stack(1, 1, 0)
        maxima(0, 0)

        def staged(n, par):
            sp.wait_ge(proj_v, n - 1)
            sp.dma_start(xs[par][:], t["xT"][bass.ds(n, 1)].rearrange("o (k p) s -> p (o k) s", p=P)
                         if not isinstance(n, int) else t["xT"][n].rearrange("(k p) s -> p k s", p=P)).then_inc(d_xs[par], 16)

        def body(n, par, stage, proj, maxi):
            if maxi:
                stack(n + 1, 1 - par, 1)
            at_least(sp, d_x, n * 16)
            sp.dma_start(X[:, :, bass.ds(n * S, S)] if not isinstance(n, int) else X[:, :, n * S:n * S + S],
                         t["xT"][bass.ds(n, 1)].rearrange("o (k p) s -> p (o k) s", p=P)
                         if not isinstance(n, int) else t["xT"][n].rearrange("(k p) s -> p k s", p=P)).then_inc(d_x, 16)
            if proj:
                stack(n + 2, par, 0)
            if stage:
                staged(n + 3, 1 - par)
            if maxi:
                maxima(n + 1, 1 - par)

        staged(2, 0)
        body(0, 0, True, True, True)
        body(1, 1, True, True, True)
        if NB > 6:
            with pairs(sp, 2, NB - 4) as n:
                body(n, 0, True, True, True)
                body(n + 1, 1, True, True, True)
        body(NB - 4, 0, True, True, True)
        body(NB - 3, 1, False, True, True)
        body(NB - 2, 0, False, False, True)
        body(NB - 1, 1, False, False, False)

    @block.gpsimd
    def _(pool):
        for half in stack_free:
            pool.sem_inc(half, 2)
        for i in range(2):
            pool.memset(k_st[i][96:97].bitcast(F32), 1.0).then_inc(zero_done, 1)
            pool.wait_ge(zero_done, 2 * i + 1)
            pool.memset(v_pad[i][:], 1.0).then_inc(zero_done, 1)
            pool.wait_ge(zero_done, 2 * i + 2)
        def masks(n, par):
            pool.tensor_copy(mix_m[:], mix[:, n] if isinstance(n, int) else mix[:, bass.ds(n, 1)].rearrange("p o f -> p (o f)"))\
                .then_inc(mixm_done, 1)
            at_least(pool, w_ready, n - 1 if not (isinstance(n, int) and n < 2) else n)
            at_least(pool, m_ready, n)
            pool.wait_ge(mixm_done, n + 1)
            pool.tensor_tensor(t_sparse[:], absent[:], mix_m[:, 0:1].unsqueeze(2).to_broadcast([P, C, S]), ALU.mult).then_inc(m_step, 1)
            pool.tensor_scalar(t_off[:], off[:], mix_m[:, 3:4], None, ALU.mult).then_inc(m_step, 1)
            pool.wait_ge(m_step, n * 2 + 2)
            if not (isinstance(n, int) and n < 2):
                pool.wait_ge(s_done, (n - 1) * 2 * GROUPS)
            pool.tensor_tensor(add_m[par][:], t_off[:], t_sparse[:], ALU.add).then_inc(m_ready, 1)

        def weights(n, par):
            pool.tensor_copy(mix_w[:], mix[:, n] if isinstance(n, int) else mix[:, bass.ds(n, 1)].rearrange("p o f -> p (o f)"))\
                .then_inc(mixw_done, 1)
            at_least(pool, w_ready, n)
            pool.wait_ge(m_ready, NB if isinstance(n, int) and n + 2 > NB else (1 if isinstance(n, int) and n == 0 else n + 2))
            pool.wait_ge(mixw_done, n + 1)
            pool.tensor_tensor(t_sparse[:], cnt_t[:], mix_w[:, 0:1].unsqueeze(2).to_broadcast([P, C, S]), ALU.mult).then_inc(w_step, 1)
            pool.tensor_scalar(t_off[:], off_t[:], mix_w[:, 2:3], mix_w[:, 1:2], ALU.mult, ALU.add).then_inc(w_step, 1)
            pool.wait_ge(w_step, n * 2 + 2)
            if not (isinstance(n, int) and n < 2):
                pool.wait_ge(p_done, (n - 1) * GROUPS)
            pool.tensor_tensor(w_t[par][:], t_off[:], t_sparse[:], ALU.add).then_inc(w_ready, 1)

        def low_parts(n):
            pool.wait_ge(khi_done, n + 1)
            pool.tensor_tensor(k_lo[:], k_full[:], k_hi[:].bitcast(F32), ALU.subtract).then_inc(klo_done, 1)
            pool.wait_ge(qhi_done, n + 1)
            pool.tensor_tensor(q_lo[:], q_full[:], q_hi[:].bitcast(F32), ALU.subtract).then_inc(qlo_done, 1)

        def residual(n):
            pool.wait_ge(delta_done, n + 1)
            pool.wait_ge(d_x, 16 * (n + 1))
            xo = X[:, :, n * S:n * S + S] if isinstance(n, int) else X[:, :, bass.ds(n * S, S)]
            pool.tensor_tensor(xo, delta[:], xo, ALU.add).then_inc(x1_done, 1)

        def body(n, par, proj, maxi, finish):
            if proj:
                masks(n + 2, par)
            if maxi:
                weights(n + 1, 1 - par)
            if proj:
                low_parts(n + 2)
            if finish:
                residual(n - 1)

        low_parts(0)
        pool.wait_ge(mix_done, 1)
        pool.wait_ge(setup_done, 1)
        masks(0, 0)
        low_parts(1)
        weights(0, 0)
        masks(1, 1)
        batches(pool, body)
        residual(NB - 1)
        pool.wait_ge(x1_done, NB)

    @block.vector
    def _(dve):
        done = [0]

        def link(ins):
            done[0] += 1
            ins.then_inc(g_step, 1)
            dve.wait_ge(g_step, done[0])

        dve.wait_ge(d_idx, 16 * 2)
        link(dve.tensor_copy(idx_f, idx_i[:]))
        link(dve.tensor_copy(val_f, val_u[:]))
        link(dve.tensor_scalar(idx_f, idx_f, 1.0, None, ALU.add))
        link(dve.tensor_tensor(idx_f, idx_f, val_f, ALU.mult))
        link(dve.tensor_scalar(idx_f, idx_f, -1.0, None, ALU.add))
        link(dve.memset(cnt, 0.0))
        dve.wait_ge(lam_exp, 1)
        dve.tensor_scalar(lam[:], lam[:], 10.0, None, ALU.mult).then_inc(lam_done, 1)
        base = done[0]
        for j in range(K_SPARSE):
            for k in range(C):
                if j:
                    dve.wait_ge(g_step, base + (j - 1) * C + k + 1)
                dve.scalar_tensor_tensor(out=cnt[:, k], in0=iota[:], scalar=idx_f[:, k, j:j + 1], in1=cnt[:, k],
                                         op0=ALU.is_equal, op1=ALU.add).then_inc(g_step, 1)
        done[0] = base + C * K_SPARSE
        dve.wait_ge(g_step, done[0])
        link(dve.tensor_scalar(absent[:], cnt, 0.0, NEG, ALU.is_equal, ALU.mult))
        dve.wait_ge(d_mask, 16 * 2)
        link(dve.tensor_copy(off[:], msk_u[:, 0]))
        link(dve.tensor_copy(off_t[:], msk_u[:, 1]))
        link(dve.tensor_scalar(off[:], off[:], -1.0, 1.0, ALU.mult, ALU.add))
        link(dve.tensor_scalar(off_t[:], off_t[:], -1.0, 1.0, ALU.mult, ALU.add))
        dve.wait_ge(lam_done, 1)
        dve.wait_ge(decay_exp, 1)
        link(dve.tensor_scalar(mix[:, :, 0], lam[:], 1.0, None, ALU.is_ge))
        link(dve.tensor_scalar(mix[:, :, 1], mix[:, :, 0], -1.0, 1.0, ALU.mult, ALU.add))
        link(dve.tensor_scalar(decay[:], decay[:], -1.0, None, ALU.add))
        link(dve.tensor_tensor(mix[:, :, 2], mix[:, :, 1], decay[:], ALU.mult))
        link(dve.tensor_scalar(lam[:], lam[:], 1.0, -1.0, ALU.min, ALU.mult))
        dve.tensor_tensor(mix[:, :, 3], mix[:, :, 1], lam[:], ALU.mult).then_inc(mix_done, 1)
        dve.wait_ge(bo_mm, 1)
        dve.tensor_tensor(bo_all[:], ps_v[1][:, 0, 0:C], bias[:, 3], ALU.add).then_inc(bo_done, 1)
        dve.wait_ge(cnt_mm, 1)
        for k in range(C):
            dve.tensor_copy(cnt_t[:, k], bank0[:, k]).then_inc(g_step, 1)
        done[0] += C
        dve.wait_ge(g_step, done[0])
        dve.wait_ge(bo_done, 1)
        dve.sem_inc(setup_done, 1)

        def row_max(n, g):
            quad, qc = rows_group(g)
            if g == 0:
                at_least(dve, mt_done, n)
            for b in range(2):
                dve.wait_ge(s_done, 2 * (n * GROUPS + g) + b + 1)
                head = 4 * quad + 2 * b
                dve.tensor_reduce(neg_max[:, qc, head:head + 2], ps_s[b][:], AX.X, ALU.max, negate=True).then_inc(red_done, 1)

        def weigh(n, par, g):
            kc = g % 2
            dve.wait_ge(exp_done, 2 * (n * GROUPS + g + 1))
            if g == 0:
                dve.wait_ge(w_ready, n + 1)
            buf = e[g % E_BUFS]
            dve.scalar_tensor_tensor(out=buf[:], in0=buf[:], scalar=BIG,
                                     in1=w_t[par][:, kc].unsqueeze(1).to_broadcast([P, 4, S]),
                                     op0=ALU.min, op1=ALU.mult).then_inc(p_done, 1)

        def combine(n):
            dve.wait_ge(raw_done, 2 * (n + 1))
            dve.wait_ge(even_done, n + 1)
            at_least(dve, wo_done, n)
            dve.scalar_tensor_tensor(out=att[:], in0=ps_v[1][:], scalar=par_mask[:, 1:2], in1=even[:],
                                     op0=ALU.mult, op1=ALU.add).then_inc(comb_done, 1)

        def reciprocal(n):
            dve.wait_ge(sum_done, n + 1)
            at_least(dve, rep_done, n)
            dve.reciprocal(r_den[:], bank1[:, 0, 0:P]).then_inc(rden_done, 1)

        def normalize(n):
            dve.wait_ge(rrep_done, n + 1)
            dve.wait_ge(comb_done, n + 1)
            dve.tensor_tensor(att[:], att[:], r_rep[:], ALU.mult).then_inc(att_done, 1)

        def body(n, par, proj, maxi, finish):
            for g in range(GROUPS):
                if maxi:
                    row_max(n + 1, g)
                if g == 0 and finish:
                    combine(n - 1)
                if g > 0:
                    weigh(n, par, g - 1)
                if g == 2 and finish:
                    reciprocal(n - 1)
                if g == 4 and finish:
                    normalize(n - 1)
            weigh(n, par, GROUPS - 1)

        for g in range(GROUPS):
            row_max(0, g)
        batches(dve, body)
        combine(NB - 1)
        reciprocal(NB - 1)
        normalize(NB - 1)

    @block.scalar
    def _(act):
        act.wait_ge(d_u, 16)
        act.activation(lam[:], u_all[:], ACT.Exp, scale=-5.0).then_inc(lam_exp, 1)
        act.wait_ge(d_w, 16 * 4)
        act.wait_ge(d_b, 16 * 4)
        act.activation(wq[:], wq[:], ACT.Copy, scale=0.25).then_inc(scaled, 1)
        act.activation(bq[:], bias[:, 0], ACT.Copy, scale=0.25).then_inc(scaled, 1)
        act.wait_ge(scaled, 2)
        for par in range(2):
            act.activation(bq_s[:, :, par], bq[:], ACT.Copy, scale=par_mask[:, par:par + 1]).then_inc(scaled, 1)
        act.wait_ge(scaled, 4)
        act.wait_ge(lam_done, 1)
        act.activation(decay[:], lam[:], ACT.Exp, scale=-1.0).then_inc(decay_exp, 1)
        act.wait_ge(zero_done, 4)

        def whole_q(n, k):
            if k == 0:
                at_least(act, qlo_done, n)
                act.wait_ge(proj_q, n + 1)
            for r in range(2):
                act.activation(q_full[:, k, r], bank0[:, k], ACT.Identity,
                               bias=bq_s[:, k, r:r + 1], scale=par_mask[:, r:r + 1]).then_inc(qf_done, 1)

        def high_q(n):
            if not (isinstance(n, int) and n == 0):
                for half in d_stack:
                    act.wait_ge(half, n * 16 * STACK_DMAS)
            act.wait_ge(qf_done, 2 * C * (n + 1))
            act.activation(q_hi[:], q_full[:], ACT.Copy).then_inc(qhi_done, 1)

        def whole_k(n):
            act.wait_ge(proj_k, n + 1)
            at_least(act, klo_done, n)
            for k in range(C):
                ins = act.activation(k_full[:, k], bank1[:, k], ACT.Identity, bias=bias[:, 1, k:k + 1])
            ins.then_inc(kf_done, 1)

        def high_k(n):
            if not (isinstance(n, int) and n == 0):
                for half in d_stack:
                    act.wait_ge(half, n * 16 * STACK_DMAS)
            act.wait_ge(kf_done, n + 1)
            act.activation(k_hi[:], k_full[:], ACT.Copy).then_inc(khi_done, 1)

        def projected(n):
            act.wait_ge(wo_done, n + 1)
            at_least(act, x1_done, n)
            for k in range(C):
                ins = act.activation(delta[:, k], bank0[:, k], ACT.Identity, bias=bo_all[:, k:k + 1])
            ins.then_inc(delta_done, 1)

        def values(n, par):
            act.wait_ge(proj_v, n + 1)
            if not (isinstance(n, int) and n < 2):
                act.wait_ge(pv_done, (n - 1) * GROUPS)
            for k in range(C):
                for half in range(2):
                    src = bank0[:, k].rearrange("p (c h j d) -> p c h j d", c=C, h=2, j=4)[:, :, half]
                    dst = v_pad[par][:, k].rearrange("p (c h j) w -> p c h j w", c=C, h=2)[:, :, half, :, 16 * half:16 * half + 16]
                    ins = act.activation(dst, src, ACT.Copy)
            ins.then_inc(v_done, 1)

        def exps(n, g):
            if not (isinstance(n, int) and n == 0 and g < E_BUFS):
                act.wait_ge(pv_done, n * GROUPS + g - E_BUFS + 1)
            for b in range(2):
                act.wait_ge(t_done, 2 * (n * GROUPS + g) + b + 1)
                act.activation(e[g % E_BUFS][:, 2 * b:2 * b + 2], ps_t[b][:], ACT.Exp).then_inc(exp_done, 1)

        def max_rows(n):
            act.wait_ge(mt_done, n + 1)
            if not (isinstance(n, int) and n == 0):
                act.wait_ge(d_max, 16 * n)
            act.activation(max_row[:], bank1[0:HEADS, 0], ACT.Copy).then_inc(mrow_done, 1)

        def raw(n, half):
            act.wait_ge(pv_done, n * GROUPS + 4 * (half + 1))
            at_least(act, sum_done, n)
            act.activation(raw_v[half][:], ps_v[half][:], ACT.Copy).then_inc(raw_done, 1)
            if half == 0:
                at_least(act, comb_done, n)
                act.activation(even[:], ps_v[0][:], ACT.Copy, scale=par_mask[:, 0:1]).then_inc(even_done, 1)

        def spread(n):
            act.wait_ge(rep_done, n + 1)
            at_least(act, att_done, n)
            act.activation(r_rep[:], bank1[:], ACT.Copy).then_inc(rrep_done, 1)

        def body(n, par, proj, maxi, finish):
            for g in range(GROUPS):
                if g == 0 and proj:
                    whole_q(n + 2, 0)
                exps(n, g)
                if proj:
                    if g == 1:
                        whole_k(n + 2)
                        whole_q(n + 2, 1)
                    elif g == 2:
                        high_k(n + 2)
                    elif g == 3:
                        high_q(n + 2)
                if g == 6 and maxi:
                    values(n + 1, 1 - par)
                if g == 3 and finish:
                    spread(n - 1)
                if g == 6:
                    raw(n, 0)
                if g == 7 and finish:
                    projected(n - 1)
            if maxi:
                max_rows(n + 1)
            raw(n, 1)

        for n in range(2):
            whole_q(n, 0)
            whole_q(n, 1)
            whole_k(n)
            if n == 0:
                values(0, 0)
            high_k(n)
            high_q(n)
        max_rows(0)
        batches(act, body)
        spread(NB - 1)
        projected(NB - 1)

    @block.tensor
    def _(pe):
        pe.wait_ge(d_w, 16 * 4)
        pe.wait_ge(d_b, 16 * 4)
        for m in range(C):
            for k in range(C):
                ins = pe.matmul(ps_v[1][:, 0, m:m + 1], wo[:, k, m * P:m * P + P], bias[:, 2, k:k + 1],
                                start=(k == 0), stop=(k == C - 1))
        ins.then_inc(bo_mm, 1)

        def turn_counts():
            pe.wait_ge(qf_done, 2 * 2 * C)
            pe.wait_ge(g_step, 6 + C * K_SPARSE)
            for qc in range(C):
                for kc in range(C):
                    ins = pe.transpose(bank0[:, kc, qc * P:qc * P + P], cnt[:, qc, kc * P:kc * P + P], ident[:])
            ins.then_inc(cnt_mm, 1)

        def project_q(n, par):
            pe.wait_ge(d_xs[par], landed(n, par))
            if isinstance(n, int) and n < 4:
                at_least(pe, v_done, (0, 1, 1, 2)[n])
            else:
                pe.wait_ge(delta_done, n - 3)
            for m in range(C):
                for k in range(C):
                    ins = pe.matmul(bank0[:, m], wq[:, k, m * P:m * P + P], xs[par][:, k], start=(k == 0), stop=(k == C - 1))
            ins.then_inc(proj_q, 1)

        def project_k(n, par):
            if isinstance(n, int) and n == 1:
                pe.wait_ge(kf_done, 1)
            elif not (isinstance(n, int) and n == 0):
                pe.wait_ge(mrow_done, n - 1)
            for m in range(C):
                for k in range(C):
                    ins = pe.matmul(bank1[:, m], wk[:, k, m * P:m * P + P], xs[par][:, k], start=(k == 0), stop=(k == C - 1))
            ins.then_inc(proj_k, 1)

        def project_v(n, par, m):
            if m == 0:
                if isinstance(n, int) and n == NB - 1:
                    pe.wait_ge(delta_done, n - 2)
                else:
                    pe.wait_ge(qf_done, 2 * C * (1 if isinstance(n, int) and n == 0 else n + 2))
            for k in range(C):
                ins = pe.matmul(bank0[:, m], xs[par][:, k, m * P:m * P + P], wv[:, k], start=(k == 0), stop=(k == C - 1))
            if m == C - 1:
                ins.then_inc(proj_v, 1)

        def score_rows(n, par, g):
            quad, qc = rows_group(g)
            if g == 0:
                pe.wait_ge(m_ready, n + 1)
            if g % 4 == 0:
                pe.wait_ge(d_stack[g // 4], (n + 1) * 16 * STACK_DMAS)
            for b in range(2):
                if not (isinstance(n, int) and n == 0 and g == 0):
                    pe.wait_ge(red_done, 2 * (n * GROUPS + g) + b - 1)
                pe.matmul(ps_s[b][:], ident_bf[:], add_m[par][:, qc].unsqueeze(1).to_broadcast([P, 2, S]), start=True, stop=False)
                for r in range(2):
                    slot = 4 * quad + 2 * b + r
                    ins = pe.matmul(ps_s[b][:, r], q_st[par][0:96, slot, qc * P:qc * P + P],
                                    k_st[par][0:96, slot // 2], start=False, stop=(r == 1))
                ins.then_inc(s_done, 1)

        def score_cols(n, par, g):
            quad, kc = rows_group(g)
            if g == 0:
                pe.wait_ge(d_max, 16 * (n + 1))
            for b in range(2):
                if not (isinstance(n, int) and n == 0 and g == 0):
                    pe.wait_ge(exp_done, 2 * (n * GROUPS + g) + b - 1)
                pair = 2 * quad + b
                pe.matmul(ps_t[b][:], k_st[par][0:97, pair, kc * P:kc * P + P],
                          q_st[par][0:97, 2 * pair:2 * pair + 2], start=True, stop=True).then_inc(t_done, 1)

        def mix_values(n, par, g):
            quad, kc = rows_group(g)
            pe.wait_ge(p_done, n * GROUPS + g + 1)
            half = quad % 2
            if g == 0:
                pe.wait_ge(v_done, n + 1)
                at_least(pe, even_done, n)
            if g == 4:
                at_least(pe, comb_done, n)
            for j in range(4):
                ins = pe.matmul(ps_v[half][32 * j:32 * j + 32, quad // 2], v_pad[par][:, kc, 4 * quad + j], e[g % E_BUFS][:, j],
                                start=(g % 4 == 0), stop=(g % 4 == 3), tile_position=(0, 32 * j), skip_group_check=True)
                if j == 2 and g % 4 == 1:
                    ins.then_inc(stack_free[g // 4], 1)
            ins.then_inc(pv_done, 1)

        def transpose_max(n):
            pe.wait_ge(red_done, (n + 1) * 2 * GROUPS)
            if isinstance(n, int) and n < 2:
                pe.wait_ge(kf_done, n + 2)
            else:
                pe.wait_ge(rrep_done, n - 1)
            for qc in range(C):
                ins = pe.transpose(bank1[0:HEADS, 0, qc * P:qc * P + P], neg_max[:, qc], ident[:])
            ins.then_inc(mt_done, 1)

        def collect(n):
            pe.wait_ge(raw_done, 2 * (n + 1))
            if isinstance(n, int) and n == NB - 1:
                pe.wait_ge(rrep_done, n)
            elif isinstance(n, int) and n + 4 > NB:
                pe.wait_ge(mrow_done, n + 2)
            else:
                pe.wait_ge(kf_done, n + 4)
            steps = [(qc, quad) for qc in range(C) for quad in range(4)]
            for qc, quad in steps:
                ins = pe.matmul(bank1[:, 0, 0:P], sel_sum[:, qc, quad], raw_v[quad % 2][:, quad // 2, qc * P:qc * P + P],
                                start=((qc, quad) == steps[0]), stop=((qc, quad) == steps[-1]))
            ins.then_inc(sum_done, 1)

        def spread(n):
            pe.wait_ge(rden_done, n + 1)
            for c in range(C):
                for qc in range(C):
                    ins = pe.matmul(bank1[:, c, qc * P:qc * P + P], sel_rep[:, qc, c], r_den[:], start=True, stop=True)
            ins.then_inc(rep_done, 1)

        def project_out(n):
            pe.wait_ge(att_done, n + 1)
            if isinstance(n, int) and n + 3 > NB:
                pe.wait_ge(v_done, NB)
                at_least(pe, delta_done, n)
            else:
                pe.wait_ge(v_done, n + 3)
            for m in range(C):
                for k in range(C):
                    ins = pe.matmul(bank0[:, m], wo[:, k, m * P:m * P + P], att[:, k], start=(k == 0), stop=(k == C - 1))
            ins.then_inc(wo_done, 1)

        def body(n, par, proj, maxi, finish):
            for g in range(GROUPS):
                if maxi:
                    score_rows(n + 1, 1 - par, g)
                if g == 0 and proj:
                    project_q(n + 2, par)
                if g == 1 and proj:
                    project_k(n + 2, par)
                score_cols(n, par, g)
                if finish:
                    if g == 2:
                        collect(n - 1)
                    elif g == 3:
                        spread(n - 1)
                    elif g == 7:
                        project_out(n - 1)
                if maxi and g in (4, 5):
                    project_v(n + 1, 1 - par, g - 4)
                if g > 1:
                    mix_values(n, par, g - 2)
            if maxi:
                transpose_max(n + 1)
            mix_values(n, par, GROUPS - 2)
            mix_values(n, par, GROUPS - 1)

        pe.wait_ge(scaled, 4)
        for n in range(2):
            project_q(n, n)
            project_k(n, n)
            if n == 0:
                project_v(0, 0, 0)
                project_v(0, 0, 1)
        turn_counts()
        for g in range(GROUPS):
            score_rows(0, 0, g)
        transpose_max(0)
        batches(pe, body)
        collect(NB - 1)
        spread(NB - 1)
        project_out(NB - 1)

TRACES = 32
HID1 = 64
STEP = 8
CHUNKS = S // STEP
LATE = 16
TABLE = CHUNKS + LATE


def trace_layer(nc, sem_ctx, ctx, t, X, NB, consts):
    def sb(name, shape, dt=F32):
        return ctx.enter_context(nc.sbuf_tensor("b_" + name, shape, dt))

    def ps(name, shape, dt=F32):
        return ctx.enter_context(nc.psum_tensor("b_" + name, shape, dt))

    def sem(name):
        return sem_ctx.enter_context(nc.semaphore("b_" + name))

    ident = consts["ident"]
    wg = sb("wg", [P, 2 * C, D])
    wn1 = sb("wn1", [P, C, HID1])
    wn2 = sb("wn2", [HID1 + 1, TRACES])
    wn2_3 = sb("wn2_3", [HID1 + 1, 3 * TRACES])
    wsoma, wtemp, wout = sb("wsoma", [P, C, D]), sb("wtemp", [P, C, D]), sb("wout", [P, C, D])
    parts = lambda n, shape: (sb(n + "_hi", shape, F32R), sb(n + "_lo", shape, F32R))
    wg_p, wn1_p = parts("wg", [P, 2 * C, D]), parts("wn1", [P, C, HID1])
    wsoma_p, wtemp_p, wout_p = (parts(n, [P, C, D]) for n in ("wsoma", "wtemp", "wout"))
    x_p = [parts(f"x{i}", [P, C, S]) for i in range(2)]
    ctx_p, temp_p, mixed_p = (parts(n, [P, C, S]) for n in ("ctx", "temp", "mixed"))
    bg_h, bsoma, btemp_h, gamma, beta = (sb(n, [P, C]) for n in ("bg", "bsoma", "btemp", "gamma", "beta"))
    bn1 = sb("bn1", [HID1, 1])
    tau_c = sb("tau_c", [P, 1])
    tau_col = sb("tau_col", [P, 1])
    tau_row = sb("tau_row", [P, TRACES])
    sp_c, sp_col, sp_row = sb("sp_c", [P, 1]), sb("sp_col", [P, 1]), sb("sp_row", [P, TRACES])
    alpha_c = sb("alpha_c", [P, 1])
    lag_n = sb("lag_n", [P, TABLE])
    lag_on = sb("lag_on", [P, TABLE])
    ramp = sb("ramp", [P, 32])
    own = sb("own", [P, 32])
    table = sb("table", [P, TABLE, TRACES])
    spread_w = sb("spread_w", [P, 32])
    power = sb("power", [P, STEP])
    blend_t = sb("blend_t", [P, C, TRACES])
    bl_max = sb("bl_max", [P, C])
    bl_sum = sb("bl_sum", [P, C])
    bl_inv = sb("bl_inv", [P, C])
    bl_rep = sb("bl_rep", [P, C, 4, TRACES])
    w_rep = sb("w_rep", [P, D])
    w_lag = sb("w_lag", [P, STEP, D])
    w_st = sb("w_st", [P, STEP, D], F32R)
    mean_w = sb("mean_w", [P, C])
    mean_mat = sb("mean_mat", [P, P])
    eps = sb("eps", [P, 1])
    table_pick = sb("table_pick", [P, 1])

    ctx_e = sb("ctx_e", [P, C, S])
    th_g = sb("th_g", [P, C, S])
    gated = [sb(f"gated{i}", [P, C, S]) for i in range(2)]
    gated_t = [sb(f"gated_t{i}", [P, C, D]) for i in range(2)]
    h1 = sb("h1", [HID1 + 1, S])
    th_m = sb("th_m", [3 * TRACES, S])
    mod_f = sb("mod_f", [3 * TRACES, S])
    mod_st = [sb(f"mod_st{i}", [3 * TRACES, S], F32R) for i in range(2)]
    th_t = sb("th_t", [P, C, TRACES])
    mod_t = sb("mod_t", [P, C, TRACES])
    decayed = [sb(f"decayed{i}", [P, TABLE, TRACES]) for i in range(2)]
    state = [sb(f"state{i}", [P, 2, D]) for i in range(2)]
    inner = sb("inner", [P, C, S])
    prod = [sb(f"prod{i}", [P, C, S]) for i in range(2)]
    outer_t = sb("outer_t", [P, C, D])
    temporal = sb("temporal", [P, C, S])
    th_o = sb("th_o", [P, C, S])
    soma = sb("soma", [P, C, S])
    mixed = sb("mixed", [P, C, S])
    square = sb("square", [P, C, S])
    std = sb("std", [P, S])
    rstd = sb("rstd", [P, S])
    normed = sb("normed", [P, C, S])
    scaled = sb("scaled", [P, C, S])

    pA = ps("pA", [P, C, S])
    pB = ps("pB", [P, 2, S])
    pS = [ps(f"pS{i}", [P, 2, D]) for i in range(2)]
    pL = [ps(f"pL{i}", [P, C, S]) for i in range(2)]
    pY = ps("pY", [P, C, S])
    pZ = ps("pZ", [P, C, S])

    d_tab, w_hi, w_lo, ones_done = sem("d_tab"), sem("w_hi"), sem("w_lo"), sem("ones")
    xhi_done, xlo_done, chi_done, clo_done, temphi_done, templo_done, mixhi_done, mixlo_done = (
        sem(n) for n in ("xhi", "xlo", "chi", "clo", "temphi", "templo", "mixhi", "mixlo"))
    d_in, v_step, a_set, a_bl, pe_set, set_done = (sem(n) for n in ("d_in", "v_step", "a_set", "a_bl", "pe_set", "set_done"))
    ctx_done, wg_done, thg_done, gated_done = (sem(n) for n in ("ctx", "wg", "thg", "gated"))
    h1_done, gelu1_done, mod_done, thm_done, modst_done, vmod = (sem(n) for n in ("h1", "gelu1", "mod", "thm", "modst", "vmod"))
    modt_done, tht_done, modt_ready, dec_done = (sem(n) for n in ("modt", "tht", "modt_ready", "dec"))
    gt_done, gtev_done = sem("gt"), sem("gtev")
    st_done, sw_done, yin_done, yev_done, ytr_done = (sem(n) for n in ("st", "sw", "yin", "yev", "ytr"))
    lag_done, prod_done, inner_done, temp_done = (sem(n) for n in ("lag", "prod", "inner", "temp"))
    soma_mm, soma_done, gate_mm, tho_done, mixed_done = (sem(n) for n in ("soma_mm", "soma", "gate_mm", "tho", "mixed"))
    out_mm, sq_done, var_mm, std_done, rstd_done, normed_done, scaled_done, x2_done = (
        sem(n) for n in ("out_mm", "sq", "var_mm", "std", "rstd", "normed", "scaled", "x2"))

    TABLES = {"tau_c": tau_c, "tau_col": tau_col, "tau_row": tau_row, "blend_t": blend_t, "lag_n": lag_n, "ramp": ramp,
              "lag_on": lag_on, "own": own}
    WEIGHTS = {"wn1": wn1, "wg": wg, "wsoma": wsoma, "wtemp": wtemp, "wout": wout, "bg": bg_h, "bn1": bn1, "wn2": wn2,
               "wn2_3": wn2_3, "bsoma": bsoma, "btemp": btemp_h, "gamma": gamma, "beta": beta}

    def xn(n, k=None):
        at = slice(n * S, n * S + S) if isinstance(n, int) else bass.ds(n * S, S)
        return X[:, :, at] if k is None else X[:, k, at]

    def rows(w):
        return w[:].rearrange("p c s -> p (c s)")

    block = ctx.enter_context(nc.Block())

    def loop(eng, body):
        body(0, 0, True, False)
        if NB > 2:
            with pairs(eng, 1, NB - 1) as n:
                body(n, 1, True, True)
                body(n + 1, 0, True, True)
        body(NB - 1, 1, False, True)

    @block.sync
    def _(sp):
        for loads, landed_sem in ((TABLES, d_tab), (WEIGHTS, d_in)):
            for name, tile in loads.items():
                src = t[name]
                if name in ("wg", "wn1", "wsoma", "wtemp", "wout", "blend_t"):
                    src = src.rearrange("(k p) e -> p k e", p=P)
                if name in ("tau_c", "tau_row"):
                    src = src.partition_broadcast(P)
                sp.dma_start(tile[:], src).then_inc(landed_sem, 16)

    @block.gpsimd
    def _(pool):
        pool.memset(h1[HID1:HID1 + 1], 1.0).then_inc(ones_done, 1)
        pool.wait_ge(ones_done, 1)
        pool.wait_ge(w_hi, 1)
        for i, (w, (hi, lo)) in enumerate(((wn1, wn1_p), (wg, wg_p), (wsoma, wsoma_p), (wtemp, wtemp_p))):
            pool.tensor_tensor(lo[:], w[:], hi[:].bitcast(F32), ALU.subtract).then_inc(w_lo, 1)
            pool.wait_ge(w_lo, i + 1)

        def decays(n, par):
            pool.wait_ge(modt_ready, n + 1)
            if not (isinstance(n, int) and n < 2):
                pool.wait_ge(st_done, (n - 1) * 4)
            for k, lo, cnt in ((0, 0, CHUNKS), (1, CHUNKS, LATE)):
                ins = pool.tensor_tensor(decayed[par][:, lo:lo + cnt], table[:, lo:lo + cnt],
                                         mod_t[:, k].unsqueeze(1).to_broadcast([P, cnt, TRACES]), ALU.mult)
            ins.then_inc(dec_done, 1)

        def residual(n):
            pool.wait_ge(scaled_done, n + 1)
            pool.tensor_tensor(xn(n), scaled[:], xn(n), ALU.add).then_inc(x2_done, 1)

        def low_inputs(n, par):
            pool.wait_ge(xhi_done, n + 1)
            pool.tensor_tensor(x_p[par][1][:], xn(n), x_p[par][0][:].bitcast(F32), ALU.subtract).then_inc(xlo_done, 1)
            pool.wait_ge(chi_done, n + 1)
            pool.tensor_tensor(ctx_p[1][:], ctx_e[:], ctx_p[0][:].bitcast(F32), ALU.subtract).then_inc(clo_done, 1)

        def body(n, par, has_a, has_c):
            if has_a:
                low_inputs(n + 1, 1 - par)
                decays(n + 1, 1 - par)
            if has_c:
                residual(n - 1)

        low_inputs(0, 0)
        pool.wait_ge(set_done, 1)
        decays(0, 0)
        loop(pool, body)
        residual(NB - 1)
        pool.wait_ge(x2_done, NB)

    @block.vector
    def _(dve):
        done = [0]

        def link(ins):
            done[0] += 1
            ins.then_inc(v_step, 1)
            dve.wait_ge(v_step, done[0])

        def context(n):
            at_least(dve, clo_done, n)
            for k in range(C):
                ins = dve.tensor_tensor_scan(ctx_e[:, k], alpha_c[:].to_broadcast([P, S]), xn(n, k), 0.0, ALU.mult, ALU.add)
            ins.then_inc(ctx_done, 1)

        dve.wait_ge(d_tab, 16 * len(TABLES))
        link(dve.memset(eps[:], 1e-5))
        link(dve.memset(mean_mat[:], 1.0 / D))
        for tau in (tau_c, tau_col, tau_row):
            link(dve.tensor_scalar(tau[:], tau[:], 80.0, None, ALU.min))
        link(dve.tensor_reduce(bl_max[:], blend_t[:], AX.X, ALU.max, negate=True))
        dve.wait_ge(a_set, 1)
        for sp_, tau in ((sp_c, tau_c), (sp_col, tau_col), (sp_row, tau_row)):
            link(dve.tensor_scalar(sp_[:], tau[:], 1.0, None, ALU.add))
        dve.wait_ge(a_set, 2)
        for sp_ in (sp_c, sp_col, sp_row):
            link(dve.tensor_scalar(sp_[:], sp_[:], -1.0, None, ALU.mult))
        link(dve.tensor_tensor(table[:], lag_n[:].unsqueeze(2).to_broadcast([P, TABLE, TRACES]),
                               sp_row[:].unsqueeze(1).to_broadcast([P, TABLE, TRACES]), ALU.mult))
        link(dve.tensor_scalar(spread_w[:], ramp[:], sp_col[:], None, ALU.mult))
        link(dve.tensor_scalar(power[:], ramp[:, 0:STEP], -1.0, sp_col[:], ALU.add, ALU.mult))
        dve.wait_ge(a_bl, C)
        link(dve.tensor_reduce(bl_sum[:], blend_t[:], AX.X, ALU.add))
        link(dve.reciprocal(bl_inv[:], bl_sum[:]))
        for k in range(C):
            link(dve.tensor_scalar(blend_t[:, k], blend_t[:, k], bl_inv[:, k:k + 1], 0.5, ALU.mult, ALU.mult))
        link(dve.tensor_copy(bl_rep[:], blend_t[:].unsqueeze(2).to_broadcast([P, C, 4, TRACES])))
        dve.wait_ge(d_in, 16 * len(WEIGHTS))
        link(dve.tensor_reduce(mean_w[:], wout[:], AX.X, ALU.add))
        link(dve.tensor_scalar(mean_w[:], mean_w[:], -1.0 / D, None, ALU.mult))
        for k in range(C):
            link(dve.tensor_scalar(wout[:, k], wout[:, k], mean_w[:, k:k + 1], 0.5, ALU.add, ALU.mult))
        link(dve.tensor_scalar(bg_h[:], bg_h[:], 0.5, None, ALU.mult))
        link(dve.tensor_scalar(btemp_h[:], btemp_h[:], 0.5, None, ALU.mult))
        dve.wait_ge(a_set, 3)
        context(0)
        link(dve.tensor_tensor(table[:], table[:], lag_on[:].unsqueeze(2).to_broadcast([P, TABLE, TRACES]), ALU.mult))
        link(dve.tensor_tensor(spread_w[:], spread_w[:], own[:], ALU.mult))
        dve.wait_ge(pe_set, 1)
        link(dve.tensor_copy(w_rep[:], pY[:, 0]))
        for lag in range(STEP):
            link(dve.tensor_scalar(w_lag[:, lag], w_rep[:], power[:, lag:lag + 1], None, ALU.mult))
        link(dve.tensor_copy(w_st[:], w_lag[:]))
        low = slice(2 * TRACES, 3 * TRACES)
        link(dve.tensor_tensor(w_st[low], w_lag[low], w_st[low].bitcast(F32), ALU.subtract))
        dve.wait_ge(w_hi, 2)
        link(dve.tensor_tensor(wout_p[1][:], wout[:], wout_p[0][:].bitcast(F32), ALU.subtract))
        dve.sem_inc(set_done, 1)

        def gating(n, par):
            dve.wait_ge(thg_done, n + 1)
            if not (isinstance(n, int) and n < 2):
                dve.wait_ge(inner_done, (STEP - 1) * (n - 1))
                dve.wait_ge(gt_done, n - 1)
            dve.scalar_tensor_tensor(out=gated[par][:], in0=th_g[:], scalar=1.0, in1=xn(n), op0=ALU.add, op1=ALU.mult)\
               .then_inc(gated_done, 1)

        def modulation(n, par):
            dve.wait_ge(thm_done, n + 1)
            if not (isinstance(n, int) and n < 2):
                dve.wait_ge(lag_done, (n - 1) * STEP)
            dve.tensor_scalar(mod_st[par][:], th_m[:], 0.5, 1.0, ALU.mult, ALU.add).then_inc(vmod, 1)
            low = slice(TRACES, 2 * TRACES)
            dve.tensor_scalar(mod_f[low], th_m[low], 0.5, 1.0, ALU.mult, ALU.add).then_inc(vmod, 1)
            dve.wait_ge(vmod, 2 * n + 2)
            dve.tensor_tensor(mod_st[par][low], mod_f[low], mod_st[par][low].bitcast(F32), ALU.subtract).then_inc(modst_done, 1)

        def states(n, q):
            dve.wait_ge(st_done, 4 * n + q + 1)
            if not (isinstance(n, int) and n == 0 and q < 2):
                dve.wait_ge(yin_done, 4 * n + q - 1)
            dve.tensor_tensor(state[q % 2][:], pS[q % 2][:], w_rep[:].unsqueeze(1).to_broadcast([P, 2, D]), ALU.mult)\
               .then_inc(sw_done, 1)

        def lag_sum(n, par, lag):
            dve.wait_ge(lag_done, STEP * n + lag + 1)
            m = rows(pL[lag % 2]).rearrange("p (a j) -> p a j", j=STEP)
            g = rows(gated[par]).rearrange("p (a j) -> p a j", j=STEP)
            if lag == 0:
                at_least(dve, temp_done, n)
                dve.tensor_tensor(rows(inner), rows(gated[par]), rows(pL[0]), ALU.mult).then_inc(prod_done, 1)
                return
            pr = rows(prod[lag % 2]).rearrange("p (a j) -> p a j", j=STEP)[:, :, 0:STEP - lag]
            dve.tensor_tensor(pr, g[:, :, 0:STEP - lag], m[:, :, 0:STEP - lag], ALU.mult).then_inc(prod_done, 1)
            dve.wait_ge(prod_done, STEP * n + lag + 1)
            if lag > 1:
                dve.wait_ge(inner_done, (STEP - 1) * n + lag - 1)
            y = rows(inner).rearrange("p (a j) -> p a j", j=STEP)[:, :, lag:STEP]
            dve.tensor_tensor(y, y, pr, ALU.add).then_inc(inner_done, 1)

        def total(n):
            dve.wait_ge(ytr_done, n + 1)
            dve.wait_ge(inner_done, (STEP - 1) * (n + 1))
            at_least(dve, templo_done, n)
            dve.tensor_tensor(temporal[:], inner[:], pY[:], ALU.add).then_inc(temp_done, 1)

        def low_temporal(n):
            dve.wait_ge(temphi_done, n + 1)
            dve.tensor_tensor(temp_p[1][:], temporal[:], temp_p[0][:].bitcast(F32), ALU.subtract).then_inc(templo_done, 1)

        def low_mixed(n):
            dve.wait_ge(mixhi_done, n + 1)
            dve.tensor_tensor(mixed_p[1][:], mixed[:], mixed_p[0][:].bitcast(F32), ALU.subtract).then_inc(mixlo_done, 1)

        def mixing(n):
            dve.wait_ge(tho_done, n + 1)
            dve.wait_ge(soma_done, n + 1)
            at_least(dve, mixlo_done, n)
            dve.scalar_tensor_tensor(out=mixed[:], in0=th_o[:], scalar=1.0, in1=soma[:], op0=ALU.add, op1=ALU.mult)\
               .then_inc(mixed_done, 1)

        def norm(n):
            dve.wait_ge(std_done, n + 1)
            at_least(dve, normed_done, n)
            dve.reciprocal(rstd[:], std[:]).then_inc(rstd_done, 1)
            dve.wait_ge(rstd_done, n + 1)
            at_least(dve, scaled_done, n)
            dve.tensor_tensor(normed[:], pZ[:], rstd[:].unsqueeze(1).to_broadcast([P, C, S]), ALU.mult).then_inc(normed_done, 1)

        def body(n, par, has_a, has_c):
            if has_a:
                context(n + 1)
            if has_c:
                low_temporal(n - 1)
            states(n, 0)
            states(n, 1)
            lag_sum(n, par, 0)
            if has_c:
                mixing(n - 1)
            lag_sum(n, par, 1)
            if has_c:
                low_mixed(n - 1)
            lag_sum(n, par, 2)
            lag_sum(n, par, 3)
            if has_a:
                modulation(n + 1, 1 - par)
            states(n, 2)
            lag_sum(n, par, 4)
            if has_c:
                norm(n - 1)
            states(n, 3)
            lag_sum(n, par, 5)
            if has_a:
                gating(n + 1, 1 - par)
            lag_sum(n, par, 6)
            lag_sum(n, par, 7)
            total(n)

        gating(0, 0)
        modulation(0, 0)
        loop(dve, body)
        low_temporal(NB - 1)
        mixing(NB - 1)
        low_mixed(NB - 1)
        norm(NB - 1)

    @block.scalar
    def _(act):
        act.wait_ge(v_step, 6)
        for tau in (tau_c, tau_col):
            act.activation(tau[:], tau[:], ACT.Exp)
        act.activation(tau_row[:], tau_row[:], ACT.Exp).then_inc(a_set, 1)
        act.wait_ge(v_step, 9)
        for sp_ in (sp_c, sp_col):
            act.activation(sp_[:], sp_[:], ACT.Ln)
        act.activation(sp_row[:], sp_row[:], ACT.Ln).then_inc(a_set, 1)
        for k in range(C):
            act.activation(blend_t[:, k], blend_t[:, k], ACT.Exp, bias=bl_max[:, k:k + 1]).then_inc(a_bl, 1)
        act.wait_ge(d_in, 16 * len(WEIGHTS))
        for w, (hi, lo) in ((wn1, wn1_p), (wg, wg_p), (wsoma, wsoma_p), (wtemp, wtemp_p)):
            ins = act.activation(hi[:], w[:], ACT.Copy)
        ins.then_inc(w_hi, 1)
        act.wait_ge(v_step, 15)
        act.activation(alpha_c[:], sp_c[:], ACT.Exp)
        act.activation(table[:], table[:], ACT.Exp)
        act.activation(spread_w[:], spread_w[:], ACT.Exp)
        act.activation(power[:], power[:], ACT.Exp).then_inc(a_set, 1)
        act.wait_ge(v_step, 26)
        act.activation(wout_p[0][:], wout[:], ACT.Copy).then_inc(w_hi, 1)

        def high_x(n, par):
            if not (isinstance(n, int) and n < 2):
                act.wait_ge(soma_mm, n - 1)
            act.activation(x_p[par][0][:], xn(n), ACT.Copy).then_inc(xhi_done, 1)

        def high_context(n):
            act.wait_ge(ctx_done, n + 1)
            at_least(act, wg_done, C * n)
            act.activation(ctx_p[0][:], ctx_e[:], ACT.Copy).then_inc(chi_done, 1)

        def high_temporal(n):
            act.wait_ge(temp_done, n + 1)
            at_least(act, gate_mm, n)
            act.activation(temp_p[0][:], temporal[:], ACT.Copy).then_inc(temphi_done, 1)

        def high_mixed(n):
            act.wait_ge(mixed_done, n + 1)
            at_least(act, out_mm, n)
            act.activation(mixed_p[0][:], mixed[:], ACT.Copy).then_inc(mixhi_done, 1)

        def input_gate(n):
            act.wait_ge(wg_done, C * (n + 1))
            at_least(act, gated_done, n)
            for m in range(C):
                ins = act.activation(th_g[:, m], pA[:, m], ACT.Tanh, bias=bg_h[:, m:m + 1], scale=0.5)
            ins.then_inc(thg_done, 1)

        def hidden(n):
            act.wait_ge(h1_done, n + 1)
            at_least(act, modt_done, n)
            act.activation(h1[0:HID1], pB[0:HID1, 0], ACT.Gelu, bias=bn1[:]).then_inc(gelu1_done, 1)

        def mod_rows(n):
            act.wait_ge(mod_done, n + 1)
            at_least(act, modst_done, n)
            act.activation(th_m[:], pB[0:3 * TRACES, 1], ACT.Tanh, scale=0.5).then_inc(thm_done, 1)

        def mod_cols(n):
            act.wait_ge(modt_done, n + 1)
            act.activation(th_t[:], pB[:, 0, 0:C * TRACES].rearrange("p (c d) -> p c d", c=C), ACT.Tanh, scale=0.5)\
               .then_inc(tht_done, 1)
            act.wait_ge(tht_done, n + 1)
            at_least(act, dec_done, n)
            act.activation(mod_t[:], th_t[:], ACT.Copy, scale=0.5, bias=1.0).then_inc(modt_ready, 1)

        def turned(n, par):
            act.wait_ge(gt_done, n + 1)
            if not (isinstance(n, int) and n < 2):
                act.wait_ge(st_done, (n - 1) * 4)
            act.activation(gated_t[par][:], pA[:], ACT.Copy).then_inc(gtev_done, 1)

        def spread_out(n):
            act.wait_ge(yin_done, 4 * (n + 1))
            at_least(act, ytr_done, n)
            act.activation(outer_t[:], pY[:], ACT.Copy).then_inc(yev_done, 1)

        def somas(n):
            act.wait_ge(soma_mm, n + 1)
            at_least(act, mixed_done, n)
            for m in range(C):
                ins = act.activation(soma[:, m], pZ[:, m], ACT.Gelu, bias=bsoma[:, m:m + 1])
            ins.then_inc(soma_done, 1)

        def output_gate(n):
            act.wait_ge(gate_mm, n + 1)
            at_least(act, mixed_done, n)
            for m in range(C):
                ins = act.activation(th_o[:, m], pY[:, m], ACT.Tanh, bias=btemp_h[:, m:m + 1], scale=0.5)
            ins.then_inc(tho_done, 1)

        def squares(n):
            act.wait_ge(out_mm, n + 1)
            at_least(act, var_mm, n)
            act.activation(square[:], pZ[:], ACT.Square).then_inc(sq_done, 1)

        def deviation(n):
            act.wait_ge(var_mm, n + 1)
            at_least(act, rstd_done, n)
            act.activation(std[:], pB[:, 0], ACT.Sqrt, bias=eps[:]).then_inc(std_done, 1)
            act.activation(table_pick[:], eps[:], ACT.Gelu)

        def scaling(n):
            act.wait_ge(normed_done, n + 1)
            at_least(act, x2_done, n)
            for m in range(C):
                ins = act.activation(scaled[:, m], normed[:, m], ACT.Identity, bias=beta[:, m:m + 1], scale=gamma[:, m:m + 1])
            ins.then_inc(scaled_done, 1)

        def body(n, par, has_a, has_c):
            if has_a:
                high_x(n + 1, 1 - par)
            if has_c:
                high_temporal(n - 1)
            if has_a:
                high_context(n + 1)
            if has_c:
                somas(n - 1)
                output_gate(n - 1)
            if has_a:
                hidden(n + 1)
            if has_c:
                high_mixed(n - 1)
            if has_a:
                mod_rows(n + 1)
                mod_cols(n + 1)
            if has_c:
                squares(n - 1)
                deviation(n - 1)
            if has_a:
                input_gate(n + 1)
            if has_c:
                scaling(n - 1)
            spread_out(n)
            if has_a:
                turned(n + 1, 1 - par)

        high_x(0, 0)
        high_context(0)
        hidden(0)
        input_gate(0)
        mod_rows(0)
        mod_cols(0)
        turned(0, 0)
        loop(act, body)
        high_temporal(NB - 1)
        somas(NB - 1)
        output_gate(NB - 1)
        high_mixed(NB - 1)
        squares(NB - 1)
        deviation(NB - 1)
        scaling(NB - 1)

    @block.tensor
    def _(pe):
        pe.wait_ge(v_step, 20)
        for k in range(C):
            ins = pe.transpose(pY[:, 0, k * P:k * P + P], bl_rep[:, k].rearrange("p r d -> p (r d)"), ident[:])
        ins.then_inc(pe_set, 1)
        pe.wait_ge(w_lo, 1)

        def product(out, w_parts, x_parts, ks, m, width=P, first=True, last=True):
            terms = [(w, x, kw, kx) for kw, kx in ks for w, x in
                     ((w_parts[0], x_parts[0]), (w_parts[1], x_parts[0]), (w_parts[0], x_parts[1]))]
            for i, (w, x, kw, kx) in enumerate(terms):
                ins = pe.matmul(out, w[:, kw, m * P:m * P + width], x[:, kx],
                                start=(first and i == 0), stop=(last and i == len(terms) - 1))
            return ins

        def gate_in(n, par, m):
            if m == 0:
                pe.wait_ge(xlo_done, n + 1)
                at_least(pe, gtev_done, n)
            product(pA[:, m], wg_p, x_p[par], [(k, k) for k in range(C)], m, last=False)
            if m == 0:
                pe.wait_ge(clo_done, n + 1)
            product(pA[:, m], wg_p, ctx_p, [(C + k, k) for k in range(C)], m, first=False).then_inc(wg_done, 1)

        def hidden(n, par):
            pe.wait_ge(xlo_done, n + 1)
            if not (isinstance(n, int) and n < 3):
                pe.wait_ge(std_done, n - 2)
            product(pB[0:HID1, 0], wn1_p, x_p[par], [(k, k) for k in range(C)], 0, width=HID1).then_inc(h1_done, 1)

        def modulate_rows(n):
            pe.wait_ge(gelu1_done, n + 1)
            pe.matmul(pB[0:3 * TRACES, 1], wn2_3[:], h1[:], start=True, stop=True).then_inc(mod_done, 1)

        def modulate_cols(n):
            pe.wait_ge(thm_done, n + 1)
            for k in range(C):
                ins = pe.matmul(pB[:, 0, k * TRACES:k * TRACES + TRACES], h1[:, k * P:k * P + P], wn2[:], start=True, stop=True)
            ins.then_inc(modt_done, 1)

        def turn(n, par):
            pe.wait_ge(tht_done, n + 1)
            pe.wait_ge(thg_done, n + 1)
            pe.wait_ge(gated_done, n + 1)
            for k in range(C):
                for c in range(C):
                    ins = pe.transpose(pA[:, k, c * P:c * P + P], gated[par][:, c, k * P:k * P + P], ident[:])
            ins.then_inc(gt_done, 1)

        def states(n, par, q):
            if q == 0:
                pe.wait_ge(dec_done, n + 1)
                pe.wait_ge(gtev_done, n + 1)
            if not (isinstance(n, int) and n == 0 and q < 2):
                pe.wait_ge(sw_done, 4 * n + q - 1)
            for i in range(2):
                g = 2 * q + i
                late = g >= 4
                columns = (4 * g, CHUNKS + 4 * g - LATE) if late else (4 * g,)
                for k, lo in enumerate(columns):
                    ins = pe.matmul(pS[q % 2][:, i], decayed[par][:, lo:lo + 4].rearrange("p a d -> p (a d)"),
                                    gated_t[par][:, k], start=(k == 0), stop=(k == len(columns) - 1))
            ins.then_inc(st_done, 1)

        def spread(n, q):
            pe.wait_ge(sw_done, 4 * n + q + 1)
            if q == 0:
                at_least(pe, tho_done, n)
            for i in range(2):
                j = (2 * q + i) % 4
                ins = pe.matmul(pY[32 * j:32 * j + 32, q // 2], spread_w[:], state[q % 2][:, i],
                                start=True, stop=True, tile_position=(0, 32 * j))
            ins.then_inc(yin_done, 1)

        def turn_back(n):
            pe.wait_ge(yev_done, n + 1)
            for k in range(C):
                for c in range(C):
                    ins = pe.transpose(pY[:, c, k * P:k * P + P], outer_t[:, k, c * P:c * P + P], ident[:])
            ins.then_inc(ytr_done, 1)

        def lags(n, par, lag):
            if lag == 0:
                pe.wait_ge(modst_done, n + 1)
            if not (isinstance(n, int) and n == 0 and lag < 2):
                pe.wait_ge(prod_done, STEP * n + lag - 1)
            for c in range(C):
                ins = pe.matmul(pL[lag % 2][:, c], w_st[0:3 * TRACES, lag, c * P:c * P + P], mod_st[par][:],
                                start=True, stop=True)
            ins.then_inc(lag_done, 1)

        def soma_in(n, par):
            at_least(pe, normed_done, n)
            for m in range(C):
                ins = product(pZ[:, m], wsoma_p, x_p[par], [(k, k) for k in range(C)], m)
            ins.then_inc(soma_mm, 1)

        def gate_out(n):
            pe.wait_ge(templo_done, n + 1)
            for m in range(C):
                ins = product(pY[:, m], wtemp_p, temp_p, [(k, k) for k in range(C)], m)
            ins.then_inc(gate_mm, 1)

        def output(n):
            pe.wait_ge(mixlo_done, n + 1)
            for m in range(C):
                ins = product(pZ[:, m], wout_p, mixed_p, [(k, k) for k in range(C)], m)
            ins.then_inc(out_mm, 1)

        def mean_square(n):
            pe.wait_ge(tht_done, NB if isinstance(n, int) and n + 3 > NB else n + 3)
            pe.wait_ge(sq_done, n + 1)
            for k in range(C):
                ins = pe.matmul(pB[:, 0], mean_mat[:], square[:, k], start=(k == 0), stop=(k == C - 1))
            ins.then_inc(var_mm, 1)

        def body(n, par, has_a, has_c):
            lags(n, par, 0)
            lags(n, par, 1)
            states(n, par, 0)
            states(n, par, 1)
            if has_c:
                gate_out(n - 1)
            if has_a:
                hidden(n + 1, 1 - par)
            lags(n, par, 2)
            if has_a:
                gate_in(n + 1, 1 - par, 0)
            spread(n, 0)
            lags(n, par, 3)
            if has_a:
                modulate_rows(n + 1)
            if has_c:
                output(n - 1)
            if has_a:
                modulate_cols(n + 1)
            spread(n, 1)
            states(n, par, 2)
            if has_c:
                mean_square(n - 1)
            lags(n, par, 4)
            if has_a:
                gate_in(n + 1, 1 - par, 1)
            lags(n, par, 5)
            states(n, par, 3)
            spread(n, 2)
            lags(n, par, 6)
            spread(n, 3)
            lags(n, par, 7)
            soma_in(n, par)
            if has_a:
                turn(n + 1, 1 - par)
            turn_back(n)

        hidden(0, 0)
        pe.wait_ge(w_lo, 2)
        gate_in(0, 0, 0)
        gate_in(0, 0, 1)
        pe.wait_ge(ones_done, 1)
        modulate_rows(0)
        modulate_cols(0)
        turn(0, 0)
        pe.wait_ge(w_lo, 4)
        pe.wait_ge(set_done, 1)
        loop(pe, body)
        gate_out(NB - 1)
        output(NB - 1)
        mean_square(NB - 1)

HIDDEN = 1024
HC = HIDDEN // P
ROUNDS = HC // 2
SHARED = 192
EXPERTS = 8
STAGES = 6


def expert_and_final(nc, sem_ctx, ctx, t, X, NB, consts):
    def sb(name, shape, dt=F32):
        return ctx.enter_context(nc.sbuf_tensor("c_" + name, shape, dt))

    def ps(name, shape, dt=F32):
        return ctx.enter_context(nc.psum_tensor("c_" + name, shape, dt))

    def sem(name):
        return sem_ctx.enter_context(nc.semaphore("c_" + name))

    ident = consts["ident"]
    w1 = sb("w1", [P, C, HIDDEN])
    w1_hi, w1_lo = sb("w1_hi", [P, C, HIDDEN], F32R), sb("w1_lo", [P, C, HIDDEN], F32R)
    b1 = sb("b1", [P, HC])
    w2 = sb("w2", [P, HC, SHARED])
    w2a_hi, w2a_lo = sb("w2a_hi", [P, HC, P], F32R), sb("w2a_lo", [P, HC, P], F32R)
    w2b_hi = [sb(f"w2b_hi{i}", [P, HC, P], F32R) for i in range(2)]
    w2b_lo = [sb(f"w2b_lo{i}", [P, HC, P], F32R) for i in range(2)]
    we = [sb(f"we{i}", [P, HC, D - SHARED]) for i in range(2)]
    b2 = [sb(f"b2{i}", [P, C]) for i in range(2)]
    expert_i = sb("expert_i", [1, NB], I32)
    stage_i = sb("stage_i", [1, NB], I32)
    embed_all = sb("embed_all", [P, STAGES, S])
    embed = [sb(f"embed{i}", [P, S]) for i in range(2)]
    key_t = [sb(f"key_t{i}", [P, C, S]) for i in range(2)]
    value = [sb(f"value{i}", [P, C, D]) for i in range(2)]
    x_hi = [sb(f"x_hi{i}", [P, C, S], F32R) for i in range(2)]
    x_lo = [sb(f"x_lo{i}", [P, C, S], F32R) for i in range(2)]
    hid = [sb(f"hid{i}", [P, 2, S]) for i in range(2)]
    hid_hi = [sb(f"hid_hi{i}", [P, 2, S], F32R) for i in range(ROUNDS)]
    hid_lo = [sb(f"hid_lo{i}", [P, 2, S], F32R) for i in range(ROUNDS)]
    query = sb("query", [P, C, S])
    neg_max = sb("neg_max", [P, C])
    row_sum = sb("row_sum", [P, C])
    row_inv = sb("row_inv", [P, C])
    prob = sb("prob", [P, C, S])
    prob_t = sb("prob_t", [P, C, S])
    y = [sb(f"y{i}", [P, C, S]) for i in range(2)]

    pH = [ps(f"pH{i}", [P, 2, S]) for i in range(ROUNDS)]
    pO, pS, pT, pV = (ps(n, [P, C, S]) for n in ("pO", "pS", "pT", "pV"))

    d_in = sem("d_in")
    d_exp, d_bias, d_emb, d_key, d_val, stored = ([sem(f"{n}{i}") for i in range(2)]
                                                  for n in ("d_exp", "d_bias", "d_emb", "d_key", "d_val", "stored"))
    d_w1, d_b1, d_w2, w_hi, w_lo = (sem(n) for n in ("d_w1", "d_b1", "d_w2", "w_hi", "w_lo"))
    xhi_done, xlo_done, ehi_done, elo_done = (sem(n) for n in ("xhi", "xlo", "ehi", "elo"))
    hid_mm, gelu_done, hhi_done, hlo_done, out_mm, x3_done = (sem(n) for n in ("hid_mm", "gelu", "hhi", "hlo", "out_mm", "x3"))
    query_done, s_mm, max_done, exp_done, inv_done, prob_done = (sem(n) for n in ("query", "s_mm", "max", "exp", "inv", "prob"))
    t_mm, pt_done, v_mm, y_done = (sem(n) for n in ("t_mm", "pt", "v_mm", "y"))

    def xn(n, k):
        at = slice(n * S, n * S + S) if isinstance(n, int) else bass.ds(n * S, S)
        return X[:, k, at]

    def batch_of(src, n):
        if isinstance(n, int):
            return src[n]
        return src[bass.ds(n, 1)]

    LOADS = 7
    block = ctx.enter_context(nc.Block())

    def loop(eng, body):
        body(0, 0, True, True, False)
        body(1, 1, True, True, True)
        if NB > 4:
            with pairs(eng, 2, NB - 2) as n:
                body(n, 0, True, True, True)
                body(n + 1, 1, True, True, True)
        body(NB - 2, 0, True, False, True)
        body(NB - 1, 1, False, False, True)

    @block.sync
    def _(sp):
        sp.dma_start(w1[:], t["w1"].rearrange("(k p) e -> p k e", p=P)).then_inc(d_w1, 16)
        sp.dma_start(b1[:], t["b1"]).then_inc(d_b1, 16)
        sp.dma_start(w2[:], t["w2"].rearrange("(k p) e -> p k e", p=P)).then_inc(d_w2, 16)
        sp.dma_start(expert_i[:], t["expert"]).then_inc(d_in, 16)
        sp.dma_start(stage_i[:], t["stage"]).then_inc(d_in, 16)
        for i in range(2):
            sp.dma_start(b2[i][:, 0:1], t["b2"][0:P]).then_inc(d_in, 16)
            sp.dma_start(b2[i][0:SHARED - P, 1:2], t["b2"][P:SHARED]).then_inc(d_in, 16)
        sp.dma_start(embed_all[:], t["embed"].partition_broadcast(P)).then_inc(d_in, 16)
        sp.wait_ge(d_in, 16 * LOADS)

        def load(n, par):
            at = slice(n, n + 1) if isinstance(n, int) else bass.ds(n, 1)
            expert = sp.value_load(expert_i[0:1, at], min_val=0, max_val=EXPERTS - 1)
            stage = sp.value_load(stage_i[0:1, at], min_val=0, max_val=STAGES - 1)
            if not (isinstance(n, int) and n < 2):
                sp.wait_ge(elo_done, n - 1)
            sp.dma_start(we[par][:], t["we"][bass.ds(expert, 1)].rearrange("o p k e -> p (o k) e")).then_inc(d_exp[par], 16)
            if not (isinstance(n, int) and n < 2):
                sp.wait_ge(x3_done, n - 1)
            sp.dma_start(b2[par][SHARED - P:P, 1:2], t["be"][bass.ds(expert, 1)].rearrange("o p f -> p (o f)")).then_inc(d_bias[par], 16)
            if not (isinstance(n, int) and n < 2):
                sp.wait_ge(query_done, n - 1)
            sp.dma_start(embed[par][:], embed_all[:, bass.ds(stage, 1)].rearrange("p o f -> p (o f)")).then_inc(d_emb[par], 16)
            if not (isinstance(n, int) and n < 2):
                sp.wait_ge(s_mm, n - 1)
            src = batch_of(t["keyT"], n)
            sp.dma_start(key_t[par][:], src.rearrange("(k p) s -> p k s", p=P) if isinstance(n, int)
                         else src.rearrange("o (k p) s -> p (o k) s", p=P)).then_inc(d_key[par], 16)
            if not (isinstance(n, int) and n < 2):
                sp.wait_ge(v_mm, n - 1)
            src = batch_of(t["key"], n)
            sp.dma_start(value[par][:], src.rearrange("(k p) s -> p k s", p=P) if isinstance(n, int)
                         else src.rearrange("o (k p) s -> p (o k) s", p=P)).then_inc(d_val[par], 16)

        def body(n, par, ahead, splits, has_3):
            if ahead:
                load(n + 1, 1 - par)

        load(0, 0)
        loop(sp, body)

    @block.gpsimd
    def _(pool):
        def store(n, par):
            pool.wait_ge(y_done, n + 1)
            dst = batch_of(t["out"], n)
            pool.dma_start(dst.rearrange("(k p) s -> p k s", p=P) if isinstance(n, int)
                           else dst.rearrange("o (k p) s -> p (o k) s", p=P), y[par][:]).then_inc(stored[par], 16)

        def expert_low(n, par):
            pool.wait_ge(ehi_done, n + 1)
            pool.tensor_tensor(w2b_lo[par][:, :, SHARED - P:P], we[par][:], w2b_hi[par][:, :, SHARED - P:P].bitcast(F32),
                               ALU.subtract).then_inc(elo_done, 1)

        def body(n, par, ahead, splits, has_3):
            if ahead:
                expert_low(n + 1, 1 - par)
            if has_3:
                store(n - 1, 1 - par)

        expert_low(0, 0)
        loop(pool, body)
        store(NB - 1, 1)
        for par in range(2):
            pool.wait_ge(stored[par], landed(NB - 2 + par, par))

    @block.vector
    def _(dve):
        def low_x(n, par):
            dve.wait_ge(xhi_done, n + 1)
            at = slice(n * S, n * S + S) if isinstance(n, int) else bass.ds(n * S, S)
            dve.tensor_tensor(x_lo[par][:], X[:, :, at], x_hi[par][:].bitcast(F32), ALU.subtract).then_inc(xlo_done, 1)

        def split(n, r):
            dve.wait_ge(gelu_done, ROUNDS * n + r + 1)
            if not (isinstance(n, int) and n == 0):
                dve.wait_ge(out_mm, ROUNDS * n + r - (ROUNDS - 1))
            dve.tensor_copy(hid_hi[r][:], hid[r % 2][:]).then_inc(hhi_done, 1)
            dve.wait_ge(hhi_done, ROUNDS * n + r + 1)
            dve.tensor_tensor(hid_lo[r][:], hid[r % 2][:], hid_hi[r][:].bitcast(F32), ALU.subtract).then_inc(hlo_done, 1)

        def residual(n, par):
            dve.wait_ge(out_mm, ROUNDS * (n + 1))
            dve.wait_ge(d_bias[par], landed(n, par))
            for k in range(C):
                ins = dve.scalar_tensor_tensor(out=xn(n, k), in0=pO[:, k], scalar=b2[par][:, k:k + 1], in1=xn(n, k),
                                               op0=ALU.add, op1=ALU.add)
            ins.then_inc(x3_done, 1)

        def queries(n, par):
            dve.wait_ge(x3_done, n + 1)
            dve.wait_ge(d_emb[par], landed(n, par))
            at_least(dve, s_mm, n)
            at = slice(n * S, n * S + S) if isinstance(n, int) else bass.ds(n * S, S)
            dve.tensor_tensor(query[:], X[:, :, at], embed[par][:].unsqueeze(1).to_broadcast([P, C, S]), ALU.add)\
               .then_inc(query_done, 1)

        def maxima(n):
            dve.wait_ge(s_mm, n + 1)
            dve.tensor_reduce(neg_max[:], pS[:], AX.X, ALU.max, negate=True).then_inc(max_done, 1)

        def normalize(n):
            dve.wait_ge(exp_done, n + 1)
            at_least(dve, prob_done, C * n)
            dve.reciprocal(row_inv[:], row_sum[:]).then_inc(inv_done, 1)
            dve.wait_ge(inv_done, n + 1)
            for k in range(C):
                dve.tensor_scalar(prob[:, k], prob[:, k], row_inv[:, k:k + 1], None, ALU.mult).then_inc(prob_done, 1)

        def final(n, par):
            dve.wait_ge(v_mm, n + 1)
            if not (isinstance(n, int) and n < 2):
                dve.wait_ge(stored[par], landed(n - 2, par))
            at = slice(n * S, n * S + S) if isinstance(n, int) else bass.ds(n * S, S)
            dve.tensor_tensor(y[par][:], pV[:], X[:, :, at], ALU.add).then_inc(y_done, 1)

        def body(n, par, ahead, splits, has_3):
            if has_3:
                maxima(n - 1)
            if ahead:
                split(n + 1, 0)
            if has_3:
                normalize(n - 1)
            if ahead:
                split(n + 1, 1)
                split(n + 1, 2)
            if splits:
                low_x(n + 2, par)
            residual(n, par)
            queries(n, par)
            if ahead:
                split(n + 1, 3)
            if has_3:
                final(n - 1, 1 - par)

        low_x(0, 0)
        dve.wait_ge(w_hi, 1)
        dve.tensor_tensor(w1_lo[:], w1[:], w1_hi[:].bitcast(F32), ALU.subtract).then_inc(w_lo, 1)
        low_x(1, 1)
        dve.wait_ge(w_hi, 2)
        dve.tensor_tensor(w2a_lo[:], w2[:, :, 0:P], w2a_hi[:].bitcast(F32), ALU.subtract)
        for i in range(2):
            ins = dve.tensor_tensor(w2b_lo[i][:, :, 0:SHARED - P], w2[:, :, P:SHARED],
                                    w2b_hi[i][:, :, 0:SHARED - P].bitcast(F32), ALU.subtract)
        ins.then_inc(w_lo, 1)
        dve.wait_ge(d_in, 16 * LOADS)
        for r in range(ROUNDS):
            split(0, r)
        loop(dve, body)
        maxima(NB - 1)
        normalize(NB - 1)
        final(NB - 1, 1)

    @block.scalar
    def _(act):
        def high_x(n, par):
            if not (isinstance(n, int) and n < 2):
                act.wait_ge(hid_mm, ROUNDS * (n - 1))
            at = slice(n * S, n * S + S) if isinstance(n, int) else bass.ds(n * S, S)
            act.activation(x_hi[par][:], X[:, :, at], ACT.Copy).then_inc(xhi_done, 1)

        def expert_high(n, par):
            act.wait_ge(d_exp[par], landed(n, par))
            if not (isinstance(n, int) and n < 2):
                act.wait_ge(out_mm, ROUNDS * (n - 1))
            act.activation(w2b_hi[par][:, :, SHARED - P:P], we[par][:], ACT.Copy).then_inc(ehi_done, 1)

        def hidden(n, r):
            act.wait_ge(hid_mm, ROUNDS * n + r + 1)
            if not (isinstance(n, int) and n == 0 and r < 2):
                act.wait_ge(hlo_done, ROUNDS * n + r - 1)
            for i in range(2):
                ins = act.activation(hid[r % 2][:, i], pH[r][:, i], ACT.Gelu, bias=b1[:, 2 * r + i:2 * r + i + 1])
            ins.then_inc(gelu_done, 1)

        def exps(n):
            act.wait_ge(max_done, n + 1)
            at_least(act, t_mm, n)
            at_least(act, inv_done, n)
            for k in range(C):
                ins = act.activation(prob[:, k], pS[:, k], ACT.Exp, bias=neg_max[:, k:k + 1], accum_out=row_sum[:, k:k + 1])
            ins.then_inc(exp_done, 1)

        def turned(n):
            act.wait_ge(t_mm, n + 1)
            at_least(act, v_mm, n)
            act.activation(prob_t[:], pT[:], ACT.Copy).then_inc(pt_done, 1)

        def body(n, par, ahead, splits, has_3):
            if ahead:
                hidden(n + 1, 0)
            if has_3:
                exps(n - 1)
            if ahead:
                hidden(n + 1, 1)
                hidden(n + 1, 2)
            if has_3:
                turned(n - 1)
            if splits:
                high_x(n + 2, par)
            if ahead:
                expert_high(n + 1, 1 - par)
                hidden(n + 1, 3)

        high_x(0, 0)
        act.wait_ge(d_w1, 16)
        act.activation(w1_hi[:], w1[:], ACT.Copy).then_inc(w_hi, 1)
        high_x(1, 1)
        act.wait_ge(d_w2, 16)
        act.activation(w2a_hi[:], w2[:, :, 0:P], ACT.Copy)
        for i in range(2):
            ins = act.activation(w2b_hi[i][:, :, 0:SHARED - P], w2[:, :, P:SHARED], ACT.Copy)
        ins.then_inc(w_hi, 1)
        act.wait_ge(d_b1, 16)
        for r in range(ROUNDS):
            hidden(0, r)
        expert_high(0, 0)
        loop(act, body)
        exps(NB - 1)
        turned(NB - 1)

    @block.tensor
    def _(pe):
        pe.wait_ge(w_lo, 1)

        def hidden(n, par, r):
            if r == 0:
                pe.wait_ge(xlo_done, n + 1)
            if not (isinstance(n, int) and n == 0):
                pe.wait_ge(gelu_done, ROUNDS * n + r - (ROUNDS - 1))
            terms = [(w, x, k) for k in range(C) for w, x in ((w1_hi, x_hi), (w1_lo, x_hi), (w1_hi, x_lo))]
            for i in range(2):
                m = 2 * r + i
                for w, x, k in terms:
                    ins = pe.matmul(pH[r][:, i], w[:, k, m * P:m * P + P], x[par][:, k],
                                    start=(w is w1_hi and x is x_hi and k == 0), stop=(x is x_lo and k == C - 1))
            ins.then_inc(hid_mm, 1)

        def output(n, par, r):
            pe.wait_ge(hlo_done, ROUNDS * n + r + 1)
            if r == 0:
                pe.wait_ge(elo_done, n + 1)
                at_least(pe, x3_done, n)
            for i in range(2):
                m = 2 * r + i
                for half, (hi, lo) in enumerate(((w2a_hi, w2a_lo), (w2b_hi[par], w2b_lo[par]))):
                    for term, (w, h) in enumerate(((hi, hid_hi[r]), (lo, hid_hi[r]), (hi, hid_lo[r]))):
                        ins = pe.matmul(pO[:, half], w[:, m], h[:, i], start=(m == 0 and half == 0 and term == 0),
                                        stop=(m == HC - 1 and half == 1 and term == 2), skip_group_check=True)
            ins.then_inc(out_mm, 1)

        def scores(n, par):
            pe.wait_ge(query_done, n + 1)
            pe.wait_ge(d_key[par], landed(n, par))
            at_least(pe, exp_done, n)
            for m in range(C):
                for k in range(C):
                    ins = pe.matmul(pS[:, m], query[:, k, m * P:m * P + P], key_t[par][:, k], start=(k == 0), stop=(k == C - 1))
            ins.then_inc(s_mm, 1)

        def turn(n):
            pe.wait_ge(prob_done, C * (n + 1))
            at_least(pe, pt_done, n)
            for k in range(C):
                for m in range(C):
                    ins = pe.transpose(pT[:, m, k * P:k * P + P], prob[:, k, m * P:m * P + P], ident[:])
            ins.then_inc(t_mm, 1)

        def mix_values(n, par):
            pe.wait_ge(pt_done, n + 1)
            pe.wait_ge(d_val[par], landed(n, par))
            at_least(pe, y_done, n)
            for m in range(C):
                for k in range(C):
                    ins = pe.matmul(pV[:, m], value[par][:, k, m * P:m * P + P], prob_t[:, k], start=(k == 0), stop=(k == C - 1))
            ins.then_inc(v_mm, 1)

        def body(n, par, ahead, splits, has_3):
            if ahead:
                hidden(n + 1, 1 - par, 0)
            if has_3:
                scores(n - 1, 1 - par)
            output(n, par, 0)
            if ahead:
                hidden(n + 1, 1 - par, 1)
            output(n, par, 1)
            if ahead:
                hidden(n + 1, 1 - par, 2)
            if has_3:
                turn(n - 1)
            output(n, par, 2)
            if ahead:
                hidden(n + 1, 1 - par, 3)
            output(n, par, 3)
            if has_3:
                mix_values(n - 1, 1 - par)

        for r in range(ROUNDS):
            hidden(0, 0, r)
        pe.wait_ge(w_lo, 2)
        loop(pe, body)
        scores(NB - 1, 1)
        turn(NB - 1)
        mix_values(NB - 1, 1)


def build_program(nc, t):
    NB = t["xT"].shape[0]
    with ExitStack() as whole:
        X = whole.enter_context(nc.sbuf_tensor("x_all", [P, C, NB * S], F32))
        shapes = {"ident": [P, P], "iota": [P, S], "sel_sum": [P, C, 4, P], "sel_rep": [P, C, C, P], "par_mask": [P, 2]}
        consts = {name: whole.enter_context(nc.sbuf_tensor(name, shape, F32)) for name, shape in shapes.items()}
        consts["ident_bf"] = whole.enter_context(nc.sbuf_tensor("ident_bf", [P, P], BF16))
        const_loaded = whole.enter_context(nc.semaphore("const_loaded"))
        const_cast = whole.enter_context(nc.semaphore("const_cast"))

        with nc.Block() as block:
            @block.sync
            def _(sp):
                for name in shapes:
                    sp.dma_start(consts[name][:], t[name]).then_inc(const_loaded, 16)
                sp.wait_ge(const_loaded, 16 * len(shapes))

            @block.vector
            def _(dve):
                dve.wait_ge(const_loaded, 16 * len(shapes))
                dve.tensor_copy(consts["ident_bf"][:], consts["ident"][:]).then_inc(const_cast, 1)
                dve.wait_ge(const_cast, 1)

        for layer in (attention_layer, trace_layer, expert_and_final):
            with ExitStack() as tiles:
                layer(nc, whole, tiles, t, X, NB, consts)



def shape_constants():
    import numpy as np
    p, o, i = np.arange(P), np.arange(P), np.arange(32)
    f = np.float32
    sums = [32 * (o // 32) + DH * (1 - q % 2) for q in range(4)]
    sel_sum = np.stack([np.stack([((p[:, None] == sums[q][None]) & (o[None] % 8 == 4 * qc + q)).astype(f)
                                  for q in range(4)], 1) for qc in range(C)], 1)
    sel_rep = np.stack([np.stack([(p[:, None] == (32 * (o // 32) + 4 * qc + 2 * c + o % 32 // 16)[None]).astype(f)
                                  for c in range(C)], 1) for qc in range(C)], 1)
    before = np.concatenate([STEP * np.arange(CHUNKS)[None] - 1 - p[:, None],
                             STEP * np.arange(LATE, CHUNKS)[None] - 1 - P - p[:, None]], 1)
    return {
        "ident": np.eye(P, dtype=f), "iota": np.tile(np.arange(S, dtype=f), (P, 1)),
        "sel_sum": sel_sum, "sel_rep": sel_rep,
        "par_mask": np.stack([p // DH % 2 == 0, p // DH % 2 == 1], 1).astype(f),
        "lag_n": np.maximum(before, 0).astype(f), "lag_on": (before >= 0).astype(f),
        "ramp": np.tile((i % STEP + 1).astype(f), (P, 1)),
        "own": (p[:, None] // 32 == i[None] // STEP).astype(f),
    }


def layouts(a):
    import numpy as np

    def turned(w):
        return w.T

    def column(b):
        return b.reshape(-1, P).T

    def head_rows(w):
        return w.reshape((C, 2, 4, DH) + w.shape[1:]).swapaxes(1, 2).reshape(w.shape)

    l0, l1, l2 = ({k[8:]: v for k, v in a.items() if k.startswith(p)} for p in ("L0_cond_", "L1_cond_", "L2_cond_"))
    wn2 = np.concatenate([turned(a["cond_256"]), a["condB_bn2"][None]])
    out = {
        "xT": a["x"].transpose(0, 2, 1),
        "wq": turned(l0["Wq"]), "wk": turned(l0["Wk"]), "wv": turned(l0["Wv"]), "wo": head_rows(turned(l0["Wo"])),
        "bq": column(l0["bq"]), "bk": column(l0["bk"]), "bv": column(head_rows(l0["bv"])), "bo": column(l0["bo"]),
        "idx": a["itok_Sx32_0_1023"], "valid": a["mask_Sx32_bk1"],
        "mask": a["mask_SxS_bk0"], "maskT": turned(a["mask_SxS_bk0"]),
        "u": a["condB_uprev"],
        "wg": turned(l1["Wg"]), "wn1": turned(l1["Wn1"]), "wn2": wn2, "wn2_3": np.tile(wn2, (1, 3)),
        "wsoma": turned(l1["Wsoma"]), "wtemp": turned(l1["Wtemp"]), "wout": turned(l1["Wout"]),
        "bg": column(l1["bg"]), "bn1": l1["bn1"].reshape(-1, 1), "bsoma": column(l1["bsoma"]),
        "btemp": column(l1["btemp"]), "gamma": column(l1["gamma"]), "beta": column(l1["beta"]),
        "tau_c": l1["tau_ctx"].reshape(1), "tau_col": np.tile(a["condB_tauraws"], P // TRACES).reshape(P, 1),
        "tau_row": a["condB_tauraws"], "blend_t": turned(a["cond_1024"]),
        "w1": l2["W1"], "b1": column(l2["b1"]), "w2": l2["W2"], "b2": l2["b2"].reshape(-1, 1),
        "we": l2["We"].reshape(EXPERTS, HC, P, -1).swapaxes(1, 2), "be": l2["be"][:, :, None],
        "embed": a["L3_cond_braak_embed"], "expert": a["itok_B_0_7"][None], "stage": a["itok_B_0_5"][None],
        "key": a["fside_BxSxS_0"], "keyT": a["fside_BxSxS_0"].transpose(0, 2, 1),
    }
    out.update(shape_constants())
    return out


def kernel(**inputs):
    import numpy as np
    import concourse.bacc as bacc
    from concourse.bass_utils import run_bass_kernel_spmd

    data = layouts({name: np.asarray(a) for name, a in inputs.items()})
    nc = bacc.Bacc("TRN2", target_bir_lowering=False, num_devices=1)
    arrays, t = {}, {}
    for name, a in data.items():
        a = np.ascontiguousarray(a)
        arrays[f"in_{name}"] = a
        t[name] = nc.dram_tensor(f"in_{name}", a.shape, mybir.dt.from_np(a.dtype), kind="ExternalInput").ap()
    shape = data["xT"].shape
    t["out"] = nc.dram_tensor("out_0", shape, F32, kind="ExternalOutput").ap()
    build_program(nc, t)
    result = run_bass_kernel_spmd(nc, [arrays], core_ids=[0])
    return result.results[0]["out_0"].transpose(0, 2, 1)
```
